# Optimizing a Trainium2 kernel written in Bass

```python
import numpy as np
import jax
import jax.numpy as jnp

def _softmax(x, axis=-1):
    return jax.nn.softmax(x, axis=axis)

def _gelu(x):
    return jax.nn.gelu(x, approximate=True)

def _silu(x):
    return jax.nn.silu(x)

def _sigmoid(x):
    return jax.nn.sigmoid(x)

def _layernorm(x, axis=-1, eps=1e-05):
    m = jnp.mean(x, axis=axis, keepdims=True)
    v = jnp.var(x, axis=axis, keepdims=True)
    return (x - m) / jnp.sqrt(v + eps)

def _scatter_add(tgt, idx, src, axis=0):
    return tgt.at[idx].add(src)

def _segment_sum(src, seg, n):
    return jax.ops.segment_sum(src, seg, n)
kernel_name = 'mk_audio_tower_d1_tok_audfeat256_r4_2c658f'

def setup_inputs(seed: int=0):
    np.random.seed(seed)
    _w = jnp.asarray

    def _rec_inputs():
        import jax
        import jax.numpy as jnp
        _rk = jax.random.key(seed)
        x = -0.000154596 + 0.999967 * jax.random.normal(jax.random.fold_in(_rk, 1), (128, 256, 64), jnp.float32)
        return x
    x = _rec_inputs()

    def _L0_tok_setup():
        import jax, jax.numpy as jnp
        import numpy as np
        N, L, F = (32, 4096, 64)
        POOL = 4
        key = jax.random.key(seed)
        k1, k2 = jax.random.split(key)
        x = jax.random.normal(k1, (N, L, F), dtype=jnp.float32)
        W = jax.random.normal(k2, (F, F), dtype=jnp.float32) * (1.0 / np.sqrt(F))
        return {'x': x, 'W': W, 'pool_size': POOL}
    _L0_tok_all = _L0_tok_setup()
    _L0_tok_in = {k: v for k, v in _L0_tok_all.items() if k in ('W',)}
    del _L0_tok_all

    def _L0_attn_setup():
        import jax, jax.numpy as jnp
        import numpy as np
        F = 64
        key = jax.random.key(seed)
        ks = jax.random.split(key, 6)
        s = 1.0 / np.sqrt(F)
        x = jax.random.normal(ks[0], (16, 256, F), dtype=jnp.float32)
        W_alpha = jax.random.uniform(ks[1], (F, F), minval=-s, maxval=s, dtype=jnp.float32)
        W_beta = jax.random.uniform(ks[2], (F, F), minval=-s, maxval=s, dtype=jnp.float32)
        W_unary = jax.random.uniform(ks[3], (F, F), minval=-s, maxval=s, dtype=jnp.float32)
        b_unary = jax.random.uniform(ks[4], (F,), minval=-s, maxval=s, dtype=jnp.float32)
        W_r = jax.random.uniform(ks[5], (F, F), minval=-s, maxval=s, dtype=jnp.float32)
        return {'x': x, 'W_alpha': W_alpha, 'W_beta': W_beta, 'W_unary': W_unary, 'b_unary': b_unary, 'W_r': W_r}
    _L0_attn_all = _L0_attn_setup()
    _L0_attn_in = {k: v for k, v in _L0_attn_all.items() if k in ('W_alpha', 'W_beta', 'W_unary', 'b_unary', 'W_r')}
    del _L0_attn_all

    def _L0_ffn_setup():
        import jax, jax.numpy as jnp
        import numpy as np
        B, N, D = (16, 1024, 64)
        NUM_EXPERTS, TOP_K, HEADS = (4, 2, 4)
        N_EDGES = 262144
        LN_EPS = 1e-05

        def _layernorm(x, g, b):
            mu = x.mean(-1, keepdims=True)
            var = ((x - mu) ** 2).mean(-1, keepdims=True)
            return (x - mu) * jax.lax.rsqrt(var + LN_EPS) * g + b

        def _forward(x, edge_index, W_gat, att_src, att_dst, b_gat, ln_gamma, ln_beta, W1, b1, W2, b2):
            Bc, Nc, Dc = x.shape
            M = Bc * Nc
            x_flat = x.reshape(M, Dc)
            h = (x_flat @ W_gat).reshape(M, HEADS, NUM_EXPERTS)
            loops = jnp.arange(M, dtype=edge_index.dtype)
            src = jnp.concatenate([edge_index[0], loops])
            dst = jnp.concatenate([edge_index[1], loops])
            a_src = (h * att_src).sum(-1)
            a_dst = (h * att_dst).sum(-1)
            e = jax.nn.leaky_relu(a_src[src] + a_dst[dst], negative_slope=0.2)
            e_max = jax.ops.segment_max(e, dst, num_segments=M)
            ee = jnp.exp(e - e_max[dst])
            denom = jax.ops.segment_sum(ee, dst, num_segments=M)
            alpha = ee / (denom[dst] + 1e-16)
            msg = h[src] * alpha[:, :, None]
            agg = jax.ops.segment_sum(msg, dst, num_segments=M).reshape(M, HEADS * NUM_EXPERTS) + b_gat
            scores = _layernorm(agg, ln_gamma, ln_beta).reshape(M, HEADS, NUM_EXPERTS).mean(1)
            scores = scores.reshape(Bc, Nc, NUM_EXPERTS)
            topk_s, topk_i = jax.lax.top_k(scores, TOP_K)
            w = jax.nn.softmax(topk_s, axis=-1)
            out = jnp.zeros_like(x)
            for ei in range(NUM_EXPERTS):
                g = jnp.where(topk_i == ei, w, 0.0).sum(-1)
                hh = jax.nn.gelu(x @ W1[ei] + b1[ei], approximate=False)
                out = out + g[..., None] * (hh @ W2[ei] + b2[ei])
            return out
        key = jax.random.key(seed)
        ks = jax.random.split(key, 8)
        s = 0.05
        return {'x': jax.random.normal(ks[0], (B, N, D), jnp.float32), 'W_gat': jax.random.normal(ks[1], (D, HEADS * NUM_EXPERTS), jnp.float32) * s, 'att_src': jax.random.normal(ks[2], (HEADS, NUM_EXPERTS), jnp.float32) * s, 'att_dst': jax.random.normal(ks[3], (HEADS, NUM_EXPERTS), jnp.float32) * s, 'b_gat': jnp.zeros((HEADS * NUM_EXPERTS,), jnp.float32), 'ln_gamma': jnp.ones((HEADS * NUM_EXPERTS,), jnp.float32), 'ln_beta': jnp.zeros((HEADS * NUM_EXPERTS,), jnp.float32), 'W1': jax.random.normal(ks[4], (NUM_EXPERTS, D, 2 * D), jnp.float32) * s, 'b1': jnp.zeros((NUM_EXPERTS, 2 * D), jnp.float32), 'W2': jax.random.normal(ks[5], (NUM_EXPERTS, 2 * D, D), jnp.float32) * s, 'b2': jnp.zeros((NUM_EXPERTS, D), jnp.float32), 'edge_index': jax.random.randint(ks[6], (2, N_EDGES), 0, B * N, jnp.int32)}
    _L0_ffn_all = _L0_ffn_setup()
    _L0_ffn_in = {k: v for k, v in _L0_ffn_all.items() if k in ('W_gat', 'att_src', 'att_dst', 'b_gat', 'ln_gamma', 'ln_beta', 'W1', 'b1', 'W2', 'b2', 'edge_index')}
    del _L0_ffn_all
    return {'x': x, 'L0_tok_W': _L0_tok_in['W'], 'L0_attn_W_alpha': _L0_attn_in['W_alpha'], 'L0_attn_W_beta': _L0_attn_in['W_beta'], 'L0_attn_W_unary': _L0_attn_in['W_unary'], 'L0_attn_b_unary': _L0_attn_in['b_unary'], 'L0_attn_W_r': _L0_attn_in['W_r'], 'L0_ffn_W_gat': _L0_ffn_in['W_gat'], 'L0_ffn_att_src': _L0_ffn_in['att_src'], 'L0_ffn_att_dst': _L0_ffn_in['att_dst'], 'L0_ffn_b_gat': _L0_ffn_in['b_gat'], 'L0_ffn_ln_gamma': _L0_ffn_in['ln_gamma'], 'L0_ffn_ln_beta': _L0_ffn_in['ln_beta'], 'L0_ffn_W1': _L0_ffn_in['W1'], 'L0_ffn_b1': _L0_ffn_in['b1'], 'L0_ffn_W2': _L0_ffn_in['W2'], 'L0_ffn_b2': _L0_ffn_in['b2'], 'L0_ffn_edge_index': _L0_ffn_in['edge_index']}

def reference(x, L0_tok_W, L0_attn_W_alpha, L0_attn_W_beta, L0_attn_W_unary, L0_attn_b_unary, L0_attn_W_r, L0_ffn_W_gat, L0_ffn_att_src, L0_ffn_att_dst, L0_ffn_b_gat, L0_ffn_ln_gamma, L0_ffn_ln_beta, L0_ffn_W1, L0_ffn_b1, L0_ffn_W2, L0_ffn_b2, L0_ffn_edge_index):
    import jax
    import jax.numpy as jnp

    def _L0_tok_ref(x, W, pool_size):
        import jax, jax.numpy as jnp
        import numpy as np
        N, L, F = (32, 4096, 64)
        POOL = 4
        n, l, f = x.shape
        lc = l - l % pool_size
        xw = x[:, :lc, :].reshape(n, lc // pool_size, pool_size, f)
        raw = jnp.einsum('nlpf,fg->nlpg', xw, W)
        att = jax.nn.softmax(raw, axis=-2)
        return jnp.sum(xw * att, axis=-2)

    def _L0_attn_ref(x, W_alpha, W_beta, W_unary, b_unary, W_r):
        import jax, jax.numpy as jnp
        import numpy as np
        F = 64
        B, N, _ = x.shape
        alpha = jnp.einsum('bnf,gf->bng', x, W_alpha)
        beta = jnp.einsum('bnf,gf->bng', x, W_beta)
        unary = jnp.einsum('bnf,gf->bng', x, W_unary) + b_unary
        scores = jnp.einsum('bif,bjf->bij', alpha, beta)
        scores = scores * (1.0 - jnp.eye(N, dtype=x.dtype))
        att = jnp.einsum('bij,bjf->bif', scores, unary) / N
        out = jnp.einsum('bif,gf->big', att, W_r) + x
        return out

    def _L0_ffn_ref(x, W_gat, att_src, att_dst, b_gat, ln_gamma, ln_beta, W1, b1, W2, b2, edge_index):
        import jax, jax.numpy as jnp
        import numpy as np
        B, N, D = (16, 1024, 64)
        NUM_EXPERTS, TOP_K, HEADS = (4, 2, 4)
        N_EDGES = 262144
        LN_EPS = 1e-05

        def _layernorm(x, g, b):
            mu = x.mean(-1, keepdims=True)
            var = ((x - mu) ** 2).mean(-1, keepdims=True)
            return (x - mu) * jax.lax.rsqrt(var + LN_EPS) * g + b

        def _forward(x, edge_index, W_gat, att_src, att_dst, b_gat, ln_gamma, ln_beta, W1, b1, W2, b2):
            Bc, Nc, Dc = x.shape
            M = Bc * Nc
            x_flat = x.reshape(M, Dc)
            h = (x_flat @ W_gat).reshape(M, HEADS, NUM_EXPERTS)
            loops = jnp.arange(M, dtype=edge_index.dtype)
            src = jnp.concatenate([edge_index[0], loops])
            dst = jnp.concatenate([edge_index[1], loops])
            a_src = (h * att_src).sum(-1)
            a_dst = (h * att_dst).sum(-1)
            e = jax.nn.leaky_relu(a_src[src] + a_dst[dst], negative_slope=0.2)
            e_max = jax.ops.segment_max(e, dst, num_segments=M)
            ee = jnp.exp(e - e_max[dst])
            denom = jax.ops.segment_sum(ee, dst, num_segments=M)
            alpha = ee / (denom[dst] + 1e-16)
            msg = h[src] * alpha[:, :, None]
            agg = jax.ops.segment_sum(msg, dst, num_segments=M).reshape(M, HEADS * NUM_EXPERTS) + b_gat
            scores = _layernorm(agg, ln_gamma, ln_beta).reshape(M, HEADS, NUM_EXPERTS).mean(1)
            scores = scores.reshape(Bc, Nc, NUM_EXPERTS)
            topk_s, topk_i = jax.lax.top_k(scores, TOP_K)
            w = jax.nn.softmax(topk_s, axis=-1)
            out = jnp.zeros_like(x)
            for ei in range(NUM_EXPERTS):
                g = jnp.where(topk_i == ei, w, 0.0).sum(-1)
                hh = jax.nn.gelu(x @ W1[ei] + b1[ei], approximate=False)
                out = out + g[..., None] * (hh @ W2[ei] + b2[ei])
            return out
        return _forward(x, edge_index, W_gat, att_src, att_dst, b_gat, ln_gamma, ln_beta, W1, b1, W2, b2)
    h = _L0_tok_ref(x, L0_tok_W, 4)
    h = h + _L0_attn_ref(_layernorm(h, axis=-1), L0_attn_W_alpha, L0_attn_W_beta, L0_attn_W_unary, L0_attn_b_unary, L0_attn_W_r)
    h = h + _L0_ffn_ref(_layernorm(h, axis=-1), L0_ffn_W_gat, L0_ffn_att_src, L0_ffn_att_dst, L0_ffn_b_gat, L0_ffn_ln_gamma, L0_ffn_ln_beta, L0_ffn_W1, L0_ffn_b1, L0_ffn_W2, L0_ffn_b2, L0_ffn_edge_index)
    return h

_drawn_inputs = setup_inputs


def setup_inputs(seed=0):
    import zlib

    import numpy as np

    out = dict(_drawn_inputs(seed))
    spreads = {'L0_ffn_b_gat': (0.0, 2.0),
     'L0_ffn_ln_gamma': (1.0, 0.6),
     'L0_ffn_ln_beta': (0.0, 0.8),
     'L0_ffn_b1': (0.0, 0.649),
     'L0_ffn_b2': (0.0, 0.1)}
    factors = {'L0_attn_b_unary': 4.192,
     'L0_ffn_att_src': 64.0,
     'L0_ffn_att_dst': 183.183,
     'L0_ffn_W_gat': 4.577}
    for name, (base, spread) in spreads.items():
        noise = np.random.default_rng([zlib.crc32(name.encode()), seed]).standard_normal(out[name].shape)
        drawn = base * np.exp(spread * noise) if base else spread * noise
        out[name] = jnp.asarray(drawn.astype(out[name].dtype))
    for name, factor in factors.items():
        out[name] = (out[name] * factor).astype(out[name].dtype)
    return out
```

```python
import numpy as np
from contextlib import ExitStack

import concourse.bass as bass
from concourse import mybir

F32 = mybir.dt.float32
I32 = mybir.dt.int32
ALU = mybir.AluOpType
ACT = mybir.ActivationFunctionType
AX = mybir.AxisListType


def audio_tower(nc, x, tok_w, w_alpha, w_beta, w_unary, b_unary, w_r, w_gat, att_src, att_dst,
                b_gat, ln_gamma, ln_beta, w1, b1, w2, b2, edges, out):
    P = 128
    B, L, F = x.shape
    POOL = 4
    SEQ = L // POOL
    M = B * SEQ
    TILES = M // P
    E = edges.shape[1]
    W = E // P
    HALF = W // 2
    NE, _, HID = w1.shape
    HEADS = att_src.shape[0]
    HC = HEADS * NE
    ROW = HC + HEADS
    EXT = HC + 2 * HEADS
    EPS = 1e-5
    BIG = 1e30

    SRC_BITS = M.bit_length() - 1
    NODE = 1 << (2 * SRC_BITS + 2)
    FAR = 1 << (2 * SRC_BITS + 1)
    LOG_W, LOG_E = W.bit_length() - 1, E.bit_length() - 1
    STEP = 512
    HEADS_N = E // STEP
    C = 64
    HC2 = C // 2
    CHUNK = P * C
    MAX_CHUNKS = E // CHUNK
    PAD = 64
    OUTC = HEADS + HEADS + HC
    SUMS = HEADS + HC
    NS = TILES + 1
    RING = 4

    GA = 4
    GB = 8
    NB = TILES // GB

    sorted_rows = nc.dram_tensor("sorted_rows", (HEADS_N, STEP), F32).ap()
    sorted_padded = nc.dram_tensor("sorted_padded", (PAD + E + CHUNK,), F32).ap()
    heads_dram = nc.dram_tensor("heads_dram", (HEADS_N,), F32).ap()
    table = nc.dram_tensor("table", (M, ROW), F32).ap()
    inject = nc.dram_tensor("inject", (E + M, HEADS), F32).ap()
    results = nc.dram_tensor("results", (E, OUTC), F32).ap()

    with ExitStack() as ctx:
        def sb(name, shape, dt=F32):
            return ctx.enter_context(nc.sbuf_tensor(name, shape, dt))

        def sem(name):
            return ctx.enter_context(nc.semaphore(name))

        ident = sb("ident", [P, P])
        lane = sb("lane", [P, 1], I32)
        lane_bit = sb("lane_bit", [P, LOG_E - LOG_W + 1], I32)
        sign = sb("sign", [P, LOG_E - LOG_W + 1])
        turn = sb("turn", [P, LOG_E - LOG_W + 1])
        pair_mask = sb("pair_mask", [P, P])
        zeros = sb("zeros", [P, 528])
        node_i = sb("node_i", [P, NS], I32)
        node_f = sb("node_f", [P, NS])
        tok_w2 = sb("tok_w2", [P, P])
        wa = sb("wa", [F, F])
        wb = sb("wb", [F, F])
        wu = sb("wu", [F, F + 1])
        wr = sb("wr", [F, F])
        wr_t = sb("wr_t", [F, F])
        w_score = sb("w_score", [F, F])
        w_value = sb("w_value", [F + 1, F])
        w_ext = sb("w_ext", [F, EXT])
        wg_t = sb("wg_t", [HC, F])
        att_col = sb("att_col", [HC, 2])
        att_sel = sb("att_sel", [HC, 2, HEADS])
        head_mask = sb("head_mask", [HC, HEADS])
        w1_s = sb("w1_s", [F, NE, HID])
        w2_s = sb("w2_s", [HID, NE, F])
        b1_s = sb("b1_s", [HID, NE])
        b2_row = sb("b2_row", [1, NE, GB, F])
        ones_row = sb("ones_row", [1, P])
        bg = sb("bg", [P, HC])
        gamma = sb("gamma", [P, HC])
        beta = sb("beta", [P, HC])

        sort = [sb("sort0", [P, W]), sb("sort1", [P, W])]
        h = sb("h", [P, TILES, F])
        xn = sb("xn", [P, TILES, F])
        xn2_t = sb("xn2_t", [F, M])
        arena = sb("arena", [P, TILES * NE * F])
        ext = sb("ext", [P, TILES, EXT])
        ends = sb("ends", [P, TILES, OUTC])
        stat = sb("stat", [P, 2, TILES])
        nxt = sb("nxt", [P, 2, TILES])
        lower = sb("lower", [P, 2, NS])
        row_f = sb("row_f", [P, 2, NS])
        row_i = sb("row_i", [P, 2, NS], I32)
        goal = sb("goal", [P, 2, NS], I32)
        count = sb("count", [P, 2, TILES])
        has = sb("has", [P, 2, TILES])
        start_f = sb("start_f", [P, TILES])
        start_i = sb("start_i", [P, TILES], I32)
        end_i = sb("end_i", [P, TILES], I32)
        chunks_f = sb("chunks_f", [1, 1])
        chunks_i = sb("chunks_i", [1, 1], I32)

        def carve(base, at, *shape, partitions=P):
            size = int(np.prod(shape))
            ap = base[0:partitions, at:at + size]
            names = "abcd"[:len(shape)]
            if len(shape) > 1:
                ap = ap.rearrange(f"p ({' '.join(names)}) -> p {' '.join(names)}",
                                  **{n: s for n, s in zip(names[1:], shape[1:])})
            return ap, at + size

        at = 0
        frames, frames_t, logits, tree = [], [], [], []
        for s in range(2):
            a, at = carve(arena, at, GA, POOL * F)
            frames.append(a)
            a, at = carve(arena, at, GA * POOL // 2, P)
            frames_t.append(a)
            a, at = carve(arena, at, GA, POOL, F)
            logits.append(a)
            a, at = carve(arena, at, GA, 3, F)
            tree.append(a)
        xg, at = carve(arena, at, GB, F)
        xg_t, at = carve(arena, at, GB * P, partitions=F + 1)
        t_t, at = carve(arena, at, GB * P, partitions=F)
        value, at = carve(arena, at, GB, F)
        score, at = carve(arena, at, GB, P)
        attended, at = carve(arena, at, GB, F)
        assert at <= TILES * NE * F
        square = arena[:, 0:TILES * F].rearrange("p (t f) -> p t f", f=F)
        experts = arena[:, :].rearrange("p (t e f) -> p t e f", e=NE, f=F)
        x2g = sb("x2g", [P, GB, F])
        hidden = sort[1][:].rearrange("p (a b) -> p a b", a=2)

        keys = sb("keys", [P, C + 1], I32)
        segs = sb("segs", [P, C + 1], I32)
        same_next = sb("same_next", [P, C])
        same = sb("same", [P, C])
        src_a = sb("src_a", [P, HC2], I32)
        src_b = sb("src_b", [P, HC2], I32)
        rows_a = sb("rows_a", [P, HC2, ROW])
        rows_b = sb("rows_b", [P, HC2, ROW])
        inj = sb("inj", [P, C, HEADS])
        fence = sb("fence", [P, C])
        lasts = sb("lasts", [P, 1])
        a_s = sb("a_s", [P, HEADS, C])
        a_d = sb("a_d", [P, HEADS, C])
        top = sb("top", [P, HEADS, C + 1])
        xn_flat = xn[:].rearrange("p t f -> p (t f)")
        at = 0
        h_s, at = carve(xn_flat, at, HC, C)
        wgt, at = carve(xn_flat, at, SUMS, C)
        part, at = carve(xn_flat, at, SUMS, C)
        logit, at = carve(xn_flat, at, HEADS, C)
        keep, at = carve(xn_flat, at, HEADS, C)
        assert at <= TILES * F
        results_s = sb("results_s", [P, C, OUTC])
        tails = sb("tails", [P, 2, SUMS])
        passing = sb("passing", [P, HEADS])
        across = sb("across", [SUMS, 2, P])
        state_d = sb("state_d", [HEADS, P + 1])
        state_m = sb("state_m", [HEADS, P + 1])
        state_s = sb("state_s", [SUMS, P + 1])
        carry_d = sb("carry_d", [P, HEADS])
        carry_m = sb("carry_m", [P, HEADS])
        carry_s = sb("carry_s", [P, SUMS])
        clamped = sb("clamped", [P, ROW])

        at = 0
        mg, at = carve(sort[0], at, 3, TILES, HEADS)
        mtop, at = carve(sort[0], at, TILES, HEADS)
        cmp, at = carve(sort[0], at, TILES, NE)
        gate, at = carve(sort[0], at, TILES, NE)
        sc, at = carve(sort[0], at, TILES, NE)
        st2 = sb("st2", [P, 2, TILES])

        heads_all = sb("heads_all", [P, HEADS_N])
        ring = [sort[0][:, i * STEP:(i + 1) * STEP] for i in range(RING)]
        less = sb("less", [P, STEP], mybir.dt.bfloat16)

        pt = [ctx.enter_context(nc.psum_tensor(f"pt{i}", [P, 1024], F32)) for i in range(4)]

        names = """weights_in wr_in wg_in edges_in frames_in0 frames_in1 lane_ready ident_ready mask_ready
            node_ready zeros_ready prep_pe prep_act prep_dve v_chain sorted_ops turned up_done down_done
            hi_ready frames_free frames_t_done frames_t_ready logits_done logits_free shifted pool_exp
            pool_steps pool_max pooled p_chain norm_var norm_sd norm_done x_staged x_t_done x_t_ready t_done t_ready
            score_done score_ready score_masked att_done att_ready attn_added ext_x_done
            ext_x_staged ext_x_ready ext_done ext_ready hidden_done hidden_ready expert_done expert_ready
            srt_out heads_out heads_in row_idx row_in0 row_in1 row_in2 row_in3 row_used bound_ready shift_in table_out zero_out scatter_ready scattered
            keys_in keys_free inj_in inj_free idx_a idx_b rows_a_in rows_b_in rows_a_free rows_b_free
            e_chain h_copied tail_ready tail_t state_ready carry_t exp_go exp_done res_ready res_out
            far_idx ends_idx ends_in clamped_in mg_go mg_exp f_chain var_go sd_ready gate_go gate_exp
            y_done out_done pad_out results_zero held_pe held_pool""".split()
        S = {n: sem(n) for n in names}

        def hold(eng, name, value):
            eng.wait_ge(S[name], value)
            eng.sem_inc(S["held_" + ("pe" if eng is nc.tensor else "pool")], 1)

        class Counted:
            def __init__(self, eng, s, first=0):
                self.eng, self.s, self.n = eng, s, 0
                self.first = first

            def mark(self, ins):
                ins.then_inc(self.s, 1)
                self.n += 1

            def link(self, ins):
                self.mark(ins)
                self.eng.wait_ge(self.s, self.first + self.n)

        block = ctx.enter_context(nc.Block())

        IN_ROW = LOG_W - 1
        IN_ROW_OPS = 4 * IN_ROW * (IN_ROW + 1) // 2

        def level_start(k):
            ops, cur = IN_ROW_OPS, (IN_ROW * (IN_ROW + 1) // 2) % 2
            for j in range(LOG_W, k):
                if j == LOG_W:
                    ops += 2 + 4 * (LOG_W - 1)
                    cur = (cur + 1 + LOG_W) % 2
                else:
                    ops += 4 * (j - LOG_W) + 2 + 12 + 28
                    cur = (cur + j - LOG_W - 1 + 4 + 7) % 2
            return ops, cur

        def level_down(k):
            ops, cur = level_start(k)
            return ops + 4 * (k - LOG_W) + 2 + 12, (cur + k - LOG_W - 1 + 4) % 2

        SORT_OPS, SORT_END = level_start(LOG_E + 1)

        def half(buf, i):
            return sort[buf][:, i * HALF:(i + 1) * HALF]

        def pairs(ap, s):
            return ap.rearrange("p (a t s) -> p a t s", t=2, s=s)

        GATHERS = HC2 * 16
        slots = [S[f"row_in{i}"] for i in range(RING)]

        @block.sync
        def _(sp):
            words = edges.rearrange("t (p w) -> p t w", p=P)
            raw = xn2_t
            sp.dma_start(sort[0][:].bitcast(I32), words[:, 1, :]).then_inc(S["edges_in"], 16)
            sp.dma_start(sort[1][:].bitcast(I32), words[:, 0, :]).then_inc(S["edges_in"], 16)
            n_w = 0
            for dst, src in (
                (tok_w2[0:F, 0:F], tok_w), (tok_w2[F:P, F:P], tok_w), (wa[:], w_alpha), (wb[:], w_beta),
                (wu[:, 0:F], w_unary), (wu[:, F:F + 1], b_unary.rearrange("(f a) -> f a", a=1)),
                (wr[:], w_r), (w_ext[:, 0:HC], w_gat),
                (att_col[:, 0:1], att_src.rearrange("h (c a) -> (h c) a", a=1)),
                (att_col[:, 1:2], att_dst.rearrange("h (c a) -> (h c) a", a=1)),
            ):
                if n_w == 0:
                    sp.wait_ge(S["zeros_ready"], 2)
                sp.dma_start(dst, src).then_inc(S["weights_in"], 16)
                n_w += 1
            assert n_w == 10
            fr = x.rearrange("b (s w) f -> (b s) (w f)", w=POOL).rearrange("(t p) c -> p t c", p=P)
            with sp.Fori(0, TILES // GA // 2) as k:
                for s in range(2):
                    sp.wait_ge(S["frames_free"], 2 * k + s + 1)
                    sp.dma_start(frames[s], fr[:, bass.ds((2 * k + s) * GA, GA), :])\
                      .then_inc(S[f"frames_in{s}"], 16)
            for dst, src in (
                (w1_s[:], w1.rearrange("e d f -> d e f")), (w2_s[:], w2.rearrange("e f d -> f e d")),
                *[(b1_s[:, e:e + 1], b1[e, :].rearrange("(f a) -> f a", a=1)) for e in range(NE)],
                (bg[:], b_gat.partition_broadcast(P)), (gamma[:], ln_gamma.partition_broadcast(P)),
                (beta[:], ln_beta.partition_broadcast(P)),
            ):
                sp.dma_start(dst, src).then_inc(S["weights_in"], 16)
            for g in range(GB):
                sp.dma_start(b2_row[:, :, g, :], b2.rearrange("(a e) f -> a e f", a=1))\
                  .then_inc(S["weights_in"], 16)
            flat = inject.rearrange("e h -> (e h)")
            part_n = P * 528
            for i in range((E + M) * HEADS // part_n):
                sp.dma_start(flat[i * part_n:(i + 1) * part_n].rearrange("(p c) -> p c", p=P), zeros[:])\
                  .then_inc(S["zero_out"], 16)
            for i in range(16):
                n = E // 16
                sp.dma_start(results[i * n:(i + 1) * n, :].rearrange("(p c) o -> p (c o)", p=P)
                             .rearrange("p (r z) -> p r z", z=512),
                             zeros[:, 0:512].unsqueeze(1).broadcast_to([P, n * OUTC // P // 512, 512]))\
                  .then_inc(S["results_zero"], 16)
            sp.dma_start(sorted_padded[0:PAD].rearrange("(p c) -> p c", p=PAD), zeros[0:PAD, 0:1])\
              .then_inc(S["pad_out"], 16)
            sp.dma_start(sorted_padded[PAD + E:].rearrange("(p c) -> p c", p=P), zeros[:, 0:C])\
              .then_inc(S["pad_out"], 16)
            sp.wait_ge(S["sorted_ops"], SORT_OPS)
            done = sort[SORT_END]
            with nc.allow_non_contiguous_dma(reason="512 single words"):
                sp.dma_start(heads_dram.rearrange("(p c a) -> p c a", p=P, a=1),
                             done[:].rearrange("p (c s) -> p c s", s=STEP)[:, :, 0:1])\
                  .then_inc(S["heads_out"], 16)
            sp.dma_start(sorted_rows.rearrange("(p c) s -> p (c s)", p=P), done[:]).then_inc(S["srt_out"], 16)
            sp.dma_start(sorted_padded[PAD:PAD + E].rearrange("(p c) -> p c", p=P), done[:])\
              .then_inc(S["srt_out"], 16)
            sp.wait_ge(S["heads_out"], 16)
            sp.dma_start(heads_all[:], heads_dram.partition_broadcast(P)).then_inc(S["heads_in"], 16)
            sp.wait_ge(S["ext_ready"], NB)
            sp.dma_start(table.rearrange("(t p) c -> p t c", p=P), ext[:, :, 0:ROW]).then_inc(S["table_out"], 16)
            sp.wait_ge(S["table_out"], 16)
            sp.dma_start(clamped[:], table[M - 1, :].partition_broadcast(P)).then_inc(S["clamped_in"], 16)

            def next_lane(cls):
                low, to = lower[:, cls, :], nxt[:, cls, :]
                sp.dma_start(to[0:112, :], low[1:113, 0:TILES]).then_inc(S["shift_in"], 16)
                sp.dma_start(to[112:P - 1, :], low[113:P, 0:TILES]).then_inc(S["shift_in"], 16)
                sp.dma_start(to[P - 1:P, :], low[0:1, 1:NS]).then_inc(S["shift_in"], 16)

            sp.wait_ge(S["bound_ready"], 1)
            next_lane(0)
            sp.wait_ge(S["pad_out"], 32)
            sp.wait_ge(S["srt_out"], 32)

            def load_keys(k):
                first = PAD - 1 + k * CHUNK
                sp.dma_start(keys[:].bitcast(F32), bass.AP(tensor=sorted_padded.tensor, offset=first,
                                                           ap=[[C, P], [1, C + 1]]))\
                  .then_inc(S["keys_in"], 16)

            load_keys(0)
            sp.wait_ge(S["scatter_ready"], 1)
            chunks = sp.value_load(chunks_i[0:1, 0:1], min_val=1, max_val=MAX_CHUNKS)
            sp.wait_ge(S["scattered"], 16 * TILES)
            res = results.rearrange("(k p c) o -> k p (c o)", p=P, c=C)
            injs = inject[0:E, :].rearrange("(k p c) h -> k p (c h)", p=P, c=C)
            sp.wait_ge(S["results_zero"], 16 * 16)
            with sp.Fori(0, chunks) as k:
                sp.wait_ge(S["inj_free"], k + 1)
                sp.dma_start(inj[:].rearrange("p c h -> p (c h)"), injs[bass.ds(k, 1), :, :].rearrange("a p c -> (a p) c"))\
                  .then_inc(S["inj_in"], 16)
                sp.wait_ge(S["keys_free"], k + 1)
                sp.dma_start(keys[:].bitcast(F32), bass.AP(tensor=sorted_padded.tensor,
                                                           offset=PAD - 1 + CHUNK + k * CHUNK,
                                                           ap=[[C, P], [1, C + 1]]))\
                  .then_inc(S["keys_in"], 16)
                sp.wait_ge(S["res_ready"], k + 1)
                sp.dma_start(res[bass.ds(k, 1), :, :].rearrange("a p c -> (a p) c"),
                             results_s[:].rearrange("p c o -> p (c o)")).then_inc(S["res_out"], 16)
            sp.wait_ge(S["bound_ready"], 2)
            next_lane(1)
            rows_out = out.rearrange("b s f -> (b s) f").rearrange("(t p) f -> p t f", p=P)
            for i in range(4):
                sp.wait_ge(S["y_done"], i + 1)
                q = TILES // 4
                sp.dma_start(rows_out[:, i * q:(i + 1) * q, :], h[:, i * q:(i + 1) * q, :])\
                  .then_inc(S["out_done"], 16)
            sp.wait_ge(S["out_done"], 64)

        @block.gpsimd
        def _(pool):
            g = nc.gpsimd
            g.memset(zeros[:], 0.0).then_inc(S["zeros_ready"], 1)
            g.memset(tok_w2[:], 0.0).then_inc(S["zeros_ready"], 1)
            g.iota(lane[:], pattern=[[0, 1]], base=0, channel_multiplier=1).then_inc(S["lane_ready"], 1)
            g.iota(node_i[:], pattern=[[P, NS]], base=0, channel_multiplier=1).then_inc(S["node_ready"], 1)
            ch = Counted(pool, S["p_chain"])
            ch.link(g.memset(ident[:], 0.0))
            ch.link(g.memset(pair_mask[:], 0.0))
            ch.link(g.memset(head_mask[:], 1.0))
            ch.link(g.memset(ones_row[:], 1.0))
            ch.link(g.memset(xg_t[F:F + 1, :], 1.0))
            g.affine_select(out=ident[:], in_=ident[:], compare_op=ALU.not_equal, fill=1.0, base=0,
                            pattern=[[-1, P]], channel_multiplier=1).then_inc(S["ident_ready"], 1)
            ch.link(g.memset(pair_mask[0:SEQ, 0:SEQ], 1.0))
            ch.link(g.memset(pair_mask[SEQ:P, SEQ:P], 1.0))
            ch.link(g.affine_select(out=head_mask[:], in_=head_mask[:], compare_op=ALU.is_ge, fill=0.0, base=0,
                                    pattern=[[-NE, HEADS]], channel_multiplier=1))
            g.affine_select(out=pair_mask[:], in_=pair_mask[:], compare_op=ALU.not_equal, fill=0.0, base=0,
                            pattern=[[-1, P]], channel_multiplier=1).then_inc(S["mask_ready"], 1)
            g.affine_select(out=head_mask[:], in_=head_mask[:], compare_op=ALU.is_ge, fill=0.0, base=NE - 1,
                            pattern=[[NE, HEADS]], channel_multiplier=-1).then_inc(S["mask_ready"], 1)
            pool.wait_ge(S["mask_ready"], 2)

            A_OPS = 3
            with pool.Fori(0, TILES // GA // 2) as k:
                for s in range(2):
                    i = 2 * k + s
                    ch = Counted(pool, S["pool_steps"], i * A_OPS)
                    lg, tr = logits[s], tree[s]
                    fr = frames[s].rearrange("p t (w f) -> p t w f", w=POOL)
                    mine = bass.ds(i * GA, GA)
                    pool.wait_ge(S["pool_exp"], i + 1)
                    ch.mark(g.tensor_tensor(tr[:, :, 0:2], lg[:, :, 0:2], lg[:, :, 2:4], ALU.add))
                    ch.link(g.tensor_tensor(fr, fr, lg, ALU.mult))
                    g.tensor_tensor(xn[:, mine, :], tr[:, :, 0], tr[:, :, 1], ALU.add).then_inc(S["pooled"], 1)
                    ch.link(g.tensor_tensor(lg[:, :, 0:2], fr[:, :, 0:2], fr[:, :, 2:4], ALU.add))
                    assert ch.n == A_OPS
                    g.tensor_tensor(h[:, mine, :], lg[:, :, 0], lg[:, :, 1], ALU.add).then_inc(S["pooled"], 1)
                    pool.wait_ge(S["pooled"], 2 * i + 2)
                    pool.sem_inc(S["frames_free"], 1)

            pool.wait_ge(S["norm_done"], 1)
            with pool.Fori(0, NB) as k:
                hold(pool, "score_ready", k + 1)
                g.tensor_tensor(score, score, pair_mask[:].unsqueeze(1).broadcast_to([P, GB, P]), ALU.mult)\
                 .then_inc(S["score_masked"], 1)
                mine = bass.ds(k * GB, GB)
                g.tensor_tensor(h[:, mine, :], h[:, mine, :], xn[:, mine, :], ALU.add).then_inc(S["p_chain"], 1)
                pool.wait_ge(S["p_chain"], 9 + k)
                hold(pool, "att_ready", k + 1)
                g.tensor_tensor(h[:, mine, :], h[:, mine, :], attended, ALU.add).then_inc(S["attn_added"], 1)

            def fetch(cls):
                pool.wait_ge(S["row_idx"], cls + 1)
                for t in range(NS):
                    n = cls * NS + t
                    if n >= RING:
                        pool.wait_ge(S["row_used"], n - RING + 1)
                    g.indirect_dma_start(ring[n % RING], None, sorted_rows,
                                         bass.IndirectOffsetOnAxis(ap=row_i[:, cls, t:t + 1], axis=0))\
                     .then_inc(slots[n % RING], 16)

            pool.wait_ge(S["srt_out"], 32)
            pool.wait_ge(S["heads_out"], 16)
            fetch(0)
            pool.wait_ge(S["zero_out"], 16 * 16)
            pool.wait_ge(S["ext_ready"], NB)
            pool.wait_ge(S["scatter_ready"], 1)
            for t in range(TILES):
                g.indirect_dma_start(inject, bass.IndirectOffsetOnAxis(ap=start_i[:, t:t + 1], axis=0),
                                     ext[:, t, ROW:EXT], None).then_inc(S["scattered"], 16)
            pool.wait_ge(S["table_out"], 16)
            chunks = pool.value_load(chunks_i[0:1, 0:1], min_val=1, max_val=MAX_CHUNKS)
            with pool.Fori(0, chunks) as k:
                for idx, ready, rows, landed, free in (
                    (src_a, "idx_a", rows_a, "rows_a_in", "rows_a_free"),
                    (src_b, "idx_b", rows_b, "rows_b_in", "rows_b_free"),
                ):
                    hold(pool, ready, k + 1)
                    hold(pool, free, 2 * k + 2)
                    for c in range(HC2):
                        g.indirect_dma_start(rows[:, c, :], None, table,
                                             bass.IndirectOffsetOnAxis(ap=idx[:, c:c + 1], axis=0))\
                         .then_inc(S[landed], 16)
            fetch(1)
            hold(pool, "res_out", 16 * chunks + 16)
            for t in range(TILES):
                g.indirect_dma_start(ends[:, t, :], None, results,
                                     bass.IndirectOffsetOnAxis(ap=end_i[:, t:t + 1], axis=0))\
                 .then_inc(S["ends_in"], 16)

        @block.scalar
        def _(act):
            a = nc.scalar

            def copy(dst, src, **kw):
                return a.activation(dst, src, ACT.Copy, **kw)

            act.wait_ge(S["prep_pe"], 1)
            copy(w_score[:], pt[0][0:F, 0:F]).then_inc(S["prep_act"], 1)
            copy(wr_t[:], pt[0][0:F, 128:128 + F]).then_inc(S["prep_act"], 1)
            copy(wg_t[:], pt[0][0:HC, 256:256 + F]).then_inc(S["prep_act"], 1)
            act.wait_ge(S["prep_pe"], 2)
            copy(w_value[:], pt[1][0:F + 1, 0:F], scale=1.0 / SEQ).then_inc(S["prep_act"], 1)
            copy(w_ext[:, HC:EXT], pt[1][0:F, 128:128 + 2 * HEADS]).then_inc(S["prep_act"], 1)

            with act.Fori(0, TILES // GA // 2) as k:
                for s in range(2):
                    i = 2 * k + s
                    act.wait_ge(S["frames_t_done"], i + 1)
                    copy(frames_t[s].rearrange("p a b -> p (a b)"), pt[2 * s][:]).then_inc(S["frames_t_ready"], 1)
                    lg = logits[s].rearrange("p a b c -> p (a b c)")
                    act.wait_ge(S["shifted"], i + 1)
                    a.activation(lg, lg, ACT.Exp).then_inc(S["pool_exp"], 1)

            def root(n):
                act.wait_ge(S["norm_var"], n)
                a.activation(stat[:, 1], stat[:, 1], ACT.Sqrt).then_inc(S["norm_sd"], 1)

            root(1)

            def turned(k):
                ops, cur = level_start(k)
                for i in range(2):
                    act.wait_ge(S["sorted_ops"], ops - 2 * (1 - i))
                    copy(half(1 - cur, i), half(cur, i), scale=turn[:, k - LOG_W:k - LOG_W + 1])\
                        .then_inc(S["turned"], 1)

            turned(LOG_W)

            act.wait_ge(S["norm_done"], 1)
            with act.Fori(0, NB) as k:
                copy(xg, xn[:, bass.ds(k * GB, GB), :]).then_inc(S["x_staged"], 1)
                act.wait_ge(S["x_t_done"], k + 1)
                copy(xg_t[0:F, :], pt[0][0:F, :]).then_inc(S["x_t_ready"], 1)
                act.wait_ge(S["t_done"], k + 1)
                copy(t_t, pt[1][0:F, :]).then_inc(S["t_ready"], 1)
                copy(value.rearrange("p a b -> p (a b)"), pt[2][:, 0:512]).then_inc(S["t_ready"], 1)
                act.wait_ge(S["score_done"], k + 1)
                copy(score.rearrange("p a b -> p (a b)"), pt[3][:]).then_inc(S["score_ready"], 1)
                act.wait_ge(S["att_done"], k + 1)
                copy(attended.rearrange("p a b -> p (a b)"), pt[2][:, 512:1024]).then_inc(S["att_ready"], 1)
                act.wait_ge(S["attn_added"], k + 1)

            root(2)

            for k in range(LOG_W + 1, LOG_E + 1):
                turned(k)
                cur = level_start(k)[1]
                d = 2 ** (k - LOG_W - 1)
                n = k - LOG_W - 1
                for i in range(2):
                    act.wait_ge(S["up_done"], 2 * n + i + 1)
                    copy(pairs(half(1 - cur, i), d)[:, :, 1], pairs(pt[i][:], d)[:, :, 1])\
                        .then_inc(S["hi_ready"], 1)
                cur = level_down(k)[1]
                for i in range(2):
                    act.wait_ge(S["down_done"], 2 * n + i + 1)
                    copy(pairs(half(cur, i), P // 2)[:, :, 1], pairs(pt[2 + i][:], P // 2)[:, :, 1])\
                        .then_inc(S["hi_ready"], 1)

            act.wait_ge(S["norm_done"], 2)
            act.wait_ge(S["srt_out"], 32)
            act.wait_ge(S["heads_out"], 16)
            with act.Fori(0, NB) as k:
                copy(x2g[:], xn[:, bass.ds(k * GB, GB), :]).then_inc(S["ext_x_staged"], 1)
                act.wait_ge(S["ext_x_done"], k + 1)
                copy(xn2_t[:, bass.ds(k * GB * P, GB * P)], pt[0][0:F, :]).then_inc(S["ext_x_ready"], 1)
                copy(hidden[0:F, 0, :], pt[0][0:F, :]).then_inc(S["ext_x_ready"], 1)
                act.wait_ge(S["ext_done"], k + 1)
                copy(ext[:, bass.ds(k * GB, GB), :],
                     pt[1][:, 0:GB * EXT].rearrange("p (t c) -> p t c", c=EXT)).then_inc(S["ext_ready"], 1)

            act.wait_ge(S["weights_in"], 16 * 27)
            with act.Fori(0, NB) as k:
                for e in range(NE):
                    n = NE * k + e
                    act.wait_ge(S["hidden_done"], n + 1)
                    a.activation(hidden[:, e % 2, :], pt[e % 2][:], ACT.Gelu, bias=b1_s[:, e:e + 1])\
                     .then_inc(S["hidden_ready"], 1)
                    act.wait_ge(S["expert_done"], n + 1)
                    copy(experts[:, bass.ds(k * GB, GB), e, :],
                         pt[2][:, (e % 2) * 512:(e % 2 + 1) * 512].rearrange("p (t f) -> p t f", f=F))\
                        .then_inc(S["expert_ready"], 1)

            act.wait_ge(S["scatter_ready"], 1)
            chunks = act.value_load(chunks_i[0:1, 0:1], min_val=1, max_val=MAX_CHUNKS)
            act.sem_inc(S["rows_a_free"], 1)
            act.sem_inc(S["rows_b_free"], 1)
            with act.Fori(0, chunks) as k:
                for i, (rows, landed, free) in enumerate(((rows_a, "rows_a_in", "rows_a_free"),
                                                          (rows_b, "rows_b_in", "rows_b_free"))):
                    act.wait_ge(S[landed], GATHERS * (k + 1))
                    copy(h_s[:, :, i * HC2:(i + 1) * HC2], rows[:, :, 0:HC].rearrange("p c o -> p o c"))\
                        .then_inc(S["h_copied"], 1)
                    act.wait_ge(S["h_copied"], 2 * k + i + 1)
                    act.sem_inc(S[free], 1)
                act.wait_ge(S["exp_go"], 3 * k + 1)
                a.activation(keep, keep, ACT.Exp).then_inc(S["exp_done"], 1)
                act.wait_ge(S["exp_go"], 3 * k + 2)
                a.activation(wgt[:, 0:HEADS, :], wgt[:, 0:HEADS, :], ACT.Exp).then_inc(S["exp_done"], 1)
                act.wait_ge(S["exp_go"], 3 * k + 3)
                a.activation(passing[:], passing[:], ACT.Exp).then_inc(S["exp_done"], 1)
                act.wait_ge(S["res_ready"], k + 1)

            act.wait_ge(S["mg_go"], 1)
            a.activation(mg, mg, ACT.Exp).then_inc(S["mg_exp"], 1)
            act.wait_ge(S["var_go"], 1)
            a.activation(st2[:, 1], st2[:, 1], ACT.Sqrt).then_inc(S["sd_ready"], 1)
            act.wait_ge(S["gate_go"], 1)
            a.activation(sc, sc, ACT.Exp).then_inc(S["gate_exp"], 1)

        @block.tensor
        def _(pe):
            t = nc.tensor
            pe.wait_ge(S["weights_in"], 160)
            pe.wait_ge(S["ident_ready"], 1)
            t.matmul(pt[0][0:F, 0:F], wa[:], wb[:], start=True, stop=True)
            t.transpose(pt[0][0:F, 128:128 + F], wr[:], ident[0:F, 0:F])
            t.transpose(pt[0][0:HC, 256:256 + F], w_ext[:, 0:HC], ident[0:F, 0:F]).then_inc(S["prep_pe"], 1)
            pe.wait_ge(S["prep_act"], 3)
            pe.wait_ge(S["prep_dve"], 1)
            t.matmul(pt[1][0:F + 1, 0:F], wu[:], wr_t[:], start=True, stop=True)
            t.matmul(pt[1][0:F, 128:128 + 2 * HEADS], wg_t[:], att_sel[:].rearrange("p a b -> p (a b)"),
                     start=True, stop=True).then_inc(S["prep_pe"], 1)
            pe.wait_ge(S["prep_act"], 5)

            with pe.Fori(0, TILES // GA // 2) as k:
                for s in range(2):
                    i = 2 * k + s
                    hold(pe, f"frames_in{s}", 16 * (k + 1))
                    hold(pe, "logits_free", i + 1)
                    for j in range(GA * POOL // 2):
                        ins = t.transpose(pt[2 * s][:, j * P:(j + 1) * P],
                                          frames[s][:, j // 2, (j % 2) * P:(j % 2 + 1) * P], ident[:])
                    ins.then_inc(S["frames_t_done"], 1)
                    hold(pe, "frames_t_ready", i + 1)
                    for j in range(GA * POOL // 2):
                        ins = t.matmul(pt[2 * s + 1][:, j * P:(j + 1) * P], frames_t[s][:, j, :], tok_w2[:],
                                       start=True, stop=True)
                    ins.then_inc(S["logits_done"], 1)

            with pe.Fori(0, NB) as k:
                hold(pe, "x_staged", k + 1)
                for j in range(GB):
                    ins = t.transpose(pt[0][0:F, j * P:(j + 1) * P], xg[:, j, :], ident[:])
                ins.then_inc(S["x_t_done"], 1)
                hold(pe, "x_t_ready", k + 1)
                for j in range(2):
                    t.matmul(pt[1][0:F, j * 512:(j + 1) * 512], w_score[:], xg_t[0:F, j * 512:(j + 1) * 512],
                             start=True, stop=True)
                for j in range(GB):
                    ins = t.matmul(pt[2][:, j * F:(j + 1) * F], xg_t[:, j * P:(j + 1) * P], w_value[:],
                                   start=True, stop=True)
                ins.then_inc(S["t_done"], 1)
                hold(pe, "t_ready", 2 * k + 2)
                for j in range(GB):
                    ins = t.matmul(pt[3][:, j * P:(j + 1) * P], xg_t[0:F, j * P:(j + 1) * P],
                                   t_t[:, j * P:(j + 1) * P], start=True, stop=True)
                ins.then_inc(S["score_done"], 1)
                hold(pe, "score_masked", k + 1)
                for j in range(GB):
                    ins = t.matmul(pt[2][:, 512 + j * F:512 + (j + 1) * F], score[:, j, :], value[:, j, :],
                                   start=True, stop=True)
                ins.then_inc(S["att_done"], 1)
                hold(pe, "att_ready", k + 1)

            for k in range(LOG_W + 1, LOG_E + 1):
                cur = level_start(k)[1]
                for i in range(2):
                    pe.wait_ge(S["turned"], 2 * (k - LOG_W) + i + 1)
                    for b in range(HALF // P):
                        ins = t.transpose(pt[i][:, b * P:(b + 1) * P], half(1 - cur, i)[:, b * P:(b + 1) * P],
                                          ident[:])
                    ins.then_inc(S["up_done"], 1)
                ops, cur = level_down(k)
                for i in range(2):
                    pe.wait_ge(S["sorted_ops"], ops - 2 * (1 - i))
                    for b in range(HALF // P):
                        ins = t.transpose(pt[2 + i][:, b * P:(b + 1) * P], half(cur, i)[:, b * P:(b + 1) * P],
                                          ident[:])
                    ins.then_inc(S["down_done"], 1)
            pe.wait_ge(S["sorted_ops"], SORT_OPS)

            with pe.Fori(0, NB) as k:
                hold(pe, "ext_x_staged", k + 1)
                for j in range(GB):
                    ins = t.transpose(pt[0][0:F, j * P:(j + 1) * P], x2g[:, j, :], ident[:])
                ins.then_inc(S["ext_x_done"], 1)
                hold(pe, "ext_x_ready", 2 * k + 2)
                for j in range(GB):
                    ins = t.matmul(pt[1][:, j * EXT:(j + 1) * EXT], hidden[0:F, 0, j * P:(j + 1) * P], w_ext[:],
                                   start=True, stop=True)
                ins.then_inc(S["ext_done"], 1)
                hold(pe, "ext_ready", k + 1)

            pe.wait_ge(S["weights_in"], 16 * 27)
            with pe.Fori(0, NB) as k:
                for e in range(NE):
                    n = NE * k + e
                    for j in range(2):
                        ins = t.matmul(pt[e % 2][:, j * 512:(j + 1) * 512], w1_s[:, e, :],
                                       xn2_t[:, bass.ds(k * GB * P + j * 512, 512)], start=True, stop=True)
                    ins.then_inc(S["hidden_done"], 1)
                    hold(pe, "hidden_ready", n + 1)
                    o = pt[2][:, (e % 2) * 512:(e % 2 + 1) * 512]
                    t.matmul(o, ones_row[:], b2_row[:, e].rearrange("p a b -> p (a b)"), start=True, stop=False)
                    for j in range(GB):
                        ins = t.matmul(o[:, j * F:(j + 1) * F], hidden[:, e % 2, j * P:(j + 1) * P], w2_s[:, e, :],
                                       start=False, stop=(j == GB - 1))
                    ins.then_inc(S["expert_done"], 1)
                    hold(pe, "expert_ready", n + 1)

            pe.wait_ge(S["scatter_ready"], 1)
            chunks = pe.value_load(chunks_i[0:1, 0:1], min_val=1, max_val=MAX_CHUNKS)
            with pe.Fori(0, chunks) as k:
                for r, (n, state) in enumerate(((HEADS, state_d), (HEADS, state_m), (SUMS, state_s))):
                    hold(pe, "tail_ready", 3 * k + r + 1)
                    for j in range(2):
                        ins = t.transpose(pt[3][0:n, j * P:(j + 1) * P], tails[:, j, 0:n], ident[:])
                    ins.then_inc(S["tail_t"], 1)
                    hold(pe, "state_ready", 3 * k + r + 1)
                    t.transpose(pt[3][:, 512:512 + n], state[:, 0:P], ident[0:n, 0:n]).then_inc(S["carry_t"], 1)

        @block.vector
        def _(dve):
            v = nc.vector
            c1 = Counted(dve, S["v_chain"])
            link, mark = c1.link, c1.mark
            dve.wait_ge(S["lane_ready"], 1)
            for m in range(LOG_E - LOG_W + 1):
                last = v.tensor_scalar(lane_bit[:, m:m + 1], lane[:], m, 1, ALU.logical_shift_right,
                                       ALU.bitwise_and)
            link(last)
            link(v.tensor_scalar(sign[:], lane_bit[:], -2.0, 1.0, ALU.mult, ALU.add))
            v.tensor_copy(turn[:, 0:1], sign[:, 0:1])
            link(v.tensor_tensor(turn[:, 1:], sign[:, 0:-1], sign[:, 1:], ALU.mult))
            mark(v.memset(state_d[:], 0.0))
            mark(v.memset(state_m[:], -BIG))
            link(v.memset(state_s[:], 0.0))

            dve.wait_ge(S["edges_in"], 32)
            dst_w, src_w = sort[0][:].bitcast(I32), sort[1][:].bitcast(I32)
            far_w = xn[:].rearrange("p t f -> p (t f)").bitcast(I32)[:, 0:W]
            link(v.tensor_scalar(far_w, src_w, float(M - 1), float(FAR), ALU.is_ge, ALU.mult))
            mark(v.tensor_scalar(dst_w, dst_w, SRC_BITS, NODE, ALU.logical_shift_left, ALU.bitwise_or))
            link(v.tensor_scalar(src_w, src_w, float(M - 1), 0.0, ALU.min, ALU.max))
            link(v.tensor_tensor(dst_w, dst_w, far_w, ALU.bitwise_or))
            link(v.tensor_tensor(dst_w, dst_w, src_w, ALU.bitwise_or))
            dve.wait_ge(S["weights_in"], 160)
            dve.wait_ge(S["mask_ready"], 2)
            v.tensor_scalar(att_sel[:, 0], head_mask[:], att_col[:, 0:1], None, ALU.mult)
            v.tensor_scalar(att_sel[:, 1], head_mask[:], att_col[:, 1:2], None, ALU.mult).then_inc(S["prep_dve"], 1)

            ended = [0, 0]
            ops = 0

            def compare(halves, lo, hi, lesser, greater):
                nonlocal ops
                v.tensor_tensor(lesser, lo, hi, ALU.min).then_inc(S["sorted_ops"], 1)
                v.tensor_tensor(greater, lo, hi, ALU.max).then_inc(S["sorted_ops"], 1)
                ops += 2
                for i in halves:
                    ended[i] = ops

            def one_half(i, src, dst, d, hi=None):
                if ended[i]:
                    dve.wait_ge(S["sorted_ops"], ended[i])
                a, b = pairs(src, d), pairs(dst, d)
                compare((i,), a[:, :, 0], a[:, :, 1] if hi is None else pairs(hi, d)[:, :, 1],
                        b[:, :, 0], b[:, :, 1])

            def both_halves(cur, d):
                for i in range(2):
                    one_half(i, half(cur, i), half(1 - cur, i), d)
                return 1 - cur

            def across_halves(cur):
                dve.wait_ge(S["sorted_ops"], max(ended))
                compare((0, 1), half(cur, 0), half(cur, 1), half(1 - cur, 0), half(1 - cur, 1))
                return 1 - cur

            def shift_logits(i):
                s = i % 2
                lg = pt[2 * s + 1][:].rearrange("p (t w f) -> p t w f", w=POOL, f=F)
                most = tree[s][:, :, 2]
                dve.wait_ge(S["logits_done"], i + 1)
                if i >= 2:
                    dve.wait_ge(S["pooled"], 2 * (i - 1))
                v.tensor_reduce(most, lg.rearrange("p t w f -> p t f w"), AX.X, ALU.max).then_inc(S["pool_max"], 1)
                dve.wait_ge(S["pool_max"], i + 1)
                v.tensor_tensor(logits[s], lg, most.unsqueeze(2).broadcast_to([P, GA, POOL, F]), ALU.subtract)\
                 .then_inc(S["shifted"], 1)
                dve.wait_ge(S["shifted"], i + 1)
                dve.sem_inc(S["logits_free"], 1)

            dve.sem_inc(S["frames_free"], 2)
            dve.sem_inc(S["logits_free"], 2)
            cur, stages = 0, 0
            for k in range(1, LOG_W):
                for j in range(k - 1, -1, -1):
                    if ops:
                        dve.wait_ge(S["sorted_ops"], ops)
                    a, b = (sort[s][:].rearrange("p (u r a t s) -> p u r a t s", r=2, a=2 ** (k - j - 1), t=2,
                                                 s=2 ** j) for s in (cur, 1 - cur))
                    for r in range(2):
                        compare((0, 1), a[:, :, r, :, 0], a[:, :, r, :, 1], b[:, :, r, :, r], b[:, :, r, :, 1 - r])
                    cur = 1 - cur
                    stages += 1
                    if stages % 3 == 0 and stages // 3 <= TILES // GA:
                        shift_logits(stages // 3 - 1)

            def normalise(n):
                mean, sd = stat[:, 0], stat[:, 1]

                def over(ap):
                    return ap.unsqueeze(2).broadcast_to([P, TILES, F])
                link(v.tensor_reduce(mean, h[:], AX.X, ALU.add))
                link(v.tensor_scalar(mean, mean, 1.0 / F, None, ALU.mult))
                link(v.tensor_tensor(xn[:], h[:], over(mean), ALU.subtract))
                link(v.tensor_tensor(square, xn[:], xn[:], ALU.mult))
                link(v.tensor_reduce(sd, square, AX.X, ALU.add))
                v.tensor_scalar(sd, sd, 1.0 / F, EPS, ALU.mult, ALU.add).then_inc(S["norm_var"], 1)
                dve.wait_ge(S["norm_sd"], n)
                link(v.reciprocal(sd, sd))
                v.tensor_tensor(xn[:], xn[:], over(sd), ALU.mult).then_inc(S["norm_done"], 1)

            dve.wait_ge(S["pooled"], 2 * (TILES // GA))
            link(v.reciprocal(xn[:], xn[:]))
            link(v.tensor_tensor(h[:], h[:], xn[:], ALU.mult))
            normalise(1)

            cur = 1 - cur
            dve.wait_ge(S["turned"], 2)
            cur = across_halves(cur)
            for j in range(LOG_W - 2, -1, -1):
                cur = both_halves(cur, 2 ** j)
            assert (ops, cur) == level_start(LOG_W + 1)

            dve.wait_ge(S["attn_added"], NB)
            normalise(2)

            for k in range(LOG_W + 1, LOG_E + 1):
                n = k - LOG_W - 1
                for i in range(2):
                    dve.wait_ge(S["hi_ready"], 4 * n + i + 1)
                    one_half(i, pt[i][:], half(cur, i), 2 ** n, hi=half(1 - cur, i))
                for m in range(n - 1, -1, -1):
                    cur = both_halves(cur, 2 ** m)
                cur = across_halves(cur)
                for d in (4 * P, 2 * P, P):
                    cur = both_halves(cur, d)
                assert (ops, cur) == level_down(k)
                for i in range(2):
                    dve.wait_ge(S["hi_ready"], 4 * n + i + 3)
                    one_half(i, pt[2 + i][:], half(1 - cur, i), P // 2, hi=half(cur, i))
                cur = 1 - cur
                for m in range(5, -1, -1):
                    cur = both_halves(cur, 2 ** m)
            assert (ops, cur) == (SORT_OPS, SORT_END)

            dve.wait_ge(S["node_ready"], 1)
            mark(v.tensor_copy(node_f[:], node_i[:]))
            link(v.tensor_scalar(goal[:, 0], node_i[:], SRC_BITS, NODE, ALU.logical_shift_left, ALU.bitwise_or))
            link(v.tensor_scalar(goal[:, 1], goal[:, 0], FAR, None, ALU.bitwise_or))
            dve.wait_ge(S["heads_in"], 16)
            goal_f = goal[:].bitcast(F32)

            def heads_under(cls):
                for t in range(NS):
                    link(v.tensor_scalar(less[:], heads_all[:], goal_f[:, cls, t:t + 1], 0.0, ALU.is_lt, ALU.add,
                                         accum_out=row_f[:, cls, t:t + 1]))
                link(v.tensor_scalar(row_f[:, cls], row_f[:, cls], 1.0, 0.0, ALU.subtract, ALU.max))
                v.tensor_copy(row_i[:, cls], row_f[:, cls]).then_inc(S["row_idx"], 1)

            def words_under(cls):
                for t in range(NS):
                    n = cls * NS + t
                    dve.wait_ge(slots[n % RING], 16 * (n // RING + 1))
                    v.tensor_scalar(less[:], ring[n % RING], goal_f[:, cls, t:t + 1], 0.0, ALU.is_lt, ALU.add,
                                    accum_out=lower[:, cls, t:t + 1]).then_inc(S["row_used"], 1)
                    dve.wait_ge(S["row_used"], n + 1)
                v.scalar_tensor_tensor(lower[:, cls], row_f[:, cls], float(STEP), lower[:, cls], ALU.mult,
                                       ALU.add).then_inc(S["bound_ready"], 1)
                dve.wait_ge(S["bound_ready"], cls + 1)

            def counts(cls):
                dve.wait_ge(S["shift_in"], 48 * (cls + 1))
                link(v.tensor_tensor(count[:, cls], nxt[:, cls], lower[:, cls, 0:TILES], ALU.subtract))
                link(v.tensor_scalar(has[:, cls], count[:, cls], 0.0, None, ALU.is_gt))

            heads_under(0)
            words_under(0)
            link(v.tensor_scalar(chunks_f[:], lower[0:1, 0, TILES:NS], float(CHUNK - 1), float(CHUNK), ALU.add,
                                 ALU.max))
            link(v.tensor_copy(chunks_i[:], chunks_f[:]))
            link(v.tensor_scalar(chunks_i[:], chunks_i[:], CHUNK.bit_length() - 1, None, ALU.logical_shift_right))
            counts(0)
            link(v.tensor_scalar(start_f[:], node_f[:, 0:TILES], float(E), None, ALU.add))
            link(v.tensor_tensor(stat[:, 0], lower[:, 0, 0:TILES], start_f[:], ALU.subtract))
            link(v.tensor_tensor(stat[:, 0], stat[:, 0], has[:, 0], ALU.mult))
            link(v.tensor_tensor(start_f[:], start_f[:], stat[:, 0], ALU.add))
            link(v.tensor_scalar(stat[:, 1], nxt[:, 0], 1.0, 0.0, ALU.subtract, ALU.max))
            link(v.tensor_copy(end_i[:], stat[:, 1]))
            v.tensor_copy(start_i[:], start_f[:]).then_inc(S["scatter_ready"], 1)
            heads_under(1)

            dve.wait_ge(S["scatter_ready"], 1)
            dve.wait_ge(S["keys_in"], 16)

            def segments(ch):
                ch.link(v.tensor_scalar(segs[:], keys[:], SRC_BITS, None, ALU.logical_shift_right))
                ch.link(v.tensor_tensor(same_next[:], segs[:, 1:], segs[:, 0:C], ALU.is_equal))

            def sources(ch, idx, first, ready):
                ch.mark(v.tensor_scalar(idx[:], keys[:, 1 + first:1 + first + HC2], M - 1, None, ALU.bitwise_and))
                dve.wait_ge(ch.s, ch.first + ch.n)
                dve.sem_inc(S[ready], 1)

            segments(c1)
            sources(c1, src_a, 0, "idx_a")
            sources(c1, src_b, HC2, "idx_b")
            dve.sem_inc(S["keys_free"], 1)
            dve.sem_inc(S["inj_free"], 1)
            dve.sem_inc(S["res_out"], 16)
            dve.sem_inc(S["rows_a_free"], 1)
            dve.sem_inc(S["rows_b_free"], 1)
            chunks = dve.value_load(chunks_i[0:1, 0:1], min_val=1, max_val=MAX_CHUNKS)
            EDGE_OPS = 89
            with dve.Fori(0, chunks) as k:
                ch = Counted(dve, S["e_chain"], k * EDGE_OPS)

                def carried(r, n, state, op, to):
                    dve.wait_ge(S["tail_t"], 3 * k + r + 1)
                    ch.mark(v.tensor_copy(state[:, 0:1], state[:, P:P + 1]))
                    ch.link(v.tensor_copy(across[0:n], pt[3][0:n, 0:2 * P].rearrange("p (a b) -> p a b", a=2)))
                    v.tensor_tensor_scan(state[:, 1:P + 1], across[0:n, 1, :], across[0:n, 0, :], state[:, 0:1],
                                         op[0], op[1]).then_inc(S["state_ready"], 1)
                    dve.wait_ge(S["carry_t"], 3 * k + r + 1)
                    ch.link(v.tensor_copy(to, pt[3][:, 512:512 + n]))

                SUM, TOP = (ALU.mult, ALU.add), (ALU.add, ALU.max)
                ch.link(v.tensor_copy(same[:], same_next[:]))
                ch.mark(v.tensor_scalar(fence[:], same[:], 1.0, BIG, ALU.subtract, ALU.mult))
                ch.mark(v.tensor_reduce(lasts[:], same[:], AX.X, ALU.min))
                dve.wait_ge(S["keys_in"], 16 * (k + 2))
                segments(ch)
                dve.wait_ge(S["inj_in"], 16 * (k + 1))
                for i in range(HEADS):
                    ch.mark(v.tensor_tensor_scan(a_d[:, i], same[:], inj[:, :, i], 0.0, *SUM))
                dve.wait_ge(ch.s, ch.first + ch.n)
                ch.link(v.tensor_copy(tails[:, 0, 0:HEADS], a_d[:, :, C - 1]))
                v.tensor_copy(tails[:, 1, 0:HEADS], lasts[:].broadcast_to([P, HEADS])).then_inc(S["tail_ready"], 1)
                carried(0, HEADS, state_d, SUM, carry_d[:])
                for i in range(HEADS):
                    ch.mark(v.tensor_tensor_scan(a_d[:, i], same[:], inj[:, :, i], carry_d[:, i:i + 1], *SUM))
                dve.wait_ge(ch.s, ch.first + ch.n)
                dve.sem_inc(S["inj_free"], 1)
                for i, (rows, landed, free, idx, ready) in enumerate((
                    (rows_a, "rows_a_in", "rows_a_free", src_a, "idx_a"),
                    (rows_b, "rows_b_in", "rows_b_free", src_b, "idx_b"),
                )):
                    dve.wait_ge(S[landed], GATHERS * (k + 1))
                    sources(ch, idx, i * HC2, ready)
                    ch.link(v.tensor_copy(a_s[:, :, i * HC2:(i + 1) * HC2],
                                          rows[:, :, HC:ROW].rearrange("p c o -> p o c")))
                    dve.sem_inc(S[free], 1)
                dve.sem_inc(S["keys_free"], 1)
                ch.link(v.tensor_tensor(logit, a_s[:], a_d[:], ALU.add))
                ch.link(v.scalar_tensor_tensor(logit, logit, 0.2, logit, ALU.mult, ALU.max))
                for i in range(HEADS):
                    ch.mark(v.tensor_tensor_scan(top[:, i, 1:], fence[:], logit[:, i], -BIG, *TOP))
                dve.wait_ge(ch.s, ch.first + ch.n)
                ch.mark(v.tensor_copy(tails[:, 0, 0:HEADS], top[:, :, C]))
                ch.link(v.tensor_scalar(lasts[:], lasts[:], 1.0, BIG, ALU.subtract, ALU.mult))
                v.tensor_copy(tails[:, 1, 0:HEADS], lasts[:].broadcast_to([P, HEADS])).then_inc(S["tail_ready"], 1)
                carried(1, HEADS, state_m, TOP, carry_m[:])
                ch.mark(v.tensor_copy(top[:, :, 0], carry_m[:]))
                for i in range(HEADS):
                    ch.mark(v.tensor_tensor_scan(top[:, i, 1:], fence[:], logit[:, i], carry_m[:, i:i + 1], *TOP))
                dve.wait_ge(ch.s, ch.first + ch.n)
                ch.link(v.tensor_tensor(keep, top[:, :, 0:C], top[:, :, 1:], ALU.subtract))
                v.tensor_scalar(keep, keep, 0.0, None, ALU.min).then_inc(S["exp_go"], 1)
                v.tensor_tensor(wgt[:, 0:HEADS], logit, top[:, :, 1:], ALU.subtract).then_inc(S["exp_go"], 1)
                ch.link(v.tensor_tensor(passing[:], carry_m[:], top[:, :, C], ALU.subtract))
                v.scalar_tensor_tensor(passing[:], passing[:], 0.0, lasts[:].broadcast_to([P, HEADS]), ALU.min,
                                       ALU.add).then_inc(S["exp_go"], 1)
                dve.wait_ge(S["exp_done"], 3 * k + 1)
                ch.mark(v.tensor_tensor(keep, keep, same[:].unsqueeze(1).broadcast_to([P, HEADS, C]), ALU.mult))
                dve.wait_ge(S["exp_done"], 3 * k + 2)
                dve.wait_ge(S["h_copied"], 2 * k + 2)
                for i in range(HEADS):
                    ch.mark(v.tensor_tensor(wgt[:, HEADS + NE * i:HEADS + NE * (i + 1)], h_s[:, NE * i:NE * (i + 1)],
                                            wgt[:, i:i + 1].broadcast_to([P, NE, C]), ALU.mult))
                dve.wait_ge(ch.s, ch.first + ch.n)

                def head(c):
                    return c if c < HEADS else (c - HEADS) // NE

                for c in range(SUMS):
                    ch.mark(v.tensor_tensor_scan(part[:, c], keep[:, head(c)], wgt[:, c], 0.0, *SUM))
                dve.wait_ge(ch.s, ch.first + ch.n)
                dve.wait_ge(S["exp_done"], 3 * k + 3)
                ch.mark(v.tensor_copy(tails[:, 0, :], part[:, :, C - 1]))
                ch.mark(v.tensor_copy(tails[:, 1, 0:HEADS], passing[:]))
                v.tensor_copy(tails[:, 1, HEADS:].rearrange("p (a b) -> p a b", b=NE),
                              passing[:].unsqueeze(2).broadcast_to([P, HEADS, NE])).then_inc(S["tail_ready"], 1)
                carried(2, SUMS, state_s, SUM, carry_s[:])
                dve.wait_ge(S["res_out"], 16 * (k + 1))
                for c in range(SUMS):
                    ch.mark(v.tensor_tensor_scan(results_s[:, :, HEADS + c], keep[:, head(c)], wgt[:, c],
                                                 carry_s[:, c:c + 1], *SUM))
                v.tensor_copy(results_s[:, :, 0:HEADS].rearrange("p c o -> p o c"), top[:, :, 1:])\
                 .then_inc(S["res_ready"], 1)
                dve.wait_ge(S["res_ready"], k + 1)
                assert ch.n == EDGE_OPS, ch.n

            words_under(1)
            counts(1)

            cf = Counted(dve, S["f_chain"])
            link, mark = cf.link, cf.mark

            def by_head(ap):
                return ap.unsqueeze(2).broadcast_to([P, TILES, HEADS])

            def last_row(lo, hi):
                return clamped[:, lo:hi].unsqueeze(1).broadcast_to([P, TILES, hi - lo])

            a_dst = ext[:, :, ROW:EXT]
            dve.wait_ge(S["clamped_in"], 16)
            link(v.tensor_tensor(mg[:, 1], ext[:, :, HC:ROW], a_dst, ALU.add))
            link(v.tensor_tensor(mg[:, 2], a_dst, last_row(HC, ROW), ALU.add))
            link(v.scalar_tensor_tensor(mg[:, 1:3], mg[:, 1:3], 0.2, mg[:, 1:3], ALU.mult, ALU.max))
            link(v.tensor_scalar(has[:], has[:], 1.0, BIG, ALU.subtract, ALU.mult))
            link(v.tensor_tensor(mg[:, 2], mg[:, 2], by_head(has[:, 1]), ALU.add))
            dve.wait_ge(S["ends_in"], 16 * TILES)
            link(v.tensor_tensor(mg[:, 0], ends[:, :, 0:HEADS], by_head(has[:, 0]), ALU.add))
            link(v.tensor_tensor(mtop, mg[:, 0], mg[:, 1], ALU.max))
            link(v.tensor_tensor(mtop, mtop, mg[:, 2], ALU.max))
            v.tensor_tensor(mg, mg, mtop.unsqueeze(1).broadcast_to([P, 3, TILES, HEADS]),
                            ALU.subtract).then_inc(S["mg_go"], 1)
            dve.wait_ge(S["mg_exp"], 1)
            link(v.tensor_tensor(mg[:, 2], mg[:, 2], by_head(count[:, 1]), ALU.mult))
            total = mtop
            mark(v.tensor_tensor(total, ends[:, :, HEADS:2 * HEADS], mg[:, 0], ALU.mult))
            agg = ends[:, :, 2 * HEADS:]

            def heads4(ap):
                return ap.rearrange("p t (h c) -> p t h c", c=NE)

            def wide(ap):
                return ap.unsqueeze(3).broadcast_to([P, TILES, HEADS, NE])

            tmp = xn[:, :, 0:HC]
            tmp2 = xn[:, :, HC:2 * HC]
            for i in range(HEADS):
                s4 = slice(NE * i, NE * (i + 1))

                def w(j):
                    return mg[:, j, :, i:i + 1].broadcast_to([P, TILES, NE])
                mark(v.tensor_tensor(agg[:, :, s4], agg[:, :, s4], w(0), ALU.mult))
                mark(v.tensor_tensor(tmp[:, :, s4], ext[:, :, s4], w(1), ALU.mult))
                mark(v.tensor_tensor(tmp2[:, :, s4], w(2), last_row(NE * i, NE * (i + 1)), ALU.mult))
            dve.wait_ge(S["f_chain"], cf.n)
            mark(v.tensor_tensor(total, total, mg[:, 1], ALU.add))
            link(v.tensor_tensor(agg, agg, tmp, ALU.add))
            mark(v.tensor_tensor(total, total, mg[:, 2], ALU.add))
            link(v.tensor_tensor(agg, agg, tmp2, ALU.add))
            link(v.tensor_scalar(total, total, 1e-16, None, ALU.add))
            link(v.reciprocal(total, total))
            for i in range(HEADS):
                s4 = slice(NE * i, NE * (i + 1))
                mark(v.tensor_tensor(agg[:, :, s4], agg[:, :, s4], total[:, :, i:i + 1].broadcast_to([P, TILES, NE]),
                                     ALU.mult))
            dve.wait_ge(S["f_chain"], cf.n)

            def per_row(ap):
                return ap[:].unsqueeze(1).broadcast_to([P, TILES, HC])

            def per_token(ap, n=HC):
                return ap.unsqueeze(2).broadcast_to([P, TILES, n])

            dve.wait_ge(S["weights_in"], 16 * 27)
            link(v.tensor_tensor(agg, agg, per_row(bg), ALU.add))
            mean, sd = st2[:, 0], st2[:, 1]
            link(v.tensor_reduce(mean, agg, AX.X, ALU.add))
            link(v.tensor_scalar(mean, mean, 1.0 / HC, None, ALU.mult))
            link(v.tensor_tensor(agg, agg, per_token(mean), ALU.subtract))
            link(v.tensor_tensor(tmp, agg, agg, ALU.mult))
            link(v.tensor_reduce(sd, tmp, AX.X, ALU.add))
            v.tensor_scalar(sd, sd, 1.0 / HC, EPS, ALU.mult, ALU.add).then_inc(S["var_go"], 1)
            dve.wait_ge(S["sd_ready"], 1)
            link(v.reciprocal(sd, sd))
            link(v.tensor_tensor(agg, agg, per_token(sd), ALU.mult))
            link(v.tensor_tensor(agg, agg, per_row(gamma), ALU.mult))
            link(v.tensor_tensor(agg, agg, per_row(beta), ALU.add))
            link(v.tensor_reduce(sc, agg.rearrange("p t (h c) -> p t c h", c=NE), AX.X, ALU.add))
            link(v.tensor_scalar(sc, sc, 1.0 / HEADS, None, ALU.mult))
            link(v.memset(cmp, 0.0))
            for i in range(NE):
                for j in range(i + 1, NE):
                    link(v.tensor_tensor(mtop[:, :, 0], sc[:, :, j], sc[:, :, i], ALU.is_gt))
                    mark(v.tensor_tensor(cmp[:, :, i], cmp[:, :, i], mtop[:, :, 0], ALU.add))
                    link(v.tensor_scalar(mtop[:, :, 1], mtop[:, :, 0], -1.0, 1.0, ALU.mult, ALU.add))
                    link(v.tensor_tensor(cmp[:, :, j], cmp[:, :, j], mtop[:, :, 1], ALU.add))
            link(v.tensor_reduce(mean, sc, AX.X, ALU.max))
            v.tensor_tensor(sc, sc, per_token(mean, NE), ALU.subtract).then_inc(S["gate_go"], 1)
            link(v.tensor_scalar(cmp, cmp, 1.5, None, ALU.is_lt))
            dve.wait_ge(S["gate_exp"], 1)
            link(v.tensor_tensor(gate, sc, cmp, ALU.mult))
            link(v.tensor_reduce(mean, gate, AX.X, ALU.add))
            link(v.reciprocal(mean, mean))
            link(v.tensor_tensor(gate, gate, per_token(mean, NE), ALU.mult))
            dve.wait_ge(S["expert_ready"], NE * NB)
            q = TILES // 4
            for i in range(4):
                s = slice(i * q, (i + 1) * q)
                for e in range(NE):
                    mark(v.tensor_tensor(experts[:, s, e], experts[:, s, e],
                                         gate[:, s, e:e + 1].broadcast_to([P, q, F]), ALU.mult))
                dve.wait_ge(S["f_chain"], cf.n)
                link(v.tensor_tensor(experts[:, s, 0:2], experts[:, s, 0:2], experts[:, s, 2:4], ALU.add))
                mark(v.tensor_tensor(h[:, s, :], h[:, s, :], experts[:, s, 0], ALU.add))
                dve.wait_ge(S["f_chain"], cf.n)
                v.tensor_tensor(h[:, s, :], h[:, s, :], experts[:, s, 1], ALU.add).then_inc(S["y_done"], 1)


_INS = ["x", "L0_tok_W", "L0_attn_W_alpha", "L0_attn_W_beta", "L0_attn_W_unary", "L0_attn_b_unary",
        "L0_attn_W_r", "L0_ffn_W_gat", "L0_ffn_att_src", "L0_ffn_att_dst", "L0_ffn_b_gat",
        "L0_ffn_ln_gamma", "L0_ffn_ln_beta", "L0_ffn_W1", "L0_ffn_b1", "L0_ffn_W2", "L0_ffn_b2",
        "L0_ffn_edge_index"]


def kernel(**inputs):
    import concourse.bacc as bacc
    from concourse.bass_utils import run_bass_kernel_spmd

    nc = bacc.Bacc("TRN2", target_bir_lowering=False, num_devices=1)
    arrays, args = {}, []
    for name in _INS:
        a = np.ascontiguousarray(inputs[name])
        arrays[f"in_{name}"] = a
        args.append(nc.dram_tensor(f"in_{name}", a.shape, mybir.dt.from_np(a.dtype), kind="ExternalInput").ap())
    b, l, f = inputs["x"].shape
    args.append(nc.dram_tensor("out_0", (b, l // 4, f), F32, kind="ExternalOutput").ap())
    audio_tower(nc, *args)
    r = run_bass_kernel_spmd(nc, [arrays], core_ids=[0])
    return r.results[0]["out_0"]
```

```python
import numpy as np
from contextlib import ExitStack

import concourse.bass as bass
from concourse import mybir

F32 = mybir.dt.float32
I32 = mybir.dt.int32
BF16 = mybir.dt.bfloat16
ALU = mybir.AluOpType
ACT = mybir.ActivationFunctionType
AX = mybir.AxisListType


def audio_tower(nc, x, tok_w, w_alpha, w_beta, w_unary, b_unary, w_r, w_gat, att_src, att_dst,
                b_gat, ln_gamma, ln_beta, w1, b1, w2, b2, edges, out):
    P = 128
    B, L, F = x.shape
    POOL = 4
    SEQ = L // POOL
    M = B * SEQ
    TILES = M // P
    E = edges.shape[1]
    W = E // P
    HALF = W // 2
    NE, _, HID = w1.shape
    HEADS = att_src.shape[0]
    HC = HEADS * NE
    ROW = HC + HEADS
    EXT = HC + 2 * HEADS
    EPS = 1e-5
    BIG = 1e30

    SRC_BITS = M.bit_length() - 1
    NODE = 1 << (2 * SRC_BITS + 2)
    FAR = 1 << (2 * SRC_BITS + 1)
    TILE_BIT = SRC_BITS + P.bit_length() - 1
    LOG_W, LOG_E = W.bit_length() - 1, E.bit_length() - 1
    STEP = 512
    HEADS_N = E // STEP
    C = 32
    HC2 = C // 2
    CHUNK = P * C
    MAX_CHUNKS = E // CHUNK
    PAD = 64
    OUTC = HEADS + HEADS + HC
    SUMS = HEADS + HC
    NS = TILES + 1
    RING = 4

    GA = 4
    GB = 4
    NB = TILES // GB
    GE = 8
    NG = TILES // GE

    sorted_rows = nc.dram_tensor("sorted_rows", (HEADS_N, STEP), F32).ap()
    sorted_padded = nc.dram_tensor("sorted_padded", (PAD + E + CHUNK,), F32).ap()
    table = nc.dram_tensor("table", (M, ROW), F32).ap()
    inject = nc.dram_tensor("inject", (E + M, HEADS), F32).ap()
    results = nc.dram_tensor("results", (E, OUTC), F32).ap()

    with ExitStack() as ctx:
        def sb(name, shape, dt=F32):
            return ctx.enter_context(nc.sbuf_tensor(name, shape, dt))

        def sem(name):
            return ctx.enter_context(nc.semaphore(name))

        ident = sb("ident", [P, P])
        lane = sb("lane", [P, 1], I32)
        lane_bit = sb("lane_bit", [P, LOG_E - LOG_W + 1], I32)
        sign = sb("sign", [P, LOG_E - LOG_W + 1])
        turn = sb("turn", [P, LOG_E - LOG_W + 1])
        pair_mask = sb("pair_mask", [P, P])
        zeros = sb("zeros", [P, 528])
        node_i = sb("node_i", [P, NS], I32)
        node_f = sb("node_f", [P, NS])
        tok_w2 = sb("tok_w2", [P, P])
        wa = sb("wa", [F, F])
        wb = sb("wb", [F, F])
        wu = sb("wu", [F, F + 1])
        wr = sb("wr", [F, F])
        wr_t = sb("wr_t", [F, F])
        w_score = sb("w_score", [F, F])
        w_value = sb("w_value", [F + 1, F])
        w_ext = sb("w_ext", [F, EXT])
        wg_t = sb("wg_t", [HC, F])
        att_col = sb("att_col", [HC, 2])
        att_sel = sb("att_sel", [HC, 2, HEADS])
        head_mask = sb("head_mask", [HC, HEADS])
        w1_s = sb("w1_s", [F, NE, HID])
        w2_s = sb("w2_s", [HID, NE, F])
        b1_s = sb("b1_s", [HID, NE])
        b2_row = sb("b2_row", [1, 3, NE * F])
        b2_part = sb("b2_part", [1, 3, NE, F], BF16)
        b2_rows = sb("b2_rows", [3, NE, GE, F], BF16)
        ones_row = sb("ones_row", [3, P], BF16)
        bg = sb("bg", [P, HC])
        gamma = sb("gamma", [P, HC])
        beta = sb("beta", [P, HC])

        sort = [sb("sort0", [P, W]), sb("sort1", [P, W])]
        h = sb("h", [P, TILES, F])
        xn = sb("xn", [P, TILES, F])
        xn2_t = sb("xn2_t", [F, M])
        arena = sb("arena", [P, TILES * NE * F])
        ext = sb("ext", [P, TILES, EXT])
        ends = sb("ends", [P, TILES, OUTC])
        stat = sb("stat", [P, 2, TILES])
        nxt = sb("nxt", [P, 2, TILES])
        lower = sb("lower", [P, 2, NS])
        row_f = sb("row_f", [P, 2, NS])
        row_i = sb("row_i", [P, 2, NS], I32)
        goal = sb("goal", [P, 2, NS], I32)
        count = sb("count", [P, 2, TILES])
        has = sb("has", [P, 2, TILES])
        start_f = sb("start_f", [P, TILES])
        start_i = sb("start_i", [P, TILES], I32)
        end_i = sb("end_i", [P, TILES], I32)
        chunks_f = sb("chunks_f", [1, 1])
        chunks_i = sb("chunks_i", [1, 1], I32)

        def carve(base, at, *shape, partitions=P):
            size = int(np.prod(shape))
            ap = base[0:partitions, at:at + size]
            names = "abcd"[:len(shape)]
            if len(shape) > 1:
                ap = ap.rearrange(f"p ({' '.join(names)}) -> p {' '.join(names)}",
                                  **{n: s for n, s in zip(names[1:], shape[1:])})
            return ap, at + size

        at = 0
        frames, frames_t, logits, tree = [], [], [], []
        for s in range(2):
            a, at = carve(arena, at, GA, POOL * F)
            frames.append(a)
            a, at = carve(arena, at, GA * POOL // 2, P)
            frames_t.append(a)
            a, at = carve(arena, at, GA, POOL, F)
            logits.append(a)
            a, at = carve(arena, at, GA, 3, F)
            tree.append(a)
        def several(n, at, *shape, **kw):
            made = []
            for _ in range(n):
                a, at = carve(arena, at, *shape, **kw)
                made.append(a)
            return made, at

        x_t, at = several(3, at, GB * P, partitions=F + 1)
        t_t, at = several(2, at, GB * P, partitions=F)
        value, at = several(3, at, GB, F)
        score, at = several(2, at, GB, P)
        attended, at = several(2, at, GB, F)
        assert at <= TILES * NE * F
        lane_row_i, at = carve(arena, at, P)
        tile_row_i, at = carve(arena, at, 2, NS)
        lane_row_i, tile_row_i = lane_row_i.bitcast(I32), tile_row_i.bitcast(I32)
        square = arena[:, 0:TILES * F].rearrange("p (t f) -> p t f", f=F)
        experts = arena[:, :].rearrange("p (t e f) -> p t e f", e=NE, f=F)
        hidden = [ends[:].rearrange("p t o -> p (t o)")[:, 0:GE * P], sb("hidden", [P, GE * P])[:]]

        keys = sb("keys", [P, C + 1], I32)
        segs = sb("segs", [P, C + 1], I32)
        same_next = sb("same_next", [P, C])
        same = sb("same", [P, C])
        src_a = sb("src_a", [P, HC2], I32)
        src_b = sb("src_b", [P, HC2], I32)
        rows_a = sb("rows_a", [P, HC2, ROW])
        rows_b = sb("rows_b", [P, HC2, ROW])
        inj = sb("inj", [P, C, HEADS])
        fence = sb("fence", [P, C])
        lasts = sb("lasts", [P, 1])
        a_s = sb("a_s", [P, HEADS, C])
        a_d = sb("a_d", [P, HEADS, C])
        top = sb("top", [P, HEADS, C + 1])
        xn_flat = xn[:].rearrange("p t f -> p (t f)")
        at = 0
        h_s, at = carve(xn_flat, at, HC, C)
        wgt, at = carve(xn_flat, at, SUMS, C)
        part, at = carve(xn_flat, at, SUMS, C)
        logit, at = carve(xn_flat, at, HEADS, C)
        keep, at = carve(xn_flat, at, HEADS, C)
        assert at <= TILES * F
        results_s = sb("results_s", [P, C, OUTC])
        tails = sb("tails", [P, 2, SUMS])
        passing = sb("passing", [P, HEADS])
        across = sb("across", [SUMS, 2, P])
        state_d = sb("state_d", [HEADS, P + 1])
        state_m = sb("state_m", [HEADS, P + 1])
        state_s = sb("state_s", [SUMS, P + 1])
        carry_d = sb("carry_d", [P, HEADS])
        carry_m = sb("carry_m", [P, HEADS])
        carry_s = sb("carry_s", [P, SUMS])
        clamped = sb("clamped", [P, ROW])

        at = 0
        mg, at = carve(sort[0], at, 3, TILES, HEADS)
        mtop, at = carve(sort[0], at, TILES, HEADS)
        cmp, at = carve(sort[0], at, TILES, NE)
        gate, at = carve(sort[0], at, TILES, NE)
        sc, at = carve(sort[0], at, TILES, NE)
        st2 = sb("st2", [P, 2, TILES])

        HPP = HEADS_N // P
        head_lane_i = sb("head_lane_i", [P, HPP], I32)
        head_tile_i = sb("head_tile_i", [P, HPP], I32)
        head_lane = sb("head_lane", [P, HPP])
        head_tile = sb("head_tile", [P, HPP])
        lane_row = sb("lane_row", [P, P])
        tile_row = sb("tile_row", [P, 2, NS])
        lane_over = sb("lane_over", [P, HPP, P], BF16)
        tile_same = sb("tile_same", [P, HPP, 2 * NS], BF16)
        tile_over = sb("tile_over", [P, HPP, 2 * NS], BF16)
        ones_sq = sb("ones_sq", [P, P], BF16)
        ring = [sort[0][:, i * STEP:(i + 1) * STEP] for i in range(RING)]
        less = sb("less", [P, STEP], mybir.dt.bfloat16)

        pt = [ctx.enter_context(nc.psum_tensor(f"pt{i}", [P, 1024], F32)) for i in range(4)]

        names = """weights_in edges_in frames_in0 frames_in1 lane_ready ident_ready mask_ready
            node_ready zeros_ready prep_pe prep_act prep_dve v_chain sorted_ops turned up_done down_done
            hi_ready frames_free frames_t_done frames_t_ready logits_done logits_free shifted pool_exp
            pool_steps pool_max pooled p_chain norm_var norm_sd norm_done x_t_done x_t_ready t_done t_ready
            score_done score_ready score_masked att_done att_ready attn_added ext_x_done
            ext_x_ready ext_done ext_ready hidden_done hidden_ready expert_done expert_ready
            b2_in b2_split srt_out heads_split heads_counted row_idx row_in0 row_in1 row_in2 row_in3 row_used bound_ready shift_in table_out zero_out scatter_ready scattered
            keys_in keys_free inj_in inj_free idx_a idx_b rows_a_in rows_b_in rows_a_free rows_b_free
            e_chain h_copied tail_ready tail_t state_ready carry_t exp_go exp_done res_ready res_out
            far_idx ends_idx ends_in clamped_in mg_go mg_exp f_chain var_go sd_ready gate_go gate_exp
            y_done out_done pad_out results_zero held_pe held_pool""".split()
        S = {n: sem(n) for n in names}

        def hold(eng, name, value):
            eng.wait_ge(S[name], value)
            eng.sem_inc(S["held_" + ("pe" if eng is nc.tensor else "pool")], 1)

        class Counted:
            def __init__(self, eng, s, first=0):
                self.eng, self.s, self.n = eng, s, 0
                self.first = first

            def mark(self, ins):
                ins.then_inc(self.s, 1)
                self.n += 1

            def link(self, ins):
                self.mark(ins)
                self.eng.wait_ge(self.s, self.first + self.n)

        block = ctx.enter_context(nc.Block())

        IN_ROW = LOG_W - 1
        IN_ROW_OPS = 4 * IN_ROW * (IN_ROW + 1) // 2

        def level_start(k):
            ops, cur = IN_ROW_OPS, (IN_ROW * (IN_ROW + 1) // 2) % 2
            for j in range(LOG_W, k):
                if j == LOG_W:
                    ops += 2 + 4 * (LOG_W - 1)
                    cur = (cur + 1 + LOG_W) % 2
                else:
                    ops += 4 * (j - LOG_W) + 2 + 12 + 28
                    cur = (cur + j - LOG_W - 1 + 4 + 7) % 2
            return ops, cur

        def level_down(k):
            ops, cur = level_start(k)
            return ops + 4 * (k - LOG_W) + 2 + 12, (cur + k - LOG_W - 1 + 4) % 2

        SORT_OPS, SORT_END = level_start(LOG_E + 1)

        def half(buf, i):
            return sort[buf][:, i * HALF:(i + 1) * HALF]

        def pairs(ap, s):
            return ap.rearrange("p (a t s) -> p a t s", t=2, s=s)

        NORM_LEVEL = LOG_W + 5
        none = range(0)
        ATTENTION = {12: (range(0, 2), range(2, 5)), 13: (range(5, 7), range(7, 10)),
                     14: (range(10, 13), range(13, 16)), 15: (range(16, NB + 3), none)}
        NODES = {16: (range(0, 5), range(5, NG + 1))}
        EXPERT = {17: (range(0, 3), range(3, 5)), 18: (range(5, 8), range(8, 10))}
        N_WEIGHTS = 19 + 3 * NE

        LAST_SLOTS = range(10, NE * NG + 1)

        GATHERS = HC2 * 16
        slots = [S[f"row_in{i}"] for i in range(RING)]

        @block.sync
        def _(sp):
            words = edges.rearrange("t (p w) -> p t w", p=P)
            sp.dma_start(sort[0][:].bitcast(I32), words[:, 1, :]).then_inc(S["edges_in"], 16)
            sp.dma_start(sort[1][:].bitcast(I32), words[:, 0, :]).then_inc(S["edges_in"], 16)
            n_w = 0
            for dst, src in (
                (tok_w2[0:F, 0:F], tok_w), (tok_w2[F:P, F:P], tok_w), (wa[:], w_alpha), (wb[:], w_beta),
                (wu[:, 0:F], w_unary), (wu[:, F:F + 1], b_unary.rearrange("(f a) -> f a", a=1)),
                (wr[:], w_r), (w_ext[:, 0:HC], w_gat),
                (att_col[:, 0:1], att_src.rearrange("h (c a) -> (h c) a", a=1)),
                (att_col[:, 1:2], att_dst.rearrange("h (c a) -> (h c) a", a=1)),
            ):
                if n_w == 0:
                    sp.wait_ge(S["zeros_ready"], 2)
                sp.dma_start(dst, src).then_inc(S["weights_in"], 16)
                n_w += 1
            assert n_w == 10
            sp.dma_start(b2_row[:, 0, :], b2.rearrange("(a e) f -> a (e f)", a=1)).then_inc(S["b2_in"], 16)
            fr = x.rearrange("b (s w) f -> (b s) (w f)", w=POOL).rearrange("(t p) c -> p t c", p=P)
            with sp.Fori(0, TILES // GA // 2) as k:
                for s in range(2):
                    sp.wait_ge(S["frames_free"], 2 * k + s + 1)
                    sp.dma_start(frames[s], fr[:, bass.ds((2 * k + s) * GA, GA), :])\
                      .then_inc(S[f"frames_in{s}"], 16)
            for dst, src in (
                (w1_s[:], w1.rearrange("e d f -> d e f")), (w2_s[:], w2.rearrange("e f d -> f e d")),
                *[(b1_s[:, e:e + 1], b1[e, :].rearrange("(f a) -> f a", a=1)) for e in range(NE)],
                (bg[:], b_gat.partition_broadcast(P)), (gamma[:], ln_gamma.partition_broadcast(P)),
                (beta[:], ln_beta.partition_broadcast(P)),
            ):
                sp.dma_start(dst, src).then_inc(S["weights_in"], 16)
            sp.wait_ge(S["b2_split"], 1)
            for i in range(3):
                for e in range(NE):
                    sp.dma_start(b2_rows[i:i + 1, e], b2_part[:, i, e].unsqueeze(1).broadcast_to([1, GE, F]))\
                      .then_inc(S["weights_in"], 16)
            flat = inject.rearrange("e h -> (e h)")
            part_n = P * 528
            for i in range((E + M) * HEADS // part_n):
                sp.dma_start(flat[i * part_n:(i + 1) * part_n].rearrange("(p c) -> p c", p=P), zeros[:])\
                  .then_inc(S["zero_out"], 16)
            for i in range(16):
                n = E // 16
                sp.dma_start(results[i * n:(i + 1) * n, :].rearrange("(p c) o -> p (c o)", p=P)
                             .rearrange("p (r z) -> p r z", z=512),
                             zeros[:, 0:512].unsqueeze(1).broadcast_to([P, n * OUTC // P // 512, 512]))\
                  .then_inc(S["results_zero"], 16)
            sp.dma_start(sorted_padded[0:PAD].rearrange("(p c) -> p c", p=PAD), zeros[0:PAD, 0:1])\
              .then_inc(S["pad_out"], 16)
            sp.dma_start(sorted_padded[PAD + E:].rearrange("(p c) -> p c", p=P), zeros[:, 0:C])\
              .then_inc(S["pad_out"], 16)
            sp.wait_ge(S["sorted_ops"], SORT_OPS)
            done = sort[SORT_END]
            sp.dma_start(sorted_rows.rearrange("(p c) s -> p (c s)", p=P), done[:]).then_inc(S["srt_out"], 16)
            sp.dma_start(sorted_padded[PAD:PAD + E].rearrange("(p c) -> p c", p=P), done[:])\
              .then_inc(S["srt_out"], 16)
            sp.wait_ge(S["ext_ready"], NG)
            sp.dma_start(table.rearrange("(t p) c -> p t c", p=P), ext[:, :, 0:ROW]).then_inc(S["table_out"], 16)
            sp.wait_ge(S["table_out"], 16)
            sp.dma_start(clamped[:], table[M - 1, :].partition_broadcast(P)).then_inc(S["clamped_in"], 16)

            def next_lane(cls):
                low, to = lower[:, cls, :], nxt[:, cls, :]
                sp.dma_start(to[0:112, :], low[1:113, 0:TILES]).then_inc(S["shift_in"], 16)
                sp.dma_start(to[112:P - 1, :], low[113:P, 0:TILES]).then_inc(S["shift_in"], 16)
                sp.dma_start(to[P - 1:P, :], low[0:1, 1:NS]).then_inc(S["shift_in"], 16)

            sp.wait_ge(S["bound_ready"], 1)
            next_lane(0)
            sp.wait_ge(S["pad_out"], 32)
            sp.wait_ge(S["srt_out"], 32)

            def load_keys(k):
                first = PAD - 1 + k * CHUNK
                sp.dma_start(keys[:].bitcast(F32), bass.AP(tensor=sorted_padded.tensor, offset=first,
                                                           ap=[[C, P], [1, C + 1]]))\
                  .then_inc(S["keys_in"], 16)

            load_keys(0)
            sp.wait_ge(S["scatter_ready"], 1)
            chunks = sp.value_load(chunks_i[0:1, 0:1], min_val=1, max_val=MAX_CHUNKS)
            sp.wait_ge(S["scattered"], 16 * TILES)
            res = results.rearrange("(k p c) o -> k p (c o)", p=P, c=C)
            injs = inject[0:E, :].rearrange("(k p c) h -> k p (c h)", p=P, c=C)
            sp.wait_ge(S["results_zero"], 16 * 16)
            with sp.Fori(0, chunks) as k:
                sp.wait_ge(S["inj_free"], k + 1)
                sp.dma_start(inj[:].rearrange("p c h -> p (c h)"), injs[bass.ds(k, 1), :, :].rearrange("a p c -> (a p) c"))\
                  .then_inc(S["inj_in"], 16)
                sp.wait_ge(S["keys_free"], k + 1)
                sp.dma_start(keys[:].bitcast(F32), bass.AP(tensor=sorted_padded.tensor,
                                                           offset=PAD - 1 + CHUNK + k * CHUNK,
                                                           ap=[[C, P], [1, C + 1]]))\
                  .then_inc(S["keys_in"], 16)
                sp.wait_ge(S["res_ready"], k + 1)
                sp.dma_start(res[bass.ds(k, 1), :, :].rearrange("a p c -> (a p) c"),
                             results_s[:].rearrange("p c o -> p (c o)")).then_inc(S["res_out"], 16)
            sp.wait_ge(S["bound_ready"], 2)
            next_lane(1)
            rows_out = out.rearrange("b s f -> (b s) f").rearrange("(t p) f -> p t f", p=P)
            for i in range(4):
                sp.wait_ge(S["y_done"], i + 1)
                q = TILES // 4
                sp.dma_start(rows_out[:, i * q:(i + 1) * q, :], h[:, i * q:(i + 1) * q, :])\
                  .then_inc(S["out_done"], 16)
            sp.wait_ge(S["out_done"], 64)

        @block.gpsimd
        def _(pool):
            g = nc.gpsimd
            g.memset(zeros[:], 0.0).then_inc(S["zeros_ready"], 1)
            g.memset(tok_w2[:], 0.0).then_inc(S["zeros_ready"], 1)
            g.iota(lane[:], pattern=[[0, 1]], base=0, channel_multiplier=1).then_inc(S["lane_ready"], 1)
            g.iota(node_i[:], pattern=[[P, NS]], base=0, channel_multiplier=1).then_inc(S["node_ready"], 1)
            g.iota(lane_row_i, pattern=[[1, P]], base=0, channel_multiplier=0).then_inc(S["node_ready"], 1)
            g.iota(tile_row_i, pattern=[[FAR >> TILE_BIT, 2], [1, NS]], base=NODE >> TILE_BIT, channel_multiplier=0)\
             .then_inc(S["node_ready"], 1)
            ch = Counted(pool, S["p_chain"])
            ch.link(g.memset(ident[:], 0.0))
            ch.link(g.memset(pair_mask[:], 0.0))
            ch.link(g.memset(head_mask[:], 1.0))
            ch.link(g.memset(ones_row[:], 1.0))
            for ones in x_t:
                ch.link(g.memset(ones[F:F + 1, :], 1.0))
            ch.link(g.memset(ones_sq[:], 1.0))
            CHAIN = ch.n + 3
            g.affine_select(out=ident[:], in_=ident[:], compare_op=ALU.not_equal, fill=1.0, base=0,
                            pattern=[[-1, P]], channel_multiplier=1).then_inc(S["ident_ready"], 1)
            ch.link(g.memset(pair_mask[0:SEQ, 0:SEQ], 1.0))
            ch.link(g.memset(pair_mask[SEQ:P, SEQ:P], 1.0))
            ch.link(g.affine_select(out=head_mask[:], in_=head_mask[:], compare_op=ALU.is_ge, fill=0.0, base=0,
                                    pattern=[[-NE, HEADS]], channel_multiplier=1))
            g.affine_select(out=pair_mask[:], in_=pair_mask[:], compare_op=ALU.not_equal, fill=0.0, base=0,
                            pattern=[[-1, P]], channel_multiplier=1).then_inc(S["mask_ready"], 1)
            g.affine_select(out=head_mask[:], in_=head_mask[:], compare_op=ALU.is_ge, fill=0.0, base=NE - 1,
                            pattern=[[NE, HEADS]], channel_multiplier=-1).then_inc(S["mask_ready"], 1)
            pool.wait_ge(S["mask_ready"], 2)

            A_OPS = 3
            with pool.Fori(0, TILES // GA // 2) as k:
                for s in range(2):
                    i = 2 * k + s
                    ch = Counted(pool, S["pool_steps"], i * A_OPS)
                    lg, tr = logits[s], tree[s]
                    fr = frames[s].rearrange("p t (w f) -> p t w f", w=POOL)
                    mine = bass.ds(i * GA, GA)
                    pool.wait_ge(S["pool_exp"], i + 1)
                    ch.mark(g.tensor_tensor(tr[:, :, 0:2], lg[:, :, 0:2], lg[:, :, 2:4], ALU.add))
                    ch.link(g.tensor_tensor(fr, fr, lg, ALU.mult))
                    g.tensor_tensor(xn[:, mine, :], tr[:, :, 0], tr[:, :, 1], ALU.add).then_inc(S["pooled"], 1)
                    ch.link(g.tensor_tensor(lg[:, :, 0:2], fr[:, :, 0:2], fr[:, :, 2:4], ALU.add))
                    assert ch.n == A_OPS
                    g.tensor_tensor(h[:, mine, :], lg[:, :, 0], lg[:, :, 1], ALU.add).then_inc(S["pooled"], 1)
                    pool.wait_ge(S["pooled"], 2 * i + 2)
                    pool.sem_inc(S["frames_free"], 1)

            pool.wait_ge(S["norm_done"], 1)
            with pool.Fori(0, NB // 2) as k:
                for r in range(2):
                    n = 2 * k + r
                    hold(pool, "score_ready", n + 1)
                    g.tensor_tensor(score[r], score[r], pair_mask[:].unsqueeze(1).broadcast_to([P, GB, P]),
                                    ALU.mult).then_inc(S["score_masked"], 1)
                    mine = bass.ds(n * GB, GB)
                    g.tensor_tensor(h[:, mine, :], h[:, mine, :], xn[:, mine, :], ALU.add)\
                     .then_inc(S["p_chain"], 1)
                    pool.wait_ge(S["p_chain"], CHAIN + 1 + n)
                    hold(pool, "att_ready", n + 1)
                    g.tensor_tensor(h[:, mine, :], h[:, mine, :], attended[r], ALU.add)\
                     .then_inc(S["attn_added"], 1)

            def fetch(cls):
                for t in range(NS):
                    n = cls * NS + t
                    if n >= RING:
                        pool.wait_ge(S["row_used"], n - RING + 1)
                    g.indirect_dma_start(ring[n % RING], None, sorted_rows,
                                         bass.IndirectOffsetOnAxis(ap=row_i[:, cls, t:t + 1], axis=0))\
                     .then_inc(slots[n % RING], 16)

            pool.wait_ge(S["srt_out"], 32)
            pool.wait_ge(S["row_idx"], 1)
            fetch(0)
            pool.wait_ge(S["zero_out"], 16 * 16)
            pool.wait_ge(S["ext_ready"], NG)
            pool.wait_ge(S["scatter_ready"], 1)
            for t in range(TILES):
                g.indirect_dma_start(inject, bass.IndirectOffsetOnAxis(ap=start_i[:, t:t + 1], axis=0),
                                     ext[:, t, ROW:EXT], None).then_inc(S["scattered"], 16)
            pool.wait_ge(S["table_out"], 16)
            chunks = pool.value_load(chunks_i[0:1, 0:1], min_val=1, max_val=MAX_CHUNKS)
            with pool.Fori(0, chunks) as k:
                for idx, ready, rows, landed, free in (
                    (src_a, "idx_a", rows_a, "rows_a_in", "rows_a_free"),
                    (src_b, "idx_b", rows_b, "rows_b_in", "rows_b_free"),
                ):
                    hold(pool, ready, k + 1)
                    hold(pool, free, 2 * k + 2)
                    for c in range(HC2):
                        g.indirect_dma_start(rows[:, c, :], None, table,
                                             bass.IndirectOffsetOnAxis(ap=idx[:, c:c + 1], axis=0))\
                         .then_inc(S[landed], 16)
            fetch(1)
            hold(pool, "res_out", 16 * chunks + 16)
            for t in range(TILES):
                g.indirect_dma_start(ends[:, t, :], None, results,
                                     bass.IndirectOffsetOnAxis(ap=end_i[:, t:t + 1], axis=0))\
                 .then_inc(S["ends_in"], 16)

        @block.scalar
        def _(act):
            a = nc.scalar

            def copy(dst, src, **kw):
                return a.activation(dst, src, ACT.Copy, **kw)

            act.wait_ge(S["prep_pe"], 1)
            copy(w_score[:], pt[0][0:F, 0:F]).then_inc(S["prep_act"], 1)
            copy(wr_t[:], pt[0][0:F, 128:128 + F]).then_inc(S["prep_act"], 1)
            copy(wg_t[:], pt[0][0:HC, 256:256 + F]).then_inc(S["prep_act"], 1)
            act.wait_ge(S["prep_pe"], 2)
            copy(w_value[:], pt[1][0:F + 1, 0:F], scale=1.0 / SEQ).then_inc(S["prep_act"], 1)
            copy(w_ext[:, HC:EXT], pt[1][0:F, 128:128 + 2 * HEADS]).then_inc(S["prep_act"], 1)

            with act.Fori(0, TILES // GA // 2) as k:
                for s in range(2):
                    i = 2 * k + s
                    act.wait_ge(S["frames_t_done"], i + 1)
                    copy(frames_t[s].rearrange("p a b -> p (a b)"), pt[2 * s][:]).then_inc(S["frames_t_ready"], 1)
                    lg = logits[s].rearrange("p a b c -> p (a b c)")
                    act.wait_ge(S["shifted"], i + 1)
                    a.activation(lg, lg, ACT.Exp).then_inc(S["pool_exp"], 1)

            def root(n):
                act.wait_ge(S["norm_var"], n)
                a.activation(stat[:, 1], stat[:, 1], ACT.Sqrt).then_inc(S["norm_sd"], 1)

            root(1)

            def turned(k):
                ops, cur = level_start(k)
                for i in range(2):
                    act.wait_ge(S["sorted_ops"], ops - 2 * (1 - i))
                    copy(half(1 - cur, i), half(cur, i), scale=turn[:, k - LOG_W:k - LOG_W + 1])\
                        .then_inc(S["turned"], 1)

            turned(LOG_W)

            def attention_slot(j):
                if j < NB:
                    act.wait_ge(S["x_t_done"], j + 1)
                    copy(x_t[j % 3][0:F, :], pt[2][0:F, 0:GB * P]).then_inc(S["x_t_ready"], 1)
                if 0 <= j - 1 < NB:
                    n = j - 1
                    act.wait_ge(S["t_done"], n + 1)
                    copy(t_t[n % 2], pt[2][0:F, 512:512 + GB * P]).then_inc(S["t_ready"], 1)
                    copy(value[n % 3].rearrange("p a b -> p (a b)"), pt[3][:, 512:512 + GB * F])\
                        .then_inc(S["t_ready"], 1)
                if 0 <= j - 2 < NB:
                    n = j - 2
                    act.wait_ge(S["score_done"], n + 1)
                    copy(score[n % 2].rearrange("p a b -> p (a b)"), pt[3][:, 0:GB * P])\
                        .then_inc(S["score_ready"], 1)
                if 0 <= j - 3 < NB:
                    n = j - 3
                    act.wait_ge(S["att_done"], n + 1)
                    if n >= 2:
                        act.wait_ge(S["attn_added"], n - 1)
                    copy(attended[n % 2].rearrange("p a b -> p (a b)"), pt[3][:, 768:768 + GB * F])\
                        .then_inc(S["att_ready"], 1)

            def nodes_slot(j):
                if j < NG:
                    act.wait_ge(S["ext_x_done"], j + 1)
                    copy(xn2_t[:, j * GE * P:(j + 1) * GE * P], pt[2][0:F, :]).then_inc(S["ext_x_ready"], 1)
                if j >= 1:
                    act.wait_ge(S["ext_done"], j)
                    copy(ext[:, (j - 1) * GE:j * GE, :],
                         pt[3][:, 512:512 + GE * EXT].rearrange("p (t c) -> p t c", c=EXT))\
                        .then_inc(S["ext_ready"], 1)

            def expert_slot(j):
                if j < NE * NG:
                    e = j % NE
                    act.wait_ge(S["hidden_done"], j + 1)
                    a.activation(hidden[j % 2], pt[2][:], ACT.Gelu, bias=b1_s[:, e:e + 1])\
                     .then_inc(S["hidden_ready"], 1)
                if j >= 1:
                    g, e = divmod(j - 1, NE)
                    act.wait_ge(S["expert_done"], j)
                    copy(experts[:, g * GE:(g + 1) * GE, e, :],
                         pt[3][:, 0:GE * F].rearrange("p (t f) -> p t f", f=F)).then_inc(S["expert_ready"], 1)

            def beside(k, part):
                for j in ATTENTION.get(k, (none, none))[part]:
                    attention_slot(j)
                for j in NODES.get(k, (none, none))[part]:
                    nodes_slot(j)
                for j in EXPERT.get(k, (none, none))[part]:
                    expert_slot(j)

            for k in range(LOG_W + 1, LOG_E + 1):
                if k == NORM_LEVEL:
                    root(2)
                    act.wait_ge(S["norm_done"], 2)
                    act.wait_ge(S["weights_in"], 16 * N_WEIGHTS)
                turned(k)
                cur = level_start(k)[1]
                d = 2 ** (k - LOG_W - 1)
                n = k - LOG_W - 1
                for i in range(2):
                    act.wait_ge(S["up_done"], 2 * n + i + 1)
                    copy(pairs(half(1 - cur, i), d)[:, :, 1], pairs(pt[i][:], d)[:, :, 1])\
                        .then_inc(S["hi_ready"], 1)
                beside(k, 0)
                cur = level_down(k)[1]
                for i in range(2):
                    act.wait_ge(S["down_done"], 2 * n + i + 1)
                    copy(pairs(half(cur, i), P // 2)[:, :, 1], pairs(pt[i][:], P // 2)[:, :, 1])\
                        .then_inc(S["hi_ready"], 1)
                beside(k, 1)
            for j in LAST_SLOTS:
                expert_slot(j)

            act.wait_ge(S["scatter_ready"], 1)
            chunks = act.value_load(chunks_i[0:1, 0:1], min_val=1, max_val=MAX_CHUNKS)
            act.sem_inc(S["rows_a_free"], 1)
            act.sem_inc(S["rows_b_free"], 1)
            with act.Fori(0, chunks) as k:
                for i, (rows, landed, free) in enumerate(((rows_a, "rows_a_in", "rows_a_free"),
                                                          (rows_b, "rows_b_in", "rows_b_free"))):
                    act.wait_ge(S[landed], GATHERS * (k + 1))
                    copy(h_s[:, :, i * HC2:(i + 1) * HC2], rows[:, :, 0:HC].rearrange("p c o -> p o c"))\
                        .then_inc(S["h_copied"], 1)
                    act.wait_ge(S["h_copied"], 2 * k + i + 1)
                    act.sem_inc(S[free], 1)
                act.wait_ge(S["exp_go"], 3 * k + 1)
                a.activation(keep, keep, ACT.Exp).then_inc(S["exp_done"], 1)
                act.wait_ge(S["exp_go"], 3 * k + 2)
                a.activation(wgt[:, 0:HEADS, :], wgt[:, 0:HEADS, :], ACT.Exp).then_inc(S["exp_done"], 1)
                act.wait_ge(S["exp_go"], 3 * k + 3)
                a.activation(passing[:], passing[:], ACT.Exp).then_inc(S["exp_done"], 1)
                act.wait_ge(S["res_ready"], k + 1)

            act.wait_ge(S["mg_go"], 1)
            a.activation(mg, mg, ACT.Exp).then_inc(S["mg_exp"], 1)
            act.wait_ge(S["var_go"], 1)
            a.activation(st2[:, 1], st2[:, 1], ACT.Sqrt).then_inc(S["sd_ready"], 1)
            act.wait_ge(S["gate_go"], 1)
            a.activation(sc, sc, ACT.Exp).then_inc(S["gate_exp"], 1)

        @block.tensor
        def _(pe):
            t = nc.tensor
            pe.wait_ge(S["weights_in"], 160)
            pe.wait_ge(S["ident_ready"], 1)
            t.matmul(pt[0][0:F, 0:F], wa[:], wb[:], start=True, stop=True)
            t.transpose(pt[0][0:F, 128:128 + F], wr[:], ident[0:F, 0:F])
            t.transpose(pt[0][0:HC, 256:256 + F], w_ext[:, 0:HC], ident[0:F, 0:F]).then_inc(S["prep_pe"], 1)
            pe.wait_ge(S["prep_act"], 3)
            pe.wait_ge(S["prep_dve"], 1)
            t.matmul(pt[1][0:F + 1, 0:F], wu[:], wr_t[:], start=True, stop=True)
            t.matmul(pt[1][0:F, 128:128 + 2 * HEADS], wg_t[:], att_sel[:].rearrange("p a b -> p (a b)"),
                     start=True, stop=True).then_inc(S["prep_pe"], 1)
            pe.wait_ge(S["prep_act"], 5)

            with pe.Fori(0, TILES // GA // 2) as k:
                for s in range(2):
                    i = 2 * k + s
                    hold(pe, f"frames_in{s}", 16 * (k + 1))
                    hold(pe, "logits_free", i + 1)
                    for j in range(GA * POOL // 2):
                        ins = t.transpose(pt[2 * s][:, j * P:(j + 1) * P],
                                          frames[s][:, j // 2, (j % 2) * P:(j % 2 + 1) * P], ident[:])
                    ins.then_inc(S["frames_t_done"], 1)
                    hold(pe, "frames_t_ready", i + 1)
                    for j in range(GA * POOL // 2):
                        ins = t.matmul(pt[2 * s + 1][:, j * P:(j + 1) * P], frames_t[s][:, j, :], tok_w2[:],
                                       start=True, stop=True)
                    ins.then_inc(S["logits_done"], 1)

            def attention_slot(j):
                if j < NB:
                    if j >= 1:
                        pe.wait_ge(S["x_t_ready"], j)
                    for i in range(GB):
                        ins = t.transpose(pt[2][0:F, i * P:(i + 1) * P], xn[:, j * GB + i, :], ident[:])
                    ins.then_inc(S["x_t_done"], 1)
                if 0 <= j - 1 < NB:
                    n = j - 1
                    x_n = x_t[n % 3]
                    pe.wait_ge(S["x_t_ready"], n + 1)
                    if n >= 1:
                        pe.wait_ge(S["t_ready"], 2 * n)
                    if n >= 3:
                        pe.wait_ge(S["att_ready"], n - 2)
                    t.matmul(pt[2][0:F, 512:512 + GB * P], w_score[:], x_n[0:F, :], start=True, stop=True)
                    for i in range(GB):
                        ins = t.matmul(pt[3][:, 512 + i * F:512 + (i + 1) * F], x_n[:, i * P:(i + 1) * P], w_value[:],
                                       start=True, stop=True)
                    ins.then_inc(S["t_done"], 1)
                if 0 <= j - 2 < NB:
                    n = j - 2
                    pe.wait_ge(S["t_ready"], 2 * n + 2)
                    if n >= 1:
                        pe.wait_ge(S["score_ready"], n)
                    for i in range(GB):
                        cols = slice(i * P, (i + 1) * P)
                        ins = t.matmul(pt[3][:, cols], x_t[n % 3][0:F, cols], t_t[n % 2][:, cols],
                                       start=True, stop=True)
                    ins.then_inc(S["score_done"], 1)
                if 0 <= j - 3 < NB:
                    n = j - 3
                    pe.wait_ge(S["score_masked"], n + 1)
                    pe.wait_ge(S["t_ready"], 2 * min(j, NB))
                    for i in range(GB):
                        ins = t.matmul(pt[3][:, 768 + i * F:768 + (i + 1) * F], score[n % 2][:, i, :],
                                       value[n % 3][:, i, :], start=True, stop=True)
                    ins.then_inc(S["att_done"], 1)

            def nodes_slot(j):
                if j < NG:
                    if j >= 1:
                        pe.wait_ge(S["ext_x_ready"], j)
                    for i in range(GE):
                        ins = t.transpose(pt[2][0:F, i * P:(i + 1) * P], xn[:, j * GE + i, :], ident[:])
                    ins.then_inc(S["ext_x_done"], 1)
                if j >= 1:
                    pe.wait_ge(S["ext_x_ready"], j)
                    if j >= 2:
                        pe.wait_ge(S["ext_ready"], j - 1)
                    for i in range(GE):
                        tile = (j - 1) * GE + i
                        ins = t.matmul(pt[3][:, 512 + i * EXT:512 + (i + 1) * EXT], xn2_t[:, tile * P:(tile + 1) * P],
                                       w_ext[:], start=True, stop=True)
                    ins.then_inc(S["ext_done"], 1)

            def expert_slot(j):
                if j == 0:
                    pe.wait_ge(S["ext_x_ready"], NG)
                else:
                    pe.wait_ge(S["hidden_ready"], j)
                if j < NE * NG:
                    g, e = divmod(j, NE)
                    for i in range(2):
                        first = g * GE * P + i * 512
                        ins = t.matmul(pt[2][:, i * 512:(i + 1) * 512], w1_s[:, e, :], xn2_t[:, first:first + 512],
                                       start=True, stop=True)
                    ins.then_inc(S["hidden_done"], 1)
                if j >= 1:
                    e = (j - 1) % NE
                    if j >= 2:
                        pe.wait_ge(S["expert_ready"], j - 1)
                    t.matmul(pt[3][:, 0:GE * F], ones_row[:], b2_rows[:, e].rearrange("p a b -> p (a b)"),
                             start=True, stop=False)
                    for i in range(GE):
                        ins = t.matmul(pt[3][:, i * F:(i + 1) * F], hidden[(j - 1) % 2][:, i * P:(i + 1) * P],
                                       w2_s[:, e, :], start=False, stop=(i == GE - 1))
                    ins.then_inc(S["expert_done"], 1)

            def beside(k, part):
                for j in ATTENTION.get(k, (none, none))[part]:
                    attention_slot(j)
                for j in NODES.get(k, (none, none))[part]:
                    nodes_slot(j)
                for j in EXPERT.get(k, (none, none))[part]:
                    expert_slot(j)

            for k in range(LOG_W + 1, LOG_E + 1):
                if k == NORM_LEVEL:
                    pe.wait_ge(S["norm_done"], 2)
                    pe.wait_ge(S["weights_in"], 16 * N_WEIGHTS)
                cur = level_start(k)[1]
                for i in range(2):
                    pe.wait_ge(S["turned"], 2 * (k - LOG_W) + i + 1)
                    for b in range(HALF // P):
                        ins = t.transpose(pt[i][:, b * P:(b + 1) * P], half(1 - cur, i)[:, b * P:(b + 1) * P],
                                          ident[:])
                    ins.then_inc(S["up_done"], 1)
                beside(k, 0)
                ops, cur = level_down(k)
                for i in range(2):
                    pe.wait_ge(S["sorted_ops"], ops - 2 * (1 - i))
                    for b in range(HALF // P):
                        ins = t.transpose(pt[i][:, b * P:(b + 1) * P], half(cur, i)[:, b * P:(b + 1) * P],
                                          ident[:])
                    ins.then_inc(S["down_done"], 1)
                beside(k, 1)

            pe.wait_ge(S["heads_split"], 1)
            under = pt[0][:, 0:2 * NS]
            for c in range(HPP):
                t.matmul(under, lane_over[:, c, :], tile_same[:, c, :], start=(c == 0), stop=False)
                ins = t.matmul(under, ones_sq[:], tile_over[:, c, :], start=False, stop=(c == HPP - 1))
            ins.then_inc(S["heads_counted"], 1)
            for j in LAST_SLOTS:
                expert_slot(j)

            pe.wait_ge(S["expert_ready"], NE * NG)
            pe.wait_ge(S["scatter_ready"], 1)
            chunks = pe.value_load(chunks_i[0:1, 0:1], min_val=1, max_val=MAX_CHUNKS)
            with pe.Fori(0, chunks) as k:
                for r, (n, state) in enumerate(((HEADS, state_d), (HEADS, state_m), (SUMS, state_s))):
                    hold(pe, "tail_ready", 3 * k + r + 1)
                    for j in range(2):
                        ins = t.transpose(pt[3][0:n, j * P:(j + 1) * P], tails[:, j, 0:n], ident[:])
                    ins.then_inc(S["tail_t"], 1)
                    hold(pe, "state_ready", 3 * k + r + 1)
                    t.transpose(pt[3][:, 512:512 + n], state[:, 0:P], ident[0:n, 0:n]).then_inc(S["carry_t"], 1)

        @block.vector
        def _(dve):
            v = nc.vector
            c1 = Counted(dve, S["v_chain"])
            link, mark = c1.link, c1.mark
            dve.wait_ge(S["lane_ready"], 1)
            for m in range(LOG_E - LOG_W + 1):
                last = v.tensor_scalar(lane_bit[:, m:m + 1], lane[:], m, 1, ALU.logical_shift_right,
                                       ALU.bitwise_and)
            link(last)
            link(v.tensor_scalar(sign[:], lane_bit[:], -2.0, 1.0, ALU.mult, ALU.add))
            v.tensor_copy(turn[:, 0:1], sign[:, 0:1])
            link(v.tensor_tensor(turn[:, 1:], sign[:, 0:-1], sign[:, 1:], ALU.mult))
            mark(v.memset(state_d[:], 0.0))
            mark(v.memset(state_m[:], -BIG))
            link(v.memset(state_s[:], 0.0))

            dve.wait_ge(S["edges_in"], 32)
            dst_w, src_w = sort[0][:].bitcast(I32), sort[1][:].bitcast(I32)
            far_w = xn[:].rearrange("p t f -> p (t f)").bitcast(I32)[:, 0:W]
            link(v.tensor_scalar(far_w, src_w, float(M - 1), float(FAR), ALU.is_ge, ALU.mult))
            mark(v.tensor_scalar(dst_w, dst_w, SRC_BITS, NODE, ALU.logical_shift_left, ALU.bitwise_or))
            link(v.tensor_scalar(src_w, src_w, float(M - 1), 0.0, ALU.min, ALU.max))
            link(v.tensor_tensor(dst_w, dst_w, far_w, ALU.bitwise_or))
            link(v.tensor_tensor(dst_w, dst_w, src_w, ALU.bitwise_or))
            dve.wait_ge(S["weights_in"], 160)
            dve.wait_ge(S["mask_ready"], 2)
            v.tensor_scalar(att_sel[:, 0], head_mask[:], att_col[:, 0:1], None, ALU.mult)
            v.tensor_scalar(att_sel[:, 1], head_mask[:], att_col[:, 1:2], None, ALU.mult).then_inc(S["prep_dve"], 1)

            dve.wait_ge(S["b2_in"], 16)
            b2_of = [b2_part[:, i].rearrange("a e f -> a (e f)") for i in range(3)]
            for i in range(2):
                link(v.tensor_copy(b2_of[i], b2_row[:, i]))
                link(v.tensor_tensor(b2_row[:, i + 1], b2_row[:, i], b2_of[i], ALU.subtract))
            v.tensor_copy(b2_of[2], b2_row[:, 2]).then_inc(S["b2_split"], 1)
            dve.wait_ge(S["node_ready"], 3)
            mark(v.tensor_copy(node_f[:], node_i[:]))
            mark(v.tensor_copy(lane_row[:], lane_row_i))
            link(v.tensor_copy(tile_row[:], tile_row_i))

            ended = [0, 0]
            ops = 0

            def compare(halves, lo, hi, lesser, greater):
                nonlocal ops
                v.tensor_tensor(lesser, lo, hi, ALU.min).then_inc(S["sorted_ops"], 1)
                v.tensor_tensor(greater, lo, hi, ALU.max).then_inc(S["sorted_ops"], 1)
                ops += 2
                for i in halves:
                    ended[i] = ops

            def one_half(i, src, dst, d, hi=None):
                if ended[i]:
                    dve.wait_ge(S["sorted_ops"], ended[i])
                a, b = pairs(src, d), pairs(dst, d)
                compare((i,), a[:, :, 0], a[:, :, 1] if hi is None else pairs(hi, d)[:, :, 1],
                        b[:, :, 0], b[:, :, 1])

            def both_halves(cur, d):
                for i in range(2):
                    one_half(i, half(cur, i), half(1 - cur, i), d)
                return 1 - cur

            def across_halves(cur):
                dve.wait_ge(S["sorted_ops"], max(ended))
                compare((0, 1), half(cur, 0), half(cur, 1), half(1 - cur, 0), half(1 - cur, 1))
                return 1 - cur

            def shift_logits(i):
                s = i % 2
                lg = pt[2 * s + 1][:].rearrange("p (t w f) -> p t w f", w=POOL, f=F)
                most = tree[s][:, :, 2]
                dve.wait_ge(S["logits_done"], i + 1)
                if i >= 2:
                    dve.wait_ge(S["pooled"], 2 * (i - 1))
                v.tensor_reduce(most, lg.rearrange("p t w f -> p t f w"), AX.X, ALU.max).then_inc(S["pool_max"], 1)
                dve.wait_ge(S["pool_max"], i + 1)
                v.tensor_tensor(logits[s], lg, most.unsqueeze(2).broadcast_to([P, GA, POOL, F]), ALU.subtract)\
                 .then_inc(S["shifted"], 1)
                dve.wait_ge(S["shifted"], i + 1)
                dve.sem_inc(S["logits_free"], 1)

            dve.sem_inc(S["frames_free"], 2)
            dve.sem_inc(S["logits_free"], 2)
            cur, stages = 0, 0
            for k in range(1, LOG_W):
                for j in range(k - 1, -1, -1):
                    if ops:
                        dve.wait_ge(S["sorted_ops"], ops)
                    a, b = (sort[s][:].rearrange("p (u r a t s) -> p u r a t s", r=2, a=2 ** (k - j - 1), t=2,
                                                 s=2 ** j) for s in (cur, 1 - cur))
                    for r in range(2):
                        compare((0, 1), a[:, :, r, :, 0], a[:, :, r, :, 1], b[:, :, r, :, r], b[:, :, r, :, 1 - r])
                    cur = 1 - cur
                    stages += 1
                    if stages % 3 == 0 and stages // 3 <= TILES // GA:
                        shift_logits(stages // 3 - 1)

            def normalise(n):
                mean, sd = stat[:, 0], stat[:, 1]

                def over(ap):
                    return ap.unsqueeze(2).broadcast_to([P, TILES, F])
                link(v.tensor_reduce(mean, h[:], AX.X, ALU.add))
                link(v.tensor_scalar(mean, mean, 1.0 / F, None, ALU.mult))
                link(v.tensor_tensor(xn[:], h[:], over(mean), ALU.subtract))
                link(v.tensor_tensor(square, xn[:], xn[:], ALU.mult))
                link(v.tensor_reduce(sd, square, AX.X, ALU.add))
                v.tensor_scalar(sd, sd, 1.0 / F, EPS, ALU.mult, ALU.add).then_inc(S["norm_var"], 1)
                dve.wait_ge(S["norm_sd"], n)
                link(v.reciprocal(sd, sd))
                v.tensor_tensor(xn[:], xn[:], over(sd), ALU.mult).then_inc(S["norm_done"], 1)

            dve.wait_ge(S["pooled"], 2 * (TILES // GA))
            link(v.reciprocal(xn[:], xn[:]))
            link(v.tensor_tensor(h[:], h[:], xn[:], ALU.mult))
            normalise(1)

            cur = 1 - cur
            dve.wait_ge(S["turned"], 2)
            cur = across_halves(cur)
            for j in range(LOG_W - 2, -1, -1):
                cur = both_halves(cur, 2 ** j)
            assert (ops, cur) == level_start(LOG_W + 1)

            for k in range(LOG_W + 1, LOG_E + 1):
                if k == NORM_LEVEL:
                    dve.wait_ge(S["attn_added"], NB)
                    normalise(2)
                n = k - LOG_W - 1
                for i in range(2):
                    dve.wait_ge(S["hi_ready"], 4 * n + i + 1)
                    one_half(i, pt[i][:], half(cur, i), 2 ** n, hi=half(1 - cur, i))
                for m in range(n - 1, -1, -1):
                    cur = both_halves(cur, 2 ** m)
                cur = across_halves(cur)
                for d in (4 * P, 2 * P, P):
                    cur = both_halves(cur, d)
                assert (ops, cur) == level_down(k)
                for i in range(2):
                    dve.wait_ge(S["hi_ready"], 4 * n + i + 3)
                    one_half(i, pt[i][:], half(1 - cur, i), P // 2, hi=half(cur, i))
                cur = 1 - cur
                for m in range(5, -1, -1):
                    cur = both_halves(cur, 2 ** m)
            assert (ops, cur) == (SORT_OPS, SORT_END)

            heads = sort[SORT_END][:].rearrange("p (c s) -> p c s", s=STEP)[:, :, 0].bitcast(I32)
            dve.wait_ge(S["sorted_ops"], SORT_OPS)
            mark(v.tensor_scalar(head_tile_i[:], heads, TILE_BIT, None, ALU.logical_shift_right))
            link(v.tensor_scalar(head_lane_i[:], heads, SRC_BITS, P - 1, ALU.logical_shift_right, ALU.bitwise_and))
            mark(v.tensor_copy(head_tile[:], head_tile_i[:]))
            link(v.tensor_copy(head_lane[:], head_lane_i[:]))
            tiles_flat = tile_row[:].rearrange("p a b -> p (a b)")
            for c in range(HPP):
                mark(v.tensor_scalar(lane_over[:, c, :], lane_row[:], head_lane[:, c:c + 1], None, ALU.is_gt))
                mark(v.tensor_scalar(tile_same[:, c, :], tiles_flat, head_tile[:, c:c + 1], None, ALU.is_equal))
                mark(v.tensor_scalar(tile_over[:, c, :], tiles_flat, head_tile[:, c:c + 1], None, ALU.is_gt))
            dve.wait_ge(S["v_chain"], c1.n)
            dve.sem_inc(S["heads_split"], 1)
            link(v.tensor_scalar(goal[:, 0], node_i[:], SRC_BITS, NODE, ALU.logical_shift_left, ALU.bitwise_or))
            link(v.tensor_scalar(goal[:, 1], goal[:, 0], FAR, None, ALU.bitwise_or))
            goal_f = goal[:].bitcast(F32)

            dve.wait_ge(S["heads_counted"], 1)
            under = pt[0][:, 0:2 * NS].rearrange("p (a b) -> p a b", a=2)
            link(v.tensor_scalar(row_f[:], under, 1.0, 0.0, ALU.subtract, ALU.max))
            v.tensor_copy(row_i[:], row_f[:]).then_inc(S["row_idx"], 1)

            def words_under(cls):
                for t in range(NS):
                    n = cls * NS + t
                    dve.wait_ge(slots[n % RING], 16 * (n // RING + 1))
                    v.tensor_scalar(less[:], ring[n % RING], goal_f[:, cls, t:t + 1], 0.0, ALU.is_lt, ALU.add,
                                    accum_out=lower[:, cls, t:t + 1]).then_inc(S["row_used"], 1)
                    dve.wait_ge(S["row_used"], n + 1)
                v.scalar_tensor_tensor(lower[:, cls], row_f[:, cls], float(STEP), lower[:, cls], ALU.mult,
                                       ALU.add).then_inc(S["bound_ready"], 1)
                dve.wait_ge(S["bound_ready"], cls + 1)

            def counts(cls):
                dve.wait_ge(S["shift_in"], 48 * (cls + 1))
                link(v.tensor_tensor(count[:, cls], nxt[:, cls], lower[:, cls, 0:TILES], ALU.subtract))
                link(v.tensor_scalar(has[:, cls], count[:, cls], 0.0, None, ALU.is_gt))

            words_under(0)
            link(v.tensor_scalar(chunks_f[:], lower[0:1, 0, TILES:NS], float(CHUNK - 1), float(CHUNK), ALU.add,
                                 ALU.max))
            link(v.tensor_copy(chunks_i[:], chunks_f[:]))
            link(v.tensor_scalar(chunks_i[:], chunks_i[:], CHUNK.bit_length() - 1, None, ALU.logical_shift_right))
            counts(0)
            link(v.tensor_scalar(start_f[:], node_f[:, 0:TILES], float(E), None, ALU.add))
            link(v.tensor_tensor(stat[:, 0], lower[:, 0, 0:TILES], start_f[:], ALU.subtract))
            link(v.tensor_tensor(stat[:, 0], stat[:, 0], has[:, 0], ALU.mult))
            link(v.tensor_tensor(start_f[:], start_f[:], stat[:, 0], ALU.add))
            link(v.tensor_scalar(stat[:, 1], nxt[:, 0], 1.0, 0.0, ALU.subtract, ALU.max))
            link(v.tensor_copy(end_i[:], stat[:, 1]))
            v.tensor_copy(start_i[:], start_f[:]).then_inc(S["scatter_ready"], 1)

            dve.wait_ge(S["scatter_ready"], 1)
            dve.wait_ge(S["keys_in"], 16)

            def segments(ch):
                ch.link(v.tensor_scalar(segs[:], keys[:], SRC_BITS, None, ALU.logical_shift_right))
                ch.link(v.tensor_tensor(same_next[:], segs[:, 1:], segs[:, 0:C], ALU.is_equal))

            def sources(ch, idx, first, ready):
                ch.mark(v.tensor_scalar(idx[:], keys[:, 1 + first:1 + first + HC2], M - 1, None, ALU.bitwise_and))
                dve.wait_ge(ch.s, ch.first + ch.n)
                dve.sem_inc(S[ready], 1)

            segments(c1)
            sources(c1, src_a, 0, "idx_a")
            sources(c1, src_b, HC2, "idx_b")
            dve.sem_inc(S["keys_free"], 1)
            dve.sem_inc(S["inj_free"], 1)
            dve.sem_inc(S["res_out"], 16)
            dve.sem_inc(S["rows_a_free"], 1)
            dve.sem_inc(S["rows_b_free"], 1)
            chunks = dve.value_load(chunks_i[0:1, 0:1], min_val=1, max_val=MAX_CHUNKS)
            EDGE_OPS = 89
            with dve.Fori(0, chunks) as k:
                ch = Counted(dve, S["e_chain"], k * EDGE_OPS)

                def carried(r, n, state, op, to):
                    dve.wait_ge(S["tail_t"], 3 * k + r + 1)
                    ch.mark(v.tensor_copy(state[:, 0:1], state[:, P:P + 1]))
                    ch.link(v.tensor_copy(across[0:n], pt[3][0:n, 0:2 * P].rearrange("p (a b) -> p a b", a=2)))
                    v.tensor_tensor_scan(state[:, 1:P + 1], across[0:n, 1, :], across[0:n, 0, :], state[:, 0:1],
                                         op[0], op[1]).then_inc(S["state_ready"], 1)
                    dve.wait_ge(S["carry_t"], 3 * k + r + 1)
                    ch.link(v.tensor_copy(to, pt[3][:, 512:512 + n]))

                SUM, TOP = (ALU.mult, ALU.add), (ALU.add, ALU.max)
                ch.link(v.tensor_copy(same[:], same_next[:]))
                ch.mark(v.tensor_scalar(fence[:], same[:], 1.0, BIG, ALU.subtract, ALU.mult))
                ch.mark(v.tensor_reduce(lasts[:], same[:], AX.X, ALU.min))
                dve.wait_ge(S["keys_in"], 16 * (k + 2))
                segments(ch)
                dve.wait_ge(S["inj_in"], 16 * (k + 1))
                for i in range(HEADS):
                    ch.mark(v.tensor_tensor_scan(a_d[:, i], same[:], inj[:, :, i], 0.0, *SUM))
                dve.wait_ge(ch.s, ch.first + ch.n)
                ch.link(v.tensor_copy(tails[:, 0, 0:HEADS], a_d[:, :, C - 1]))
                v.tensor_copy(tails[:, 1, 0:HEADS], lasts[:].broadcast_to([P, HEADS])).then_inc(S["tail_ready"], 1)
                carried(0, HEADS, state_d, SUM, carry_d[:])
                for i in range(HEADS):
                    ch.mark(v.tensor_tensor_scan(a_d[:, i], same[:], inj[:, :, i], carry_d[:, i:i + 1], *SUM))
                dve.wait_ge(ch.s, ch.first + ch.n)
                dve.sem_inc(S["inj_free"], 1)
                for i, (rows, landed, free, idx, ready) in enumerate((
                    (rows_a, "rows_a_in", "rows_a_free", src_a, "idx_a"),
                    (rows_b, "rows_b_in", "rows_b_free", src_b, "idx_b"),
                )):
                    dve.wait_ge(S[landed], GATHERS * (k + 1))
                    sources(ch, idx, i * HC2, ready)
                    ch.link(v.tensor_copy(a_s[:, :, i * HC2:(i + 1) * HC2],
                                          rows[:, :, HC:ROW].rearrange("p c o -> p o c")))
                    dve.sem_inc(S[free], 1)
                dve.sem_inc(S["keys_free"], 1)
                ch.link(v.tensor_tensor(logit, a_s[:], a_d[:], ALU.add))
                ch.link(v.scalar_tensor_tensor(logit, logit, 0.2, logit, ALU.mult, ALU.max))
                for i in range(HEADS):
                    ch.mark(v.tensor_tensor_scan(top[:, i, 1:], fence[:], logit[:, i], -BIG, *TOP))
                dve.wait_ge(ch.s, ch.first + ch.n)
                ch.mark(v.tensor_copy(tails[:, 0, 0:HEADS], top[:, :, C]))
                ch.link(v.tensor_scalar(lasts[:], lasts[:], 1.0, BIG, ALU.subtract, ALU.mult))
                v.tensor_copy(tails[:, 1, 0:HEADS], lasts[:].broadcast_to([P, HEADS])).then_inc(S["tail_ready"], 1)
                carried(1, HEADS, state_m, TOP, carry_m[:])
                ch.mark(v.tensor_copy(top[:, :, 0], carry_m[:]))
                for i in range(HEADS):
                    ch.mark(v.tensor_tensor_scan(top[:, i, 1:], fence[:], logit[:, i], carry_m[:, i:i + 1], *TOP))
                dve.wait_ge(ch.s, ch.first + ch.n)
                ch.link(v.tensor_tensor(keep, top[:, :, 0:C], top[:, :, 1:], ALU.subtract))
                v.tensor_scalar(keep, keep, 0.0, None, ALU.min).then_inc(S["exp_go"], 1)
                v.tensor_tensor(wgt[:, 0:HEADS], logit, top[:, :, 1:], ALU.subtract).then_inc(S["exp_go"], 1)
                ch.link(v.tensor_tensor(passing[:], carry_m[:], top[:, :, C], ALU.subtract))
                v.scalar_tensor_tensor(passing[:], passing[:], 0.0, lasts[:].broadcast_to([P, HEADS]), ALU.min,
                                       ALU.add).then_inc(S["exp_go"], 1)
                dve.wait_ge(S["exp_done"], 3 * k + 1)
                ch.mark(v.tensor_tensor(keep, keep, same[:].unsqueeze(1).broadcast_to([P, HEADS, C]), ALU.mult))
                dve.wait_ge(S["exp_done"], 3 * k + 2)
                dve.wait_ge(S["h_copied"], 2 * k + 2)
                for i in range(HEADS):
                    ch.mark(v.tensor_tensor(wgt[:, HEADS + NE * i:HEADS + NE * (i + 1)], h_s[:, NE * i:NE * (i + 1)],
                                            wgt[:, i:i + 1].broadcast_to([P, NE, C]), ALU.mult))
                dve.wait_ge(ch.s, ch.first + ch.n)

                def head(c):
                    return c if c < HEADS else (c - HEADS) // NE

                for c in range(SUMS):
                    ch.mark(v.tensor_tensor_scan(part[:, c], keep[:, head(c)], wgt[:, c], 0.0, *SUM))
                dve.wait_ge(ch.s, ch.first + ch.n)
                dve.wait_ge(S["exp_done"], 3 * k + 3)
                ch.mark(v.tensor_copy(tails[:, 0, :], part[:, :, C - 1]))
                ch.mark(v.tensor_copy(tails[:, 1, 0:HEADS], passing[:]))
                v.tensor_copy(tails[:, 1, HEADS:].rearrange("p (a b) -> p a b", b=NE),
                              passing[:].unsqueeze(2).broadcast_to([P, HEADS, NE])).then_inc(S["tail_ready"], 1)
                carried(2, SUMS, state_s, SUM, carry_s[:])
                dve.wait_ge(S["res_out"], 16 * (k + 1))
                for c in range(SUMS):
                    ch.mark(v.tensor_tensor_scan(results_s[:, :, HEADS + c], keep[:, head(c)], wgt[:, c],
                                                 carry_s[:, c:c + 1], *SUM))
                v.tensor_copy(results_s[:, :, 0:HEADS].rearrange("p c o -> p o c"), top[:, :, 1:])\
                 .then_inc(S["res_ready"], 1)
                dve.wait_ge(S["res_ready"], k + 1)
                assert ch.n == EDGE_OPS, ch.n

            words_under(1)
            counts(1)

            cf = Counted(dve, S["f_chain"])
            link, mark = cf.link, cf.mark

            def by_head(ap):
                return ap.unsqueeze(2).broadcast_to([P, TILES, HEADS])

            def last_row(lo, hi):
                return clamped[:, lo:hi].unsqueeze(1).broadcast_to([P, TILES, hi - lo])

            a_dst = ext[:, :, ROW:EXT]
            dve.wait_ge(S["clamped_in"], 16)
            link(v.tensor_tensor(mg[:, 1], ext[:, :, HC:ROW], a_dst, ALU.add))
            link(v.tensor_tensor(mg[:, 2], a_dst, last_row(HC, ROW), ALU.add))
            link(v.scalar_tensor_tensor(mg[:, 1:3], mg[:, 1:3], 0.2, mg[:, 1:3], ALU.mult, ALU.max))
            link(v.tensor_scalar(has[:], has[:], 1.0, BIG, ALU.subtract, ALU.mult))
            link(v.tensor_tensor(mg[:, 2], mg[:, 2], by_head(has[:, 1]), ALU.add))
            dve.wait_ge(S["ends_in"], 16 * TILES)
            link(v.tensor_tensor(mg[:, 0], ends[:, :, 0:HEADS], by_head(has[:, 0]), ALU.add))
            link(v.tensor_tensor(mtop, mg[:, 0], mg[:, 1], ALU.max))
            link(v.tensor_tensor(mtop, mtop, mg[:, 2], ALU.max))
            v.tensor_tensor(mg, mg, mtop.unsqueeze(1).broadcast_to([P, 3, TILES, HEADS]),
                            ALU.subtract).then_inc(S["mg_go"], 1)
            dve.wait_ge(S["mg_exp"], 1)
            link(v.tensor_tensor(mg[:, 2], mg[:, 2], by_head(count[:, 1]), ALU.mult))
            total = mtop
            mark(v.tensor_tensor(total, ends[:, :, HEADS:2 * HEADS], mg[:, 0], ALU.mult))
            agg = ends[:, :, 2 * HEADS:]

            def heads4(ap):
                return ap.rearrange("p t (h c) -> p t h c", c=NE)

            def wide(ap):
                return ap.unsqueeze(3).broadcast_to([P, TILES, HEADS, NE])

            tmp = xn[:, :, 0:HC]
            tmp2 = xn[:, :, HC:2 * HC]
            for i in range(HEADS):
                s4 = slice(NE * i, NE * (i + 1))

                def w(j):
                    return mg[:, j, :, i:i + 1].broadcast_to([P, TILES, NE])
                mark(v.tensor_tensor(agg[:, :, s4], agg[:, :, s4], w(0), ALU.mult))
                mark(v.tensor_tensor(tmp[:, :, s4], ext[:, :, s4], w(1), ALU.mult))
                mark(v.tensor_tensor(tmp2[:, :, s4], w(2), last_row(NE * i, NE * (i + 1)), ALU.mult))
            dve.wait_ge(S["f_chain"], cf.n)
            mark(v.tensor_tensor(total, total, mg[:, 1], ALU.add))
            link(v.tensor_tensor(agg, agg, tmp, ALU.add))
            mark(v.tensor_tensor(total, total, mg[:, 2], ALU.add))
            link(v.tensor_tensor(agg, agg, tmp2, ALU.add))
            link(v.tensor_scalar(total, total, 1e-16, None, ALU.add))
            link(v.reciprocal(total, total))
            for i in range(HEADS):
                s4 = slice(NE * i, NE * (i + 1))
                mark(v.tensor_tensor(agg[:, :, s4], agg[:, :, s4], total[:, :, i:i + 1].broadcast_to([P, TILES, NE]),
                                     ALU.mult))
            dve.wait_ge(S["f_chain"], cf.n)

            def per_row(ap):
                return ap[:].unsqueeze(1).broadcast_to([P, TILES, HC])

            def per_token(ap, n=HC):
                return ap.unsqueeze(2).broadcast_to([P, TILES, n])

            dve.wait_ge(S["weights_in"], 16 * N_WEIGHTS)
            link(v.tensor_tensor(agg, agg, per_row(bg), ALU.add))
            mean, sd = st2[:, 0], st2[:, 1]
            link(v.tensor_reduce(mean, agg, AX.X, ALU.add))
            link(v.tensor_scalar(mean, mean, 1.0 / HC, None, ALU.mult))
            link(v.tensor_tensor(agg, agg, per_token(mean), ALU.subtract))
            link(v.tensor_tensor(tmp, agg, agg, ALU.mult))
            link(v.tensor_reduce(sd, tmp, AX.X, ALU.add))
            v.tensor_scalar(sd, sd, 1.0 / HC, EPS, ALU.mult, ALU.add).then_inc(S["var_go"], 1)
            dve.wait_ge(S["sd_ready"], 1)
            link(v.reciprocal(sd, sd))
            link(v.tensor_tensor(agg, agg, per_token(sd), ALU.mult))
            link(v.tensor_tensor(agg, agg, per_row(gamma), ALU.mult))
            link(v.tensor_tensor(agg, agg, per_row(beta), ALU.add))
            link(v.tensor_reduce(sc, agg.rearrange("p t (h c) -> p t c h", c=NE), AX.X, ALU.add))
            link(v.tensor_scalar(sc, sc, 1.0 / HEADS, None, ALU.mult))
            link(v.memset(cmp, 0.0))
            for i in range(NE):
                for j in range(i + 1, NE):
                    link(v.tensor_tensor(mtop[:, :, 0], sc[:, :, j], sc[:, :, i], ALU.is_gt))
                    mark(v.tensor_tensor(cmp[:, :, i], cmp[:, :, i], mtop[:, :, 0], ALU.add))
                    link(v.tensor_scalar(mtop[:, :, 1], mtop[:, :, 0], -1.0, 1.0, ALU.mult, ALU.add))
                    link(v.tensor_tensor(cmp[:, :, j], cmp[:, :, j], mtop[:, :, 1], ALU.add))
            link(v.tensor_reduce(mean, sc, AX.X, ALU.max))
            v.tensor_tensor(sc, sc, per_token(mean, NE), ALU.subtract).then_inc(S["gate_go"], 1)
            link(v.tensor_scalar(cmp, cmp, 1.5, None, ALU.is_lt))
            dve.wait_ge(S["gate_exp"], 1)
            link(v.tensor_tensor(gate, sc, cmp, ALU.mult))
            link(v.tensor_reduce(mean, gate, AX.X, ALU.add))
            link(v.reciprocal(mean, mean))
            link(v.tensor_tensor(gate, gate, per_token(mean, NE), ALU.mult))
            dve.wait_ge(S["expert_ready"], NE * NG)
            q = TILES // 4
            for i in range(4):
                s = slice(i * q, (i + 1) * q)
                for e in range(NE):
                    mark(v.tensor_tensor(experts[:, s, e], experts[:, s, e],
                                         gate[:, s, e:e + 1].broadcast_to([P, q, F]), ALU.mult))
                dve.wait_ge(S["f_chain"], cf.n)
                link(v.tensor_tensor(experts[:, s, 0:2], experts[:, s, 0:2], experts[:, s, 2:4], ALU.add))
                mark(v.tensor_tensor(h[:, s, :], h[:, s, :], experts[:, s, 0], ALU.add))
                dve.wait_ge(S["f_chain"], cf.n)
                v.tensor_tensor(h[:, s, :], h[:, s, :], experts[:, s, 1], ALU.add).then_inc(S["y_done"], 1)


_INS = ["x", "L0_tok_W", "L0_attn_W_alpha", "L0_attn_W_beta", "L0_attn_W_unary", "L0_attn_b_unary",
        "L0_attn_W_r", "L0_ffn_W_gat", "L0_ffn_att_src", "L0_ffn_att_dst", "L0_ffn_b_gat",
        "L0_ffn_ln_gamma", "L0_ffn_ln_beta", "L0_ffn_W1", "L0_ffn_b1", "L0_ffn_W2", "L0_ffn_b2",
        "L0_ffn_edge_index"]


def kernel(**inputs):
    import concourse.bacc as bacc
    from concourse.bass_utils import run_bass_kernel_spmd

    nc = bacc.Bacc("TRN2", target_bir_lowering=False, num_devices=1)
    arrays, args = {}, []
    for name in _INS:
        a = np.ascontiguousarray(inputs[name])
        arrays[f"in_{name}"] = a
        args.append(nc.dram_tensor(f"in_{name}", a.shape, mybir.dt.from_np(a.dtype), kind="ExternalInput").ap())
    b, l, f = inputs["x"].shape
    args.append(nc.dram_tensor("out_0", (b, l // 4, f), F32, kind="ExternalOutput").ap())
    audio_tower(nc, *args)
    r = run_bass_kernel_spmd(nc, [arrays], core_ids=[0])
    return r.results[0]["out_0"]
```

```python
import numpy as np
from contextlib import ExitStack

import concourse.bass as bass
from concourse import mybir

F32 = mybir.dt.float32
I32 = mybir.dt.int32
BF16 = mybir.dt.bfloat16
ALU = mybir.AluOpType
ACT = mybir.ActivationFunctionType
AX = mybir.AxisListType


def audio_tower(nc, x, tok_w, w_alpha, w_beta, w_unary, b_unary, w_r, w_gat, att_src, att_dst,
                b_gat, ln_gamma, ln_beta, w1, b1, w2, b2, edges, out):
    P = 128
    B, L, F = x.shape
    POOL = 4
    SEQ = L // POOL
    M = B * SEQ
    TILES = M // P
    E = edges.shape[1]
    W = E // P
    HALF = W // 2
    NE, _, HID = w1.shape
    HEADS = att_src.shape[0]
    HC = HEADS * NE
    ROW = HC + HEADS
    EXT = HC + 2 * HEADS
    EPS = 1e-5
    BIG = 1e30

    SRC_BITS = M.bit_length() - 1
    NODE = 1 << (2 * SRC_BITS + 2)
    FAR = 1 << (2 * SRC_BITS + 1)
    LOG_W, LOG_E = W.bit_length() - 1, E.bit_length() - 1
    STEP = 128
    HEADS_N = E // STEP
    RANGE = M // P
    NS = RANGE + 1
    BLOCK_BIT = SRC_BITS + RANGE.bit_length() - 1
    WINDOW = 6
    C = 40
    HC2 = C // 2
    CHUNK = P * C
    MAX_CHUNKS = -(-E // CHUNK)
    ROOM = MAX_CHUNKS * CHUNK
    MAX_PASSES = -(-HEADS_N // WINDOW)
    PAD = 64
    OUTC = HEADS + HEADS + HC
    SUMS = HEADS + HC

    GA = 4
    FRAMES = 4
    GB = 4
    NB = TILES // GB
    GE = 8
    NG = TILES // GE

    sorted_rows = nc.dram_tensor("sorted_rows", (HEADS_N + 1, STEP), F32).ap()
    sorted_padded = nc.dram_tensor("sorted_padded", (PAD + ROOM + 2 * CHUNK,), F32).ap()
    table = nc.dram_tensor("table", (M, ROW), F32).ap()
    inject = nc.dram_tensor("inject", (E + M, HEADS), F32).ap()
    results = nc.dram_tensor("results", (ROOM, OUTC), F32).ap()

    with ExitStack() as ctx:
        def sb(name, shape, dt=F32):
            return ctx.enter_context(nc.sbuf_tensor(name, shape, dt))

        def sem(name):
            return ctx.enter_context(nc.semaphore(name))

        ident = sb("ident", [P, P])
        lane = sb("lane", [P, 1], I32)
        lane_bit = sb("lane_bit", [P, LOG_E - LOG_W + 1], I32)
        sign = sb("sign", [P, LOG_E - LOG_W + 1])
        turn = sb("turn", [P, LOG_E - LOG_W + 1])
        pair_mask = sb("pair_mask", [P, P])
        zeros = sb("zeros", [P, 528])
        place_i = sb("place_i", [P, RANGE], I32)
        place = sb("place", [P, RANGE])
        block_row_i = sb("block_row_i", [P, 2, P + 1], I32)
        block_row = sb("block_row", [P, 2, P + 1])
        first_key_i = sb("first_key_i", [P, 2], I32)
        first_key = sb("first_key", [P, 2])
        row_of_i = sb("row_of_i", [P, WINDOW], I32)
        row_of = sb("row_of", [P, WINDOW])
        far_row = sb("far_row", [1, STEP])
        tok_w2 = sb("tok_w2", [P, P])
        wa = sb("wa", [F, F])
        wb = sb("wb", [F, F])
        wu = sb("wu", [F, F + 1])
        wr = sb("wr", [F, F])
        wr_t = sb("wr_t", [F, F])
        w_score = sb("w_score", [F, F])
        w_value = sb("w_value", [F + 1, F])
        w_ext = sb("w_ext", [F, EXT])
        wg_t = sb("wg_t", [HC, F])
        att_col = sb("att_col", [HC, 2])
        att_sel = sb("att_sel", [HC, 2, HEADS])
        head_mask = sb("head_mask", [HC, HEADS])
        w1_s = sb("w1_s", [F, NE, HID])
        w2_s = sb("w2_s", [HID, NE, F])
        b1_s = sb("b1_s", [HID, NE])
        b2_row = sb("b2_row", [1, 3, NE * F])
        b2_part = sb("b2_part", [1, 3, NE, F], BF16)
        b2_rows = sb("b2_rows", [3, NE, GE, F], BF16)
        ones_row = sb("ones_row", [3, P], BF16)
        bg = sb("bg", [P, HC])
        gamma = sb("gamma", [P, HC])
        beta = sb("beta", [P, HC])

        sort = [sb("sort0", [P, W]), sb("sort1", [P, W])]
        h = sb("h", [P, TILES, F])
        xn = sb("xn", [P, TILES, F])
        xn2_t = sb("xn2_t", [F, M])
        arena = sb("arena", [P, TILES * NE * F])
        ext = sb("ext", [P, TILES, EXT])
        ends = sb("ends", [P, TILES, OUTC])
        stat = sb("stat", [P, 2, TILES])
        lower = sb("lower", [P, 2, NS])
        under = sb("under", [P, NS])
        win_row = sb("win_row", [P, 2, WINDOW])
        win_i = sb("win_i", [P, 2, WINDOW], I32)
        count = sb("count", [P, 2, TILES])
        has = sb("has", [P, 2, TILES])
        sides = sb("sides", [P, 4, 2, RANGE])
        by_tile = sb("by_tile", [P, 3, TILES])
        start_i = sb("start_i", [P, TILES], I32)
        end_i = sb("end_i", [P, TILES], I32)
        under_row = sb("under_row", [1, 2, P + 1])
        need_row = sb("need_row", [1, 2, P])
        sizes = sb("sizes", [1, 4])
        sizes_back = sb("sizes_back", [1, 4])
        sizes_i = sb("sizes_i", [1, 4], I32)

        def carve(base, at, *shape, partitions=P):
            size = int(np.prod(shape))
            ap = base[0:partitions, at:at + size]
            names = "abcd"[:len(shape)]
            if len(shape) > 1:
                ap = ap.rearrange(f"p ({' '.join(names)}) -> p {' '.join(names)}",
                                  **{n: s for n, s in zip(names[1:], shape[1:])})
            return ap, at + size

        def several(n, at, *shape, **kw):
            made = []
            for _ in range(n):
                a, at = carve(arena, at, *shape, **kw)
                made.append(a)
            return made, at

        x_t, after = several(3, 0, GB * P, partitions=F + 1)
        frames, at = several(FRAMES, after, GA, POOL * F)
        frames_t, at = several(2, at, GA * POOL // 2, P)
        logits, at = several(2, at, GA, POOL, F)
        tree, at = several(2, at, GA, 3, F)
        assert at <= TILES * NE * F
        t_t, at = several(2, after, GB * P, partitions=F)
        value, at = several(3, at, GB, F)
        score, at = several(2, at, GB, P)
        attended, at = several(2, at, GB, F)
        square = arena[:, after:after + TILES * F].rearrange("p (t f) -> p t f", f=F)
        experts = arena[:, :].rearrange("p (t e f) -> p t e f", e=NE, f=F)
        hidden = [ends[:].rearrange("p t o -> p (t o)")[:, 0:GE * P], sb("hidden", [P, GE * P])[:]]

        keys = sb("keys", [P, C + 1], I32)
        segs = sb("segs", [P, C + 1], I32)
        same_next = sb("same_next", [P, C])
        same = sb("same", [P, C])
        src_a = sb("src_a", [P, HC2], I32)
        src_b = sb("src_b", [P, HC2], I32)
        rows_a = sb("rows_a", [P, HC2, ROW])
        rows_b = sb("rows_b", [P, HC2, ROW])
        inj = sb("inj", [P, C, HEADS])
        fence = sb("fence", [P, C])
        lasts = sb("lasts", [P, 1])
        a_s = sb("a_s", [P, HEADS, C])
        a_d = sb("a_d", [P, HEADS, C])
        top = sb("top", [P, HEADS, C + 1])
        xn_flat = xn[:].rearrange("p t f -> p (t f)")
        at = 0
        h_s, at = carve(xn_flat, at, HC, C)
        wgt, at = carve(xn_flat, at, SUMS, C)
        part, at = carve(xn_flat, at, SUMS, C)
        logit, at = carve(xn_flat, at, HEADS, C)
        keep, at = carve(xn_flat, at, HEADS, C)
        own_agg, at = carve(xn_flat, TILES * (F - HC), TILES, HC)
        tmp_all, _ = carve(xn_flat, 0, TILES, HC)
        assert at <= TILES * F
        results_s = sb("results_s", [P, C, OUTC])
        tails = sb("tails", [P, 2, SUMS])
        passing = sb("passing", [P, HEADS])
        across = sb("across", [SUMS, 2, P])
        state_d = sb("state_d", [HEADS, P + 1])
        state_m = sb("state_m", [HEADS, P + 1])
        state_s = sb("state_s", [SUMS, P + 1])
        carry_d = sb("carry_d", [P, HEADS])
        carry_m = sb("carry_m", [P, HEADS])
        carry_s = sb("carry_s", [P, SUMS])
        clamped = sb("clamped", [P, ROW])

        at = 0
        mg, at = carve(sort[0], at, 3, TILES, HEADS)
        mtop, at = carve(sort[0], at, TILES, HEADS)
        cmp, at = carve(sort[0], at, TILES, NE)
        gate, at = carve(sort[0], at, TILES, NE)
        sc, at = carve(sort[0], at, TILES, NE)
        st2 = sb("st2", [P, 2, TILES])

        HPP = HEADS_N // P
        head_i = sb("head_i", [P, HPP], I32)
        head_block = sb("head_block", [P, HPP])
        heads_under = [sb(f"heads_under{i}", [P, 2, 2, P + 1], BF16) for i in range(2)]
        SUMMED = HPP // 2 % 2
        ones_col = sb("ones_col", [P, 1], BF16)
        windows = [sort[0][:, i * WINDOW * STEP:(i + 1) * WINDOW * STEP] for i in range(2)]
        win_key = sort[1][:, 0:WINDOW * STEP].bitcast(I32)
        win_diff = sort[1][:, WINDOW * STEP:2 * WINDOW * STEP]
        win_node = sb("win_node", [P, WINDOW * STEP], BF16)
        less = [sort[i][:, 2 * WINDOW * STEP:5 * WINDOW * STEP // 2].bitcast(BF16) for i in range(2)]

        pt = [ctx.enter_context(nc.psum_tensor(f"pt{i}", [P, 1024], F32)) for i in range(4)]

        names = """weights_in edges_in frames_in0 frames_in1 frames_in2 frames_in3 lane_ready ident_ready mask_ready
            node_ready zeros_ready prep_pe prep_act prep_dve v_chain sorted_ops turned up_done down_done
            hi_ready frames_free frames_t_done frames_t_ready logits_done shifted pool_exp pool_steps pool_max
            pooled p_chain inverse norm_mean norm_centred norm_squared norm_var norm_sd norm_scale norm_done
            x_t_done x_t_ready t_done t_ready score_done score_ready score_masked att_done att_ready attn_added
            ext_x_done ext_x_ready ext_done ext_ready hidden_done hidden_ready expert_done expert_ready b2_in
            b2_split srt_out heads_split heads_counted sizes_ready win_idx0 win_idx1 win_in0 win_in1 w_chain0
            w_chain1 sides_ready sides_turned far_row_ready table_out zero_out scatter_ready scattered keys_in
            keys_free inj_in inj_free idx_a idx_b rows_a_in rows_b_in rows_a_free rows_b_free e_chain h_copied
            tail_ready tail_t state_ready carry_t exp_go exp_done res_ready res_out ends_in0 ends_in1 ends_in2
            clamped_in mg_go mg_exp f_chain var_go sd_ready gate_go gate_exp own_go own_exp gated last_gated
            y_done out_done pad_out results_zero held_pe held_pool""".split()
        S = {n: sem(n) for n in names}

        def hold(eng, name, value):
            eng.wait_ge(S[name], value)
            eng.sem_inc(S["held_" + ("pe" if eng is nc.tensor else "pool")], 1)

        class Counted:
            def __init__(self, eng, s, first=0):
                self.eng, self.s, self.n = eng, s, 0
                self.first = first

            def mark(self, ins):
                ins.then_inc(self.s, 1)
                self.n += 1

            def link(self, ins):
                self.mark(ins)
                self.eng.wait_ge(self.s, self.first + self.n)

        block = ctx.enter_context(nc.Block())

        IN_ROW = LOG_W - 1
        IN_ROW_OPS = 4 * IN_ROW * (IN_ROW + 1) // 2

        def level_start(k):
            ops, cur = IN_ROW_OPS, (IN_ROW * (IN_ROW + 1) // 2) % 2
            for j in range(LOG_W, k):
                if j == LOG_W:
                    ops += 2 + 4 * (LOG_W - 1)
                    cur = (cur + 1 + LOG_W) % 2
                else:
                    ops += 4 * (j - LOG_W) + 2 + 12 + 28
                    cur = (cur + j - LOG_W - 1 + 4 + 7) % 2
            return ops, cur

        def level_down(k):
            ops, cur = level_start(k)
            return ops + 4 * (k - LOG_W) + 2 + 12, (cur + k - LOG_W - 1 + 4) % 2

        SORT_OPS, SORT_END = level_start(LOG_E + 1)

        AHEAD_ROWS, AHEAD_UP, AHEAD_DOWN = 1, 1, 1

        def ended_rows(k, i):
            return level_start(k)[0] - 2 * (1 - i) * (AHEAD_ROWS if k > LOG_W else 1)

        def half(buf, i):
            return sort[buf][:, i * HALF:(i + 1) * HALF]

        def pairs(ap, s):
            return ap.rearrange("p (a t s) -> p a t s", t=2, s=s)

        MEAN_STAGE, VAR_STAGE = 43, 49
        TURN_SLOT = 1
        none = range(0)
        FIRST_SLOTS = range(0, 5)
        ATTENTION = {12: (range(5, 7), range(7, 10)), 13: (range(10, 13), range(13, 16)), 14: (range(16, 19), none)}
        NORM_LEVEL = LOG_W + 3
        NODES = {15: (none, range(0, 4)), 16: (range(4, 9), none)}
        EXPERT = {16: (none, range(0, 2)), 17: (range(2, 5), range(5, 8)), 18: (range(8, 11), range(11, 14))}
        LAST_SLOTS = range(14, NE * NG + 1)
        N_WEIGHTS = 19 + 3 * NE
        QUARTERS = [slice(i * TILES // 4, (i + 1) * TILES // 4) for i in range(4)]

        PARTS = ((0, 12), (12, 24), (36, 28))

        GATHERS = HC2 * 16
        FIND_SLOT, COUNT_SLOT, ROWS_SLOT = LAST_SLOTS[7], LAST_SLOTS[15], LAST_SLOTS[9]

        @block.sync
        def _(sp):
            words = edges.rearrange("t (p w) -> p t w", p=P)
            sp.dma_start(sort[0][:].bitcast(I32), words[:, 1, :]).then_inc(S["edges_in"], 16)
            sp.dma_start(sort[1][:].bitcast(I32), words[:, 0, :]).then_inc(S["edges_in"], 16)
            n_w = 0
            for dst, src in (
                (tok_w2[0:F, 0:F], tok_w), (tok_w2[F:P, F:P], tok_w), (wa[:], w_alpha), (wb[:], w_beta),
                (wu[:, 0:F], w_unary), (wu[:, F:F + 1], b_unary.rearrange("(f a) -> f a", a=1)),
                (wr[:], w_r), (w_ext[:, 0:HC], w_gat),
                (att_col[:, 0:1], att_src.rearrange("h (c a) -> (h c) a", a=1)),
                (att_col[:, 1:2], att_dst.rearrange("h (c a) -> (h c) a", a=1)),
            ):
                if n_w == 0:
                    sp.wait_ge(S["zeros_ready"], 2)
                sp.dma_start(dst, src).then_inc(S["weights_in"], 16)
                n_w += 1
            assert n_w == 10
            sp.dma_start(b2_row[:, 0, :], b2.rearrange("(a e) f -> a (e f)", a=1)).then_inc(S["b2_in"], 16)
            fr = x.rearrange("b (s w) f -> (b s) (w f)", w=POOL).rearrange("(t p) c -> p t c", p=P)
            with sp.Fori(0, TILES // GA // FRAMES) as k:
                for s in range(FRAMES):
                    i = FRAMES * k + s
                    sp.wait_ge(S["frames_free"], i + 1)
                    sp.dma_start(frames[s], fr[:, bass.ds(i * GA, GA), :])\
                      .then_inc(S[f"frames_in{s}"], 16)
            for dst, src in (
                (w1_s[:], w1.rearrange("e d f -> d e f")), (w2_s[:], w2.rearrange("e f d -> f e d")),
                *[(b1_s[:, e:e + 1], b1[e, :].rearrange("(f a) -> f a", a=1)) for e in range(NE)],
                (bg[:], b_gat.partition_broadcast(P)), (gamma[:], ln_gamma.partition_broadcast(P)),
                (beta[:], ln_beta.partition_broadcast(P)),
            ):
                sp.dma_start(dst, src).then_inc(S["weights_in"], 16)
            sp.wait_ge(S["b2_split"], 1)
            for i in range(3):
                for e in range(NE):
                    sp.dma_start(b2_rows[i:i + 1, e], b2_part[:, i, e].unsqueeze(1).broadcast_to([1, GE, F]))\
                      .then_inc(S["weights_in"], 16)
            flat = inject.rearrange("e h -> (e h)")
            part_n = P * 528
            for i in range((E + M) * HEADS // part_n):
                sp.dma_start(flat[i * part_n:(i + 1) * part_n].rearrange("(p c) -> p c", p=P), zeros[:])\
                  .then_inc(S["zero_out"], 16)
            for i in range(16):
                n = E // 16
                sp.dma_start(results[i * n:(i + 1) * n, :].rearrange("(p c) o -> p (c o)", p=P)
                             .rearrange("p (r z) -> p r z", z=512),
                             zeros[:, 0:512].unsqueeze(1).broadcast_to([P, n * OUTC // P // 512, 512]))\
                  .then_inc(S["results_zero"], 16)
            sp.dma_start(sorted_padded[0:PAD].rearrange("(p c) -> p c", p=PAD), zeros[0:PAD, 0:1])\
              .then_inc(S["pad_out"], 16)
            behind = ROOM + 2 * CHUNK - E
            sp.dma_start(sorted_padded[PAD + E:].rearrange("(p c) -> p c", p=P), zeros[:, 0:behind // P])\
              .then_inc(S["pad_out"], 16)
            sp.wait_ge(S["far_row_ready"], 1)
            sp.dma_start(sorted_rows[HEADS_N:HEADS_N + 1, :], far_row[:]).then_inc(S["pad_out"], 16)
            sp.wait_ge(S["ext_ready"], NG)
            sp.dma_start(table.rearrange("(t p) c -> p t c", p=P), ext[:, :, 0:ROW]).then_inc(S["table_out"], 16)
            sp.wait_ge(S["table_out"], 16)
            sp.dma_start(clamped[:], table[M - 1, :].partition_broadcast(P)).then_inc(S["clamped_in"], 16)
            sp.wait_ge(S["sorted_ops"], SORT_OPS)
            done = sort[SORT_END]
            sp.dma_start(sorted_rows[0:HEADS_N, :].rearrange("(p c) s -> p (c s)", p=P), done[:])\
              .then_inc(S["srt_out"], 16)
            sp.dma_start(sorted_padded[PAD:PAD + E].rearrange("(p c) -> p c", p=P), done[:])\
              .then_inc(S["srt_out"], 16)
            sp.wait_ge(S["pad_out"], 48)
            sp.wait_ge(S["srt_out"], 32)

            def load_keys(k):
                first = PAD - 1 + k * CHUNK
                sp.dma_start(keys[:].bitcast(F32), bass.AP(tensor=sorted_padded.tensor, offset=first,
                                                           ap=[[C, P], [1, C + 1]]))\
                  .then_inc(S["keys_in"], 16)

            load_keys(0)
            sp.wait_ge(S["sizes_ready"], 1)
            chunks = sp.value_load(sizes_i[0:1, 2:3], min_val=2, max_val=MAX_CHUNKS)
            sp.wait_ge(S["keys_free"], 1)
            load_keys(1)
            sp.wait_ge(S["scattered"], 16 * TILES)
            res = results.rearrange("(k p c) o -> k p (c o)", p=P, c=C)
            injs = inject[0:ROOM, :].rearrange("(k p c) h -> k p (c h)", p=P, c=C)
            sp.wait_ge(S["results_zero"], 16 * 16)
            with sp.Fori(0, chunks) as k:
                sp.wait_ge(S["inj_free"], k + 1)
                sp.dma_start(inj[:].rearrange("p c h -> p (c h)"),
                             injs[bass.ds(k, 1), :, :].rearrange("a p c -> (a p) c"))\
                  .then_inc(S["inj_in"], 16)
                sp.wait_ge(S["keys_free"], k + 2)
                sp.dma_start(keys[:].bitcast(F32), bass.AP(tensor=sorted_padded.tensor,
                                                           offset=PAD - 1 + 2 * CHUNK + k * CHUNK,
                                                           ap=[[C, P], [1, C + 1]]))\
                  .then_inc(S["keys_in"], 16)
                sp.wait_ge(S["res_ready"], k + 1)
                sp.dma_start(res[bass.ds(k, 1), :, :].rearrange("a p c -> (a p) c"),
                             results_s[:].rearrange("p c o -> p (c o)")).then_inc(S["res_out"], 16)
            rows_out = out.rearrange("b s f -> (b s) f").rearrange("(t p) f -> p t f", p=P)
            for i, (first, n) in enumerate(PARTS):
                sp.wait_ge(S["y_done"], i + 1)
                sp.dma_start(rows_out[:, first:first + n, :], h[:, first:first + n, :]).then_inc(S["out_done"], 16)
            sp.wait_ge(S["out_done"], 16 * len(PARTS))

        @block.gpsimd
        def _(pool):
            g = nc.gpsimd
            g.memset(zeros[:], 0.0).then_inc(S["zeros_ready"], 1)
            g.memset(tok_w2[:], 0.0).then_inc(S["zeros_ready"], 1)
            g.iota(lane[:], pattern=[[0, 1]], base=0, channel_multiplier=1).then_inc(S["lane_ready"], 1)
            g.iota(place_i[:], pattern=[[1, RANGE]], base=E, channel_multiplier=RANGE).then_inc(S["node_ready"], 1)
            g.iota(block_row_i[:], pattern=[[FAR >> BLOCK_BIT, 2], [1, P + 1]], base=NODE >> BLOCK_BIT,
                   channel_multiplier=0).then_inc(S["node_ready"], 1)
            g.iota(first_key_i[:], pattern=[[FAR >> SRC_BITS, 2]], base=NODE >> SRC_BITS,
                   channel_multiplier=RANGE).then_inc(S["node_ready"], 1)
            g.iota(row_of_i[:], pattern=[[1, WINDOW]], base=0, channel_multiplier=0).then_inc(S["node_ready"], 1)
            g.memset(far_row[:], 3e38).then_inc(S["far_row_ready"], 1)
            ch = Counted(pool, S["p_chain"])
            ch.link(g.memset(ident[:], 0.0))
            ch.link(g.memset(pair_mask[:], 0.0))
            ch.link(g.memset(head_mask[:], 1.0))
            ch.link(g.memset(ones_row[:], 1.0))
            for ones in x_t:
                ch.link(g.memset(ones[F:F + 1, :], 1.0))
            ch.link(g.memset(ones_col[:], 1.0))
            CHAIN = ch.n + 3
            g.affine_select(out=ident[:], in_=ident[:], compare_op=ALU.not_equal, fill=1.0, base=0,
                            pattern=[[-1, P]], channel_multiplier=1).then_inc(S["ident_ready"], 1)
            ch.link(g.memset(pair_mask[0:SEQ, 0:SEQ], 1.0))
            ch.link(g.memset(pair_mask[SEQ:P, SEQ:P], 1.0))
            ch.link(g.affine_select(out=head_mask[:], in_=head_mask[:], compare_op=ALU.is_ge, fill=0.0, base=0,
                                    pattern=[[-NE, HEADS]], channel_multiplier=1))
            g.affine_select(out=pair_mask[:], in_=pair_mask[:], compare_op=ALU.not_equal, fill=0.0, base=0,
                            pattern=[[-1, P]], channel_multiplier=1).then_inc(S["mask_ready"], 1)
            g.affine_select(out=head_mask[:], in_=head_mask[:], compare_op=ALU.is_ge, fill=0.0, base=NE - 1,
                            pattern=[[NE, HEADS]], channel_multiplier=-1).then_inc(S["mask_ready"], 1)
            pool.wait_ge(S["mask_ready"], 2)

            A_OPS = 3
            with pool.Fori(0, TILES // GA // FRAMES) as k:
                for s in range(FRAMES):
                    i = FRAMES * k + s
                    ch = Counted(pool, S["pool_steps"], i * A_OPS)
                    lg, tr = logits[s % 2], tree[s % 2]
                    fr = frames[s].rearrange("p t (w f) -> p t w f", w=POOL)
                    mine = bass.ds(i * GA, GA)
                    pool.wait_ge(S["pool_exp"], i + 1)
                    ch.mark(g.tensor_tensor(tr[:, :, 0:2], lg[:, :, 0:2], lg[:, :, 2:4], ALU.add))
                    ch.link(g.tensor_tensor(fr, fr, lg, ALU.mult))
                    g.tensor_tensor(xn[:, mine, :], tr[:, :, 0], tr[:, :, 1], ALU.add).then_inc(S["pooled"], 1)
                    ch.link(g.tensor_tensor(lg[:, :, 0:2], fr[:, :, 0:2], fr[:, :, 2:4], ALU.add))
                    assert ch.n == A_OPS
                    g.tensor_tensor(h[:, mine, :], lg[:, :, 0], lg[:, :, 1], ALU.add).then_inc(S["pooled"], 1)
                    pool.wait_ge(S["pooled"], 2 * i + 2)
                    pool.sem_inc(S["frames_free"], 1)

            def over(ap):
                return ap.unsqueeze(2).broadcast_to([P, TILES // 4, F])

            def centre(n):
                pool.wait_ge(S["norm_mean"], n)
                for q in QUARTERS:
                    g.tensor_tensor(xn[:, q], h[:, q], over(stat[:, 0, q]), ALU.subtract)\
                     .then_inc(S["norm_centred"], 1)

            def rescale(n):
                pool.wait_ge(S["norm_scale"], n)
                for q in QUARTERS:
                    g.tensor_tensor(xn[:, q], xn[:, q], over(stat[:, 1, q]), ALU.mult).then_inc(S["norm_done"], 1)

            pool.wait_ge(S["inverse"], 2)
            g.tensor_tensor(xn[:], xn[:], square, ALU.mult).then_inc(S["inverse"], 1)
            centre(1)
            rescale(1)

            pool.wait_ge(S["norm_done"], 4)
            with pool.Fori(0, NB // 2) as k:
                for r in range(2):
                    n = 2 * k + r
                    hold(pool, "score_ready", n + 1)
                    g.tensor_tensor(score[r], score[r], pair_mask[:].unsqueeze(1).broadcast_to([P, GB, P]),
                                    ALU.mult).then_inc(S["score_masked"], 1)
                    mine = bass.ds(n * GB, GB)
                    g.tensor_tensor(h[:, mine, :], h[:, mine, :], xn[:, mine, :], ALU.add)\
                     .then_inc(S["p_chain"], 1)
                    pool.wait_ge(S["p_chain"], CHAIN + 1 + n)
                    hold(pool, "att_ready", n + 1)
                    g.tensor_tensor(h[:, mine, :], h[:, mine, :], attended[r], ALU.add)\
                     .then_inc(S["attn_added"], 1)

            pool.wait_ge(S["attn_added"], NB)
            centre(2)
            rescale(2)

            pool.wait_ge(S["sizes_ready"], 1)
            pool.wait_ge(S["srt_out"], 32)
            pool.wait_ge(S["pad_out"], 48)
            for cls in range(2):
                passes = pool.value_load(sizes_i[0:1, cls:cls + 1], min_val=1, max_val=MAX_PASSES)
                with pool.Fori(0, passes) as r:
                    hold(pool, f"win_idx{cls}", r + 1)
                    for j in range(WINDOW):
                        g.indirect_dma_start(windows[cls][:, j * STEP:(j + 1) * STEP], None, sorted_rows,
                                             bass.IndirectOffsetOnAxis(ap=win_i[:, cls, j:j + 1], axis=0))\
                         .then_inc(S[f"win_in{cls}"], 16)

            def gather(k):
                for idx, ready, rows, landed, free in (
                    (src_a, "idx_a", rows_a, "rows_a_in", "rows_a_free"),
                    (src_b, "idx_b", rows_b, "rows_b_in", "rows_b_free"),
                ):
                    hold(pool, ready, k + 1)
                    hold(pool, free, 2 * k + 2)
                    for c in range(HC2):
                        g.indirect_dma_start(rows[:, c, :], None, table,
                                             bass.IndirectOffsetOnAxis(ap=idx[:, c:c + 1], axis=0))\
                         .then_inc(S[landed], 16)

            pool.wait_ge(S["table_out"], 16)
            gather(0)
            pool.wait_ge(S["zero_out"], 16 * 16)
            pool.wait_ge(S["ext_ready"], NG)
            pool.wait_ge(S["scatter_ready"], 1)
            for t in range(TILES):
                g.indirect_dma_start(inject, bass.IndirectOffsetOnAxis(ap=start_i[:, t:t + 1], axis=0),
                                     ext[:, t, ROW:EXT], None).then_inc(S["scattered"], 16)
            chunks = pool.value_load(sizes_i[0:1, 2:3], min_val=2, max_val=MAX_CHUNKS)
            with pool.Fori(1, chunks) as k:
                gather(k)
            hold(pool, "res_out", 16 * chunks + 16)
            for i, (first, n) in enumerate(PARTS):
                for t in range(first, first + n):
                    g.indirect_dma_start(ends[:, t, :], None, results[0:E, :],
                                         bass.IndirectOffsetOnAxis(ap=end_i[:, t:t + 1], axis=0))\
                     .then_inc(S[f"ends_in{i}"], 16)

        @block.scalar
        def _(act):
            a = nc.scalar

            def copy(dst, src, **kw):
                return a.activation(dst, src, ACT.Copy, **kw)

            act.wait_ge(S["prep_pe"], 1)
            copy(w_score[:], pt[0][0:F, 0:F]).then_inc(S["prep_act"], 1)
            copy(wr_t[:], pt[0][0:F, 128:128 + F]).then_inc(S["prep_act"], 1)
            copy(wg_t[:], pt[0][0:HC, 256:256 + F]).then_inc(S["prep_act"], 1)
            act.wait_ge(S["prep_pe"], 2)
            copy(w_value[:], pt[1][0:F + 1, 0:F], scale=1.0 / SEQ).then_inc(S["prep_act"], 1)
            copy(w_ext[:, HC:EXT], pt[1][0:F, 128:128 + 2 * HEADS]).then_inc(S["prep_act"], 1)

            with act.Fori(0, TILES // GA // 2) as k:
                for s in range(2):
                    i = 2 * k + s
                    act.wait_ge(S["frames_t_done"], i + 1)
                    copy(frames_t[s].rearrange("p a b -> p (a b)"), pt[2 * s][:]).then_inc(S["frames_t_ready"], 1)
                    lg = logits[s].rearrange("p a b c -> p (a b c)")
                    act.wait_ge(S["shifted"], i + 3)
                    a.activation(lg, lg, ACT.Exp).then_inc(S["pool_exp"], 1)

            act.wait_ge(S["pooled"], 2 * (TILES // GA))
            a.activation(square, xn[:], ACT.Ln).then_inc(S["inverse"], 1)
            act.wait_ge(S["inverse"], 1)
            a.activation(square, square, ACT.Exp, scale=-1.0).then_inc(S["inverse"], 1)

            def squares(n):
                for i, q in enumerate(QUARTERS):
                    act.wait_ge(S["norm_centred"], 4 * (n - 1) + i + 1)
                    a.activation(square[:, q], xn[:, q], ACT.Square).then_inc(S["norm_squared"], 1)

            def root(n):
                act.wait_ge(S["norm_var"], n)
                a.activation(stat[:, 1], stat[:, 1], ACT.Sqrt).then_inc(S["norm_sd"], 1)

            squares(1)
            root(1)

            def turned(k):
                cur = level_start(k)[1]
                for i in range(2):
                    act.wait_ge(S["sorted_ops"], ended_rows(k, i))
                    copy(half(1 - cur, i), half(cur, i), scale=turn[:, k - LOG_W:k - LOG_W + 1])\
                        .then_inc(S["turned"], 1)

            def attention_slot(j):
                if j < NB:
                    act.wait_ge(S["x_t_done"], j + 1)
                    copy(x_t[j % 3][0:F, :], pt[2][0:F, 0:GB * P]).then_inc(S["x_t_ready"], 1)
                if 0 <= j - 1 < NB:
                    n = j - 1
                    act.wait_ge(S["t_done"], n + 1)
                    copy(t_t[n % 2], pt[2][0:F, 512:512 + GB * P]).then_inc(S["t_ready"], 1)
                    copy(value[n % 3].rearrange("p a b -> p (a b)"), pt[3][:, 512:512 + GB * F])\
                        .then_inc(S["t_ready"], 1)
                if 0 <= j - 2 < NB:
                    n = j - 2
                    act.wait_ge(S["score_done"], n + 1)
                    copy(score[n % 2].rearrange("p a b -> p (a b)"), pt[3][:, 0:GB * P])\
                        .then_inc(S["score_ready"], 1)
                if 0 <= j - 3 < NB:
                    n = j - 3
                    act.wait_ge(S["att_done"], n + 1)
                    if n >= 2:
                        act.wait_ge(S["attn_added"], n - 1)
                    copy(attended[n % 2].rearrange("p a b -> p (a b)"), pt[3][:, 768:768 + GB * F])\
                        .then_inc(S["att_ready"], 1)

            def nodes_slot(j):
                if j == 0:
                    act.wait_ge(S["weights_in"], 16 * N_WEIGHTS)
                if j < NG:
                    act.wait_ge(S["ext_x_done"], j + 1)
                    copy(xn2_t[:, j * GE * P:(j + 1) * GE * P], pt[2][0:F, :]).then_inc(S["ext_x_ready"], 1)
                if j >= 1:
                    act.wait_ge(S["ext_done"], j)
                    copy(ext[:, (j - 1) * GE:j * GE, :],
                         pt[3][:, 512:512 + GE * EXT].rearrange("p (t c) -> p t c", c=EXT))\
                        .then_inc(S["ext_ready"], 1)

            def expert_slot(j):
                if j < NE * NG:
                    e = j % NE
                    act.wait_ge(S["hidden_done"], j + 1)
                    a.activation(hidden[j % 2], pt[2][:], ACT.Gelu, bias=b1_s[:, e:e + 1])\
                     .then_inc(S["hidden_ready"], 1)
                if j >= 1:
                    g, e = divmod(j - 1, NE)
                    act.wait_ge(S["expert_done"], j)
                    copy(experts[:, g * GE:(g + 1) * GE, e, :],
                         pt[3][:, 0:GE * F].rearrange("p (t f) -> p t f", f=F)).then_inc(S["expert_ready"], 1)

            def beside(k, part):
                for j in ATTENTION.get(k, (none, none))[part]:
                    attention_slot(j)
                for j in NODES.get(k, (none, none))[part]:
                    nodes_slot(j)
                for j in EXPERT.get(k, (none, none))[part]:
                    expert_slot(j)

            for j in FIRST_SLOTS:
                if j == TURN_SLOT:
                    turned(LOG_W)
                attention_slot(j)

            for k in range(LOG_W + 1, LOG_E + 1):
                turned(k)
                cur = level_start(k)[1]
                d = 2 ** (k - LOG_W - 1)
                n = k - LOG_W - 1
                for i in range(2):
                    act.wait_ge(S["up_done"], 2 * n + i + 1)
                    copy(pairs(half(1 - cur, i), d)[:, :, 1], pairs(pt[i][:], d)[:, :, 1])\
                        .then_inc(S["hi_ready"], 1)
                if k == NORM_LEVEL + 1:
                    root(2)
                beside(k, 0)
                cur = level_down(k)[1]
                for i in range(2):
                    act.wait_ge(S["down_done"], 2 * n + i + 1)
                    copy(pairs(half(cur, i), P // 2)[:, :, 1], pairs(pt[i][:], P // 2)[:, :, 1])\
                        .then_inc(S["hi_ready"], 1)
                if k == NORM_LEVEL:
                    squares(2)
                beside(k, 1)
            def copy_rows(k):
                for i, (rows, landed, free) in enumerate(((rows_a, "rows_a_in", "rows_a_free"),
                                                          (rows_b, "rows_b_in", "rows_b_free"))):
                    act.wait_ge(S[landed], GATHERS * (k + 1))
                    copy(h_s[:, :, i * HC2:(i + 1) * HC2], rows[:, :, 0:HC].rearrange("p c o -> p o c"))\
                        .then_inc(S["h_copied"], 1)
                    act.wait_ge(S["h_copied"], 2 * k + i + 1)
                    act.sem_inc(S[free], 1)

            for j in LAST_SLOTS:
                if j == ROWS_SLOT:
                    copy_rows(0)
                expert_slot(j)

            def exponentials(k):
                act.wait_ge(S["exp_go"], 3 * k + 1)
                a.activation(keep, keep, ACT.Exp).then_inc(S["exp_done"], 1)
                act.wait_ge(S["exp_go"], 3 * k + 2)
                a.activation(wgt[:, 0:HEADS, :], wgt[:, 0:HEADS, :], ACT.Exp).then_inc(S["exp_done"], 1)
                act.wait_ge(S["exp_go"], 3 * k + 3)
                a.activation(passing[:], passing[:], ACT.Exp).then_inc(S["exp_done"], 1)

            act.wait_ge(S["sizes_ready"], 1)
            chunks = act.value_load(sizes_i[0:1, 2:3], min_val=2, max_val=MAX_CHUNKS)
            with act.Fori(1, chunks) as k:
                exponentials(k)
                act.wait_ge(S["res_ready"], k)
                copy_rows(k)
            exponentials(chunks)

            act.wait_ge(S["own_go"], 1)
            a.activation(mg[:, 1:3], mg[:, 1:3], ACT.Exp).then_inc(S["own_exp"], 1)
            for i, (first, n) in enumerate(PARTS):
                s = slice(first, first + n)
                act.wait_ge(S["mg_go"], i + 1)
                a.activation(mg[:, 0:2, s], mg[:, 0:2, s], ACT.Exp).then_inc(S["mg_exp"], 1)
                act.wait_ge(S["var_go"], i + 1)
                a.activation(st2[:, 1, s], st2[:, 1, s], ACT.Sqrt).then_inc(S["sd_ready"], 1)
                act.wait_ge(S["gate_go"], i + 1)
                a.activation(sc[:, s], sc[:, s], ACT.Exp).then_inc(S["gate_exp"], 1)
                act.wait_ge(S["gated"], i + 1)
                for t in range(first, first + n):
                    copy(experts[:, t, NE - 1], experts[:, t, NE - 1], scale=gate[:, t, NE - 1:NE])\
                        .then_inc(S["last_gated"], 1)

        @block.tensor
        def _(pe):
            t = nc.tensor
            pe.wait_ge(S["weights_in"], 160)
            pe.wait_ge(S["ident_ready"], 1)
            t.matmul(pt[0][0:F, 0:F], wa[:], wb[:], start=True, stop=True)
            t.transpose(pt[0][0:F, 128:128 + F], wr[:], ident[0:F, 0:F])
            t.transpose(pt[0][0:HC, 256:256 + F], w_ext[:, 0:HC], ident[0:F, 0:F]).then_inc(S["prep_pe"], 1)
            pe.wait_ge(S["prep_act"], 3)
            pe.wait_ge(S["prep_dve"], 1)
            t.matmul(pt[1][0:F + 1, 0:F], wu[:], wr_t[:], start=True, stop=True)
            t.matmul(pt[1][0:F, 128:128 + 2 * HEADS], wg_t[:], att_sel[:].rearrange("p a b -> p (a b)"),
                     start=True, stop=True).then_inc(S["prep_pe"], 1)
            pe.wait_ge(S["prep_act"], 5)

            with pe.Fori(0, TILES // GA // FRAMES) as k:
                for f in range(FRAMES):
                    i = FRAMES * k + f
                    s = f % 2
                    hold(pe, f"frames_in{f}", 16 * (k + 1))
                    hold(pe, "shifted", i + 1)
                    for j in range(GA * POOL // 2):
                        ins = t.transpose(pt[2 * s][:, j * P:(j + 1) * P],
                                          frames[f][:, j // 2, (j % 2) * P:(j % 2 + 1) * P], ident[:])
                    ins.then_inc(S["frames_t_done"], 1)
                    hold(pe, "frames_t_ready", i + 1)
                    for j in range(GA * POOL // 2):
                        ins = t.matmul(pt[2 * s + 1][:, j * P:(j + 1) * P], frames_t[s][:, j, :], tok_w2[:],
                                       start=True, stop=True)
                    ins.then_inc(S["logits_done"], 1)

            def attention_slot(j):
                if j < NB:
                    pe.wait_ge(S["norm_done"], 4 * j // NB + 1)
                    if j >= 1:
                        pe.wait_ge(S["x_t_ready"], j)
                    for i in range(GB):
                        ins = t.transpose(pt[2][0:F, i * P:(i + 1) * P], xn[:, j * GB + i, :], ident[:])
                    ins.then_inc(S["x_t_done"], 1)
                if 0 <= j - 1 < NB:
                    n = j - 1
                    x_n = x_t[n % 3]
                    pe.wait_ge(S["x_t_ready"], n + 1)
                    if n >= 1:
                        pe.wait_ge(S["t_ready"], 2 * n)
                    if n >= 3:
                        pe.wait_ge(S["att_ready"], n - 2)
                    t.matmul(pt[2][0:F, 512:512 + GB * P], w_score[:], x_n[0:F, :], start=True, stop=True)
                    for i in range(GB):
                        ins = t.matmul(pt[3][:, 512 + i * F:512 + (i + 1) * F], x_n[:, i * P:(i + 1) * P], w_value[:],
                                       start=True, stop=True)
                    ins.then_inc(S["t_done"], 1)
                if 0 <= j - 2 < NB:
                    n = j - 2
                    pe.wait_ge(S["t_ready"], 2 * n + 2)
                    if n >= 1:
                        pe.wait_ge(S["score_ready"], n)
                    for i in range(GB):
                        cols = slice(i * P, (i + 1) * P)
                        ins = t.matmul(pt[3][:, cols], x_t[n % 3][0:F, cols], t_t[n % 2][:, cols],
                                       start=True, stop=True)
                    ins.then_inc(S["score_done"], 1)
                if 0 <= j - 3 < NB:
                    n = j - 3
                    pe.wait_ge(S["score_masked"], n + 1)
                    pe.wait_ge(S["t_ready"], 2 * min(j, NB))
                    for i in range(GB):
                        ins = t.matmul(pt[3][:, 768 + i * F:768 + (i + 1) * F], score[n % 2][:, i, :],
                                       value[n % 3][:, i, :], start=True, stop=True)
                    ins.then_inc(S["att_done"], 1)

            def nodes_slot(j):
                pe.wait_ge(S["norm_done"], 4 + min(4 * j // NG + 1, 4))
                if j == 0:
                    pe.wait_ge(S["weights_in"], 16 * N_WEIGHTS)
                if j < NG:
                    if j >= 1:
                        pe.wait_ge(S["ext_x_ready"], j)
                    for i in range(GE):
                        ins = t.transpose(pt[2][0:F, i * P:(i + 1) * P], xn[:, j * GE + i, :], ident[:])
                    ins.then_inc(S["ext_x_done"], 1)
                if j >= 1:
                    pe.wait_ge(S["ext_x_ready"], j)
                    if j >= 2:
                        pe.wait_ge(S["ext_ready"], j - 1)
                    for i in range(GE):
                        tile = (j - 1) * GE + i
                        ins = t.matmul(pt[3][:, 512 + i * EXT:512 + (i + 1) * EXT], xn2_t[:, tile * P:(tile + 1) * P],
                                       w_ext[:], start=True, stop=True)
                    ins.then_inc(S["ext_done"], 1)

            def expert_slot(j):
                if j == 0:
                    pe.wait_ge(S["ext_x_ready"], NG)
                else:
                    pe.wait_ge(S["hidden_ready"], j)
                if j < NE * NG:
                    g, e = divmod(j, NE)
                    for i in range(2):
                        first = g * GE * P + i * 512
                        ins = t.matmul(pt[2][:, i * 512:(i + 1) * 512], w1_s[:, e, :], xn2_t[:, first:first + 512],
                                       start=True, stop=True)
                    ins.then_inc(S["hidden_done"], 1)
                if j >= 1:
                    e = (j - 1) % NE
                    if j >= 2:
                        pe.wait_ge(S["expert_ready"], j - 1)
                    t.matmul(pt[3][:, 0:GE * F], ones_row[:], b2_rows[:, e].rearrange("p a b -> p (a b)"),
                             start=True, stop=False)
                    for i in range(GE):
                        ins = t.matmul(pt[3][:, i * F:(i + 1) * F], hidden[(j - 1) % 2][:, i * P:(i + 1) * P],
                                       w2_s[:, e, :], start=False, stop=(i == GE - 1))
                    ins.then_inc(S["expert_done"], 1)

            def beside(k, part):
                for j in ATTENTION.get(k, (none, none))[part]:
                    attention_slot(j)
                for j in NODES.get(k, (none, none))[part]:
                    nodes_slot(j)
                for j in EXPERT.get(k, (none, none))[part]:
                    expert_slot(j)

            for j in FIRST_SLOTS:
                attention_slot(j)

            for k in range(LOG_W + 1, LOG_E + 1):
                cur = level_start(k)[1]
                for i in range(2):
                    pe.wait_ge(S["turned"], 2 * (k - LOG_W) + i + 1)
                    for b in range(HALF // P):
                        ins = t.transpose(pt[i][:, b * P:(b + 1) * P], half(1 - cur, i)[:, b * P:(b + 1) * P],
                                          ident[:])
                    ins.then_inc(S["up_done"], 1)
                beside(k, 0)
                ops, cur = level_down(k)
                for i in range(2):
                    pe.wait_ge(S["sorted_ops"], ops - 2 * (1 - i) * AHEAD_DOWN)
                    for b in range(HALF // P):
                        ins = t.transpose(pt[i][:, b * P:(b + 1) * P], half(cur, i)[:, b * P:(b + 1) * P],
                                          ident[:])
                    ins.then_inc(S["down_done"], 1)
                beside(k, 1)

            pe.wait_ge(S["heads_split"], 1)
            for cls in range(2):
                for i in range(2):
                    t.matmul(pt[0][:, cls:cls + 1], heads_under[i][:, SUMMED, cls, 0:P], ones_col[:],
                             start=(i == 0), stop=(i == 1))
            for i in range(2):
                ins = t.matmul(pt[0][0:1, 512:512 + 2 * (P + 1)], ones_col[:],
                               heads_under[i][:, SUMMED].rearrange("p a b -> p (a b)"), start=(i == 0), stop=(i == 1))
            ins.then_inc(S["heads_counted"], 1)

            for j in LAST_SLOTS:
                if j == FIND_SLOT:
                    pe.wait_ge(S["sides_ready"], 1)
                    for i in range(3):
                        ins = t.transpose(pt[0][:, i * P:(i + 1) * P], sides[:, i].rearrange("p a b -> p (a b)"),
                                          ident[:])
                    ins.then_inc(S["sides_turned"], 1)
                if j == COUNT_SLOT:
                    pe.wait_ge(S["sides_ready"], 2)
                    t.transpose(pt[1][:, 0:P], sides[:, 3].rearrange("p a b -> p (a b)"), ident[:])\
                     .then_inc(S["sides_turned"], 1)
                expert_slot(j)

            pe.wait_ge(S["expert_ready"], NE * NG)
            pe.wait_ge(S["sizes_ready"], 1)
            chunks = pe.value_load(sizes_i[0:1, 2:3], min_val=2, max_val=MAX_CHUNKS)
            with pe.Fori(0, chunks) as k:
                for r, (n, state) in enumerate(((HEADS, state_d), (HEADS, state_m), (SUMS, state_s))):
                    hold(pe, "tail_ready", 3 * k + r + 1)
                    for j in range(2):
                        ins = t.transpose(pt[3][0:n, j * P:(j + 1) * P], tails[:, j, 0:n], ident[:])
                    ins.then_inc(S["tail_t"], 1)
                    hold(pe, "state_ready", 3 * k + r + 1)
                    t.transpose(pt[3][:, 512:512 + n], state[:, 0:P], ident[0:n, 0:n]).then_inc(S["carry_t"], 1)

        @block.vector
        def _(dve):
            v = nc.vector
            c1 = Counted(dve, S["v_chain"])
            link, mark = c1.link, c1.mark
            dve.wait_ge(S["lane_ready"], 1)
            for m in range(LOG_E - LOG_W + 1):
                last = v.tensor_scalar(lane_bit[:, m:m + 1], lane[:], m, 1, ALU.logical_shift_right,
                                       ALU.bitwise_and)
            link(last)
            link(v.tensor_scalar(sign[:], lane_bit[:], -2.0, 1.0, ALU.mult, ALU.add))
            v.tensor_copy(turn[:, 0:1], sign[:, 0:1])
            link(v.tensor_tensor(turn[:, 1:], sign[:, 0:-1], sign[:, 1:], ALU.mult))
            mark(v.memset(state_d[:], 0.0))
            mark(v.memset(state_m[:], -BIG))
            link(v.memset(state_s[:], 0.0))

            dve.wait_ge(S["edges_in"], 32)
            dst_w, src_w = sort[0][:].bitcast(I32), sort[1][:].bitcast(I32)
            far_w = xn[:].rearrange("p t f -> p (t f)").bitcast(I32)[:, 0:W]
            link(v.tensor_scalar(far_w, src_w, float(M - 1), float(FAR), ALU.is_ge, ALU.mult))
            mark(v.tensor_scalar(dst_w, dst_w, SRC_BITS, NODE, ALU.logical_shift_left, ALU.bitwise_or))
            link(v.tensor_scalar(src_w, src_w, float(M - 1), 0.0, ALU.min, ALU.max))
            link(v.tensor_tensor(dst_w, dst_w, far_w, ALU.bitwise_or))
            link(v.tensor_tensor(dst_w, dst_w, src_w, ALU.bitwise_or))
            dve.wait_ge(S["weights_in"], 160)
            dve.wait_ge(S["mask_ready"], 2)
            v.tensor_scalar(att_sel[:, 0], head_mask[:], att_col[:, 0:1], None, ALU.mult)
            v.tensor_scalar(att_sel[:, 1], head_mask[:], att_col[:, 1:2], None, ALU.mult).then_inc(S["prep_dve"], 1)

            dve.wait_ge(S["b2_in"], 16)
            b2_of = [b2_part[:, i].rearrange("a e f -> a (e f)") for i in range(3)]
            for i in range(2):
                link(v.tensor_copy(b2_of[i], b2_row[:, i]))
                link(v.tensor_tensor(b2_row[:, i + 1], b2_row[:, i], b2_of[i], ALU.subtract))
            v.tensor_copy(b2_of[2], b2_row[:, 2]).then_inc(S["b2_split"], 1)
            dve.wait_ge(S["node_ready"], 4)
            mark(v.tensor_copy(place[:], place_i[:]))
            mark(v.tensor_copy(block_row[:], block_row_i[:]))
            mark(v.tensor_copy(first_key[:], first_key_i[:]))
            mark(v.tensor_copy(row_of[:], row_of_i[:]))
            mark(v.memset(heads_under[0][:, 0], 0.0))
            link(v.memset(heads_under[1][:, 0], 0.0))

            POOL_STAGE = 4
            ended = [0, 0]
            ops = 0

            def compare(halves, lo, hi, lesser, greater):
                nonlocal ops
                v.tensor_tensor(lesser, lo, hi, ALU.min).then_inc(S["sorted_ops"], 1)
                v.tensor_tensor(greater, lo, hi, ALU.max).then_inc(S["sorted_ops"], 1)
                ops += 2
                for i in halves:
                    ended[i] = ops

            def one_half(i, src, dst, d, hi=None):
                if ended[i]:
                    dve.wait_ge(S["sorted_ops"], ended[i])
                a, b = pairs(src, d), pairs(dst, d)
                compare((i,), a[:, :, 0], a[:, :, 1] if hi is None else pairs(hi, d)[:, :, 1],
                        b[:, :, 0], b[:, :, 1])

            def ahead(n, lead, step):
                for m in range(n + lead):
                    if m < n:
                        step(0, m)
                    if m >= lead:
                        step(1, m - lead)

            def across_halves(cur):
                dve.wait_ge(S["sorted_ops"], max(ended))
                compare((0, 1), half(cur, 0), half(cur, 1), half(1 - cur, 0), half(1 - cur, 1))
                return 1 - cur

            def shift_logits(i):
                s = i % 2
                lg = pt[2 * s + 1][:].rearrange("p (t w f) -> p t w f", w=POOL, f=F)
                most = tree[s][:, :, 2]
                dve.wait_ge(S["logits_done"], i + 1)
                if i >= 2:
                    dve.wait_ge(S["pooled"], 2 * (i - 1))
                v.tensor_reduce(most, lg.rearrange("p t w f -> p t f w"), AX.X, ALU.max).then_inc(S["pool_max"], 1)
                dve.wait_ge(S["pool_max"], i + 1)
                v.tensor_tensor(logits[s], lg, most.unsqueeze(2).broadcast_to([P, GA, POOL, F]), ALU.subtract)\
                 .then_inc(S["shifted"], 1)

            def means(n):
                link(v.tensor_reduce(stat[:, 0], h[:], AX.X, ALU.add))
                v.tensor_scalar(stat[:, 0], stat[:, 0], 1.0 / F, None, ALU.mult).then_inc(S["norm_mean"], 1)

            def variances(n):
                dve.wait_ge(S["norm_squared"], 4 * n)
                link(v.tensor_reduce(stat[:, 1], square, AX.X, ALU.add))
                v.tensor_scalar(stat[:, 1], stat[:, 1], 1.0 / F, EPS, ALU.mult, ALU.add).then_inc(S["norm_var"], 1)

            def factors(n):
                dve.wait_ge(S["norm_sd"], n)
                v.reciprocal(stat[:, 1], stat[:, 1]).then_inc(S["norm_scale"], 1)

            dve.sem_inc(S["frames_free"], FRAMES)
            dve.sem_inc(S["shifted"], 2)
            cur, stages = 0, 0
            for k in range(1, LOG_W):
                for j in range(k - 1, -1, -1):
                    a, b = (sort[s][:].rearrange("p (u r a t s) -> p u r a t s", r=2, a=2 ** (k - j - 1), t=2,
                                                 s=2 ** j) for s in (cur, 1 - cur))
                    for r in range(2):
                        if ops:
                            dve.wait_ge(S["sorted_ops"], ops - 2 if j < k - 1 or r == 1 else ops)
                        compare((0, 1), a[:, :, r, :, 0], a[:, :, r, :, 1], b[:, :, r, :, r], b[:, :, r, :, 1 - r])
                    cur = 1 - cur
                    stages += 1
                    if (stages - POOL_STAGE) % 2 == 0 and 0 <= (stages - POOL_STAGE) // 2 < TILES // GA:
                        shift_logits((stages - POOL_STAGE) // 2)
                    if stages == MEAN_STAGE:
                        dve.wait_ge(S["inverse"], 3)
                        link(v.scalar_tensor_tensor(xn[:], xn[:], 2.0, square, ALU.subtract, ALU.mult))
                        link(v.scalar_tensor_tensor(h[:], h[:], -1.0, xn[:], ALU.mult, ALU.mult))
                        means(1)
                    if stages == VAR_STAGE:
                        variances(1)
                    if stages == VAR_STAGE + 1:
                        factors(1)

            cur = 1 - cur
            dve.wait_ge(S["turned"], 2)
            cur = across_halves(cur)
            def rows_step(i, m):
                src = (cur + m) % 2
                one_half(i, half(src, i), half(1 - src, i), 2 ** (LOG_W - 2 - m))
            ahead(LOG_W - 1, AHEAD_ROWS, rows_step)
            cur = (cur + LOG_W - 1) % 2
            assert (ops, cur) == level_start(LOG_W + 1)

            for k in range(LOG_W + 1, LOG_E + 1):
                n = k - LOG_W - 1
                def up_step(i, m):
                    if m == 0:
                        dve.wait_ge(S["hi_ready"], 4 * n + i + 1)
                        one_half(i, pt[i][:], half(cur, i), 2 ** n, hi=half(1 - cur, i))
                    else:
                        src = (cur + m - 1) % 2
                        one_half(i, half(src, i), half(1 - src, i), 2 ** (n - m))
                ahead(n + 1, min(AHEAD_UP, n + 1), up_step)
                cur = (cur + n) % 2
                if k == NORM_LEVEL + 1:
                    variances(2)
                cur = across_halves(cur)
                if k == NORM_LEVEL + 1:
                    factors(2)

                def columns_step(i, m):
                    src = (cur + m) % 2
                    one_half(i, half(src, i), half(1 - src, i), 4 * P >> m)
                ahead(3, AHEAD_DOWN, columns_step)
                cur = (cur + 3) % 2
                assert (ops, cur) == level_down(k)
                if k == NORM_LEVEL:
                    dve.wait_ge(S["attn_added"], NB)
                    means(2)

                def down_step(i, m):
                    if m == 0:
                        dve.wait_ge(S["hi_ready"], 4 * n + i + 3)
                        one_half(i, pt[i][:], half(1 - cur, i), P // 2, hi=half(cur, i))
                    else:
                        src = (cur + m) % 2
                        one_half(i, half(src, i), half(1 - src, i), P // 2 >> m)
                ahead(7, AHEAD_ROWS, down_step)
                cur = (cur + 7) % 2
            assert (ops, cur) == (SORT_OPS, SORT_END)

            heads = sort[SORT_END][:].rearrange("p (c s) -> p c s", s=STEP)[:, :, 0].bitcast(I32)
            dve.wait_ge(S["sorted_ops"], SORT_OPS)
            link(v.tensor_scalar(head_i[:], heads, BLOCK_BIT, None, ALU.logical_shift_right))
            link(v.tensor_copy(head_block[:], head_i[:]))
            flat_row = block_row[:].rearrange("p a b -> p (a b)")
            for c in range(HPP // 2):
                for i in range(2):
                    acc = heads_under[i][:].rearrange("p n a b -> p n (a b)")
                    if c >= 1:
                        dve.wait_ge(S["v_chain"], c1.n - 1)
                    mark(v.scalar_tensor_tensor(acc[:, (c + 1) % 2], flat_row, head_block[:, 2 * c + i:2 * c + i + 1],
                                                acc[:, c % 2], ALU.is_gt, ALU.add))
            dve.wait_ge(S["v_chain"], c1.n)
            dve.sem_inc(S["heads_split"], 1)

            dve.wait_ge(S["heads_counted"], 1)
            link(v.tensor_copy(under_row[:], pt[0][0:1, 512:512 + 2 * (P + 1)].rearrange("p (a b) -> p a b", a=2)))
            link(v.tensor_scalar(need_row[:], under_row[:, :, 0:P], 1.0, 0.0, ALU.subtract, ALU.max))
            link(v.tensor_tensor(need_row[:], under_row[:, :, 1:], need_row[:], ALU.subtract))
            mark(v.tensor_reduce(sizes[:, 0:2], need_row[:], AX.X, ALU.max))
            mark(v.tensor_scalar(sizes[:, 2:3], under_row[:, 0, P:P + 1], 1.0 / (CHUNK // STEP), 2.0, ALU.mult,
                                 ALU.max))
            dve.wait_ge(S["v_chain"], c1.n)
            link(v.tensor_scalar(sizes[:, 0:2], sizes[:, 0:2], 1.0 / WINDOW, 1.0, ALU.mult, ALU.max))
            link(v.tensor_copy(sizes_i[:, 0:3], sizes[:, 0:3]))
            link(v.tensor_copy(sizes_back[:, 0:3], sizes_i[:, 0:3]))
            link(v.tensor_tensor(sizes[:, 0:3], sizes[:, 0:3], sizes_back[:, 0:3], ALU.is_gt))
            link(v.tensor_tensor(sizes[:, 0:3], sizes[:, 0:3], sizes_back[:, 0:3], ALU.add))
            v.tensor_copy(sizes_i[:, 0:3], sizes[:, 0:3]).then_inc(S["sizes_ready"], 1)
            first_row = stat[:, 0, 0:2]
            link(v.tensor_scalar(first_row, pt[0][:, 0:2], 1.0, 0.0, ALU.subtract, ALU.max))
            for cls in range(2):
                mark(v.tensor_scalar(win_row[:, cls], row_of[:], first_row[:, cls:cls + 1], None, ALU.add))
                mark(v.tensor_scalar(lower[:, cls], first_row[:, cls:cls + 1].broadcast_to([P, NS]), float(STEP), None,
                                     ALU.mult))
            dve.wait_ge(S["v_chain"], c1.n)
            dve.wait_ge(S["sizes_ready"], 1)

            def window_rows(ch, cls):
                ch.link(v.tensor_scalar(under[:, 0:WINDOW], win_row[:, cls], float(HEADS_N), None, ALU.min))
                ch.link(v.tensor_copy(win_i[:, cls], under[:, 0:WINDOW]))
                dve.sem_inc(S[f"win_idx{cls}"], 1)
                ch.link(v.tensor_scalar(win_row[:, cls], win_row[:, cls], float(WINDOW), None, ALU.add))

            window_rows(c1, 0)
            window_rows(c1, 1)

            def words_under(cls):
                passes = dve.value_load(sizes_i[0:1, cls:cls + 1], min_val=1, max_val=MAX_PASSES)
                OPS = NS + 7
                with dve.Fori(0, passes) as r:
                    cw = Counted(dve, S[f"w_chain{cls}"], r * OPS)
                    dve.wait_ge(S[f"win_in{cls}"], 16 * WINDOW * (r + 1))
                    cw.link(v.tensor_scalar(win_key, windows[cls].bitcast(I32), SRC_BITS, None,
                                            ALU.logical_shift_right))
                    cw.link(v.tensor_scalar(win_diff, win_key, first_key[:, cls:cls + 1], -1.0, ALU.subtract, ALU.max))
                    cw.link(v.tensor_scalar(win_node[:], win_diff, float(RANGE + 1), None, ALU.min))
                    for t in range(NS):
                        if t >= 2:
                            dve.wait_ge(cw.s, cw.first + cw.n - 1)
                        cw.mark(v.tensor_scalar(less[t % 2], win_node[:], float(t), 0.0, ALU.is_lt, ALU.add,
                                                accum_out=under[:, t:t + 1]))
                    dve.wait_ge(cw.s, cw.first + cw.n)
                    cw.link(v.tensor_tensor(lower[:, cls], lower[:, cls], under[:], ALU.add))
                    window_rows(cw, cls)
                    assert cw.n == OPS

            dve.wait_ge(S["keys_in"], 16)

            def segments(ch):
                ch.link(v.tensor_scalar(segs[:], keys[:], SRC_BITS, None, ALU.logical_shift_right))
                ch.link(v.tensor_tensor(same_next[:], segs[:, 1:], segs[:, 0:C], ALU.is_equal))

            def sources(ch, idx, first, ready):
                ch.mark(v.tensor_scalar(idx[:], keys[:, 1 + first:1 + first + HC2], M - 1, None, ALU.bitwise_and))
                dve.wait_ge(ch.s, ch.first + ch.n)
                dve.sem_inc(S[ready], 1)

            segments(c1)
            sources(c1, src_a, 0, "idx_a")
            sources(c1, src_b, HC2, "idx_b")
            dve.sem_inc(S["keys_free"], 1)
            dve.sem_inc(S["rows_a_free"], 2)
            dve.sem_inc(S["rows_b_free"], 2)

            words_under(0)
            start, end, some, far = (sides[:, i, 0] for i in range(4))
            low = lower[:, 0, 0:RANGE]
            link(v.tensor_tensor(some, lower[:, 0, 1:], low, ALU.is_gt))
            mark(v.tensor_scalar(end, lower[:, 0, 1:], 1.0, 0.0, ALU.subtract, ALU.max))
            link(v.tensor_tensor(start, low, place[:], ALU.subtract))
            link(v.tensor_tensor(start, start, some, ALU.mult))
            link(v.tensor_tensor(start, start, place[:], ALU.add))
            v.tensor_copy(sides[:, 0:3, 1], sides[:, 0:3, 0]).then_inc(S["sides_ready"], 1)

            def to_tiles(to, turned):
                for i in range(2):
                    lanes = slice(i * RANGE, (i + 1) * RANGE)
                    mark(v.tensor_copy(to[lanes], turned[lanes, :, :, i]))
                dve.wait_ge(S["v_chain"], c1.n)

            dve.wait_ge(S["sides_turned"], 1)
            to_tiles(by_tile[:], pt[0][:, 0:3 * P].rearrange("p (a g two) -> p a g two", a=3, two=2))
            mark(v.tensor_copy(end_i[:], by_tile[:, 1]))
            mark(v.tensor_copy(has[:, 0], by_tile[:, 2]))
            v.tensor_copy(start_i[:], by_tile[:, 0]).then_inc(S["scatter_ready"], 1)
            words_under(1)
            link(v.tensor_tensor(far, lower[:, 1, 1:], lower[:, 1, 0:RANGE], ALU.subtract))
            v.tensor_copy(sides[:, 3, 1], far).then_inc(S["sides_ready"], 1)
            dve.wait_ge(S["sides_turned"], 2)
            to_tiles(count[:, 1:2], pt[1][:, 0:P].rearrange("p (a g two) -> p a g two", a=1, two=2))
            link(v.tensor_scalar(has[:, 1], count[:, 1], 0.0, None, ALU.is_gt))

            dve.sem_inc(S["inj_free"], 1)
            dve.sem_inc(S["exp_go"], 3)
            dve.sem_inc(S["res_out"], 16)
            chunks = dve.value_load(sizes_i[0:1, 2:3], min_val=2, max_val=MAX_CHUNKS)
            EDGE_OPS = 89
            with dve.Fori(0, chunks) as k:
                ch = Counted(dve, S["e_chain"], k * EDGE_OPS)

                def carried(r, n, state, op, to):
                    dve.wait_ge(S["tail_t"], 3 * k + r + 1)
                    ch.mark(v.tensor_copy(state[:, 0:1], state[:, P:P + 1]))
                    ch.link(v.tensor_copy(across[0:n], pt[3][0:n, 0:2 * P].rearrange("p (a b) -> p a b", a=2)))
                    v.tensor_tensor_scan(state[:, 1:P + 1], across[0:n, 1, :], across[0:n, 0, :], state[:, 0:1],
                                         op[0], op[1]).then_inc(S["state_ready"], 1)
                    dve.wait_ge(S["carry_t"], 3 * k + r + 1)
                    ch.link(v.tensor_copy(to, pt[3][:, 512:512 + n]))

                SUM, TOP = (ALU.mult, ALU.add), (ALU.add, ALU.max)
                ch.link(v.tensor_copy(same[:], same_next[:]))
                ch.mark(v.tensor_scalar(fence[:], same[:], 1.0, BIG, ALU.subtract, ALU.mult))
                ch.mark(v.tensor_reduce(lasts[:], same[:], AX.X, ALU.min))
                dve.wait_ge(S["keys_in"], 16 * (k + 2))
                segments(ch)
                def arrived(i, rows, landed, free, idx, ready):
                    dve.wait_ge(S[landed], GATHERS * (k + 1))
                    sources(ch, idx, i * HC2, ready)
                    ch.link(v.tensor_copy(a_s[:, :, i * HC2:(i + 1) * HC2],
                                          rows[:, :, HC:ROW].rearrange("p c o -> p o c")))
                    dve.sem_inc(S[free], 1)

                arrived(0, rows_a, "rows_a_in", "rows_a_free", src_a, "idx_a")
                dve.wait_ge(S["inj_in"], 16 * (k + 1))
                for i in range(HEADS):
                    ch.mark(v.tensor_tensor_scan(a_d[:, i], same[:], inj[:, :, i], 0.0, *SUM))
                dve.wait_ge(ch.s, ch.first + ch.n)
                ch.link(v.tensor_copy(tails[:, 0, 0:HEADS], a_d[:, :, C - 1]))
                v.tensor_copy(tails[:, 1, 0:HEADS], lasts[:].broadcast_to([P, HEADS])).then_inc(S["tail_ready"], 1)
                carried(0, HEADS, state_d, SUM, carry_d[:])
                for i in range(HEADS):
                    ch.mark(v.tensor_tensor_scan(a_d[:, i], same[:], inj[:, :, i], carry_d[:, i:i + 1], *SUM))
                dve.wait_ge(ch.s, ch.first + ch.n)
                dve.sem_inc(S["inj_free"], 1)
                arrived(1, rows_b, "rows_b_in", "rows_b_free", src_b, "idx_b")
                dve.sem_inc(S["keys_free"], 1)
                ch.link(v.tensor_tensor(logit, a_s[:], a_d[:], ALU.add))
                ch.link(v.scalar_tensor_tensor(logit, logit, 0.2, logit, ALU.mult, ALU.max))
                for i in range(HEADS):
                    ch.mark(v.tensor_tensor_scan(top[:, i, 1:], fence[:], logit[:, i], -BIG, *TOP))
                dve.wait_ge(ch.s, ch.first + ch.n)
                ch.mark(v.tensor_copy(tails[:, 0, 0:HEADS], top[:, :, C]))
                ch.link(v.tensor_scalar(lasts[:], lasts[:], 1.0, BIG, ALU.subtract, ALU.mult))
                v.tensor_copy(tails[:, 1, 0:HEADS], lasts[:].broadcast_to([P, HEADS])).then_inc(S["tail_ready"], 1)
                carried(1, HEADS, state_m, TOP, carry_m[:])
                ch.mark(v.tensor_copy(top[:, :, 0], carry_m[:]))
                for i in range(HEADS):
                    ch.mark(v.tensor_tensor_scan(top[:, i, 1:], fence[:], logit[:, i], carry_m[:, i:i + 1], *TOP))
                dve.wait_ge(ch.s, ch.first + ch.n)
                ch.link(v.tensor_tensor(keep, top[:, :, 0:C], top[:, :, 1:], ALU.subtract))
                v.tensor_scalar(keep, keep, 0.0, None, ALU.min).then_inc(S["exp_go"], 1)
                v.tensor_tensor(wgt[:, 0:HEADS], logit, top[:, :, 1:], ALU.subtract).then_inc(S["exp_go"], 1)
                ch.link(v.tensor_tensor(passing[:], carry_m[:], top[:, :, C], ALU.subtract))
                v.scalar_tensor_tensor(passing[:], passing[:], 0.0, lasts[:].broadcast_to([P, HEADS]), ALU.min,
                                       ALU.add).then_inc(S["exp_go"], 1)
                dve.wait_ge(S["exp_done"], 3 * k + 1)
                ch.mark(v.tensor_tensor(keep, keep, same[:].unsqueeze(1).broadcast_to([P, HEADS, C]), ALU.mult))
                dve.wait_ge(S["exp_done"], 3 * k + 2)
                dve.wait_ge(S["h_copied"], 2 * k + 2)
                for i in range(HEADS):
                    ch.mark(v.tensor_tensor(wgt[:, HEADS + NE * i:HEADS + NE * (i + 1)], h_s[:, NE * i:NE * (i + 1)],
                                            wgt[:, i:i + 1].broadcast_to([P, NE, C]), ALU.mult))
                dve.wait_ge(ch.s, ch.first + ch.n)

                def head(c):
                    return c if c < HEADS else (c - HEADS) // NE

                for c in range(SUMS):
                    ch.mark(v.tensor_tensor_scan(part[:, c], keep[:, head(c)], wgt[:, c], 0.0, *SUM))
                dve.wait_ge(ch.s, ch.first + ch.n)
                dve.wait_ge(S["exp_done"], 3 * k + 3)
                ch.mark(v.tensor_copy(tails[:, 0, :], part[:, :, C - 1]))
                ch.mark(v.tensor_copy(tails[:, 1, 0:HEADS], passing[:]))
                v.tensor_copy(tails[:, 1, HEADS:].rearrange("p (a b) -> p a b", b=NE),
                              passing[:].unsqueeze(2).broadcast_to([P, HEADS, NE])).then_inc(S["tail_ready"], 1)
                carried(2, SUMS, state_s, SUM, carry_s[:])
                dve.wait_ge(S["res_out"], 16 * (k + 1))
                for c in range(SUMS):
                    ch.mark(v.tensor_tensor_scan(results_s[:, :, HEADS + c], keep[:, head(c)], wgt[:, c],
                                                 carry_s[:, c:c + 1], *SUM))
                v.tensor_copy(results_s[:, :, 0:HEADS].rearrange("p c o -> p o c"), top[:, :, 1:])\
                 .then_inc(S["res_ready"], 1)
                dve.wait_ge(S["res_ready"], k + 1)
                assert ch.n == EDGE_OPS, ch.n

            cf = Counted(dve, S["f_chain"])
            link, mark = cf.link, cf.mark

            def by_head(ap, n=TILES):
                return ap.unsqueeze(2).broadcast_to([P, n, HEADS])

            a_dst = ext[:, :, ROW:EXT]
            last_row = clamped[:].unsqueeze(1).broadcast_to([P, TILES, ROW])
            dve.wait_ge(S["clamped_in"], 16)
            mark(v.tensor_tensor(mg[:, 1], ext[:, :, HC:ROW], a_dst, ALU.add))
            mark(v.tensor_scalar(has[:], has[:], 1.0, BIG, ALU.subtract, ALU.mult))
            link(v.tensor_tensor(mg[:, 2], a_dst, last_row[:, :, HC:ROW], ALU.add))
            link(v.scalar_tensor_tensor(mg[:, 1:3], mg[:, 1:3], 0.2, mg[:, 1:3], ALU.mult, ALU.max))
            link(v.tensor_tensor(mg[:, 2], mg[:, 2], by_head(has[:, 1]), ALU.add))
            link(v.tensor_tensor(mtop, mg[:, 1], mg[:, 2], ALU.max))
            v.tensor_tensor(mg[:, 1:3], mg[:, 1:3], mtop.unsqueeze(1).broadcast_to([P, 2, TILES, HEADS]),
                            ALU.subtract).then_inc(S["own_go"], 1)
            dve.wait_ge(S["own_exp"], 1)
            link(v.tensor_tensor(mg[:, 2], mg[:, 2], by_head(count[:, 1]), ALU.mult))
            for j in range(HEADS):
                s4 = slice(NE * j, NE * (j + 1))
                wide = [mg[:, i, :, j:j + 1].broadcast_to([P, TILES, NE]) for i in (1, 2)]
                mark(v.tensor_tensor(own_agg[:, :, s4], ext[:, :, s4], wide[0], ALU.mult))
                mark(v.tensor_tensor(tmp_all[:, :, s4], wide[1], last_row[:, :, s4], ALU.mult))
            dve.wait_ge(S["f_chain"], cf.n)
            mark(v.tensor_tensor(own_agg, own_agg, tmp_all, ALU.add))
            link(v.tensor_tensor(mg[:, 2], mg[:, 1], mg[:, 2], ALU.add))
            link(v.tensor_copy(mg[:, 1], mtop))

            def merge(i, s, n):
                def per_row(ap):
                    return ap[:].unsqueeze(1).broadcast_to([P, n, HC])

                def per_token(ap, c=HC):
                    return ap.unsqueeze(2).broadcast_to([P, n, c])

                dve.wait_ge(S[f"ends_in{i}"], 16 * n)
                top_s, total = mtop[:, s], mtop[:, s]
                link(v.tensor_tensor(mg[:, 0, s], ends[:, s, 0:HEADS], by_head(has[:, 0, s], n), ALU.add))
                link(v.tensor_tensor(top_s, mg[:, 0, s], mg[:, 1, s], ALU.max))
                v.tensor_tensor(mg[:, 0:2, s], mg[:, 0:2, s], top_s.unsqueeze(1).broadcast_to([P, 2, n, HEADS]),
                                ALU.subtract).then_inc(S["mg_go"], 1)
                dve.wait_ge(S["mg_exp"], i + 1)
                mark(v.tensor_tensor(total, ends[:, s, HEADS:2 * HEADS], mg[:, 0, s], ALU.mult))
                mark(v.tensor_tensor(mg[:, 2, s], mg[:, 2, s], mg[:, 1, s], ALU.mult))
                agg, own, tmp = ends[:, s, 2 * HEADS:], own_agg[:, s], tmp_all[:, s]
                for j in range(HEADS):
                    s4 = slice(NE * j, NE * (j + 1))
                    wide = [mg[:, kind, s, j:j + 1].broadcast_to([P, n, NE]) for kind in (0, 1)]
                    mark(v.tensor_tensor(agg[:, :, s4], agg[:, :, s4], wide[0], ALU.mult))
                    mark(v.tensor_tensor(own[:, :, s4], own[:, :, s4], wide[1], ALU.mult))
                dve.wait_ge(S["f_chain"], cf.n)
                mark(v.tensor_tensor(total, total, mg[:, 2, s], ALU.add))
                mark(v.tensor_tensor(agg, agg, own, ALU.add))
                dve.wait_ge(S["f_chain"], cf.n)
                link(v.tensor_scalar(total, total, 1e-16, None, ALU.add))
                link(v.reciprocal(total, total))
                for j in range(HEADS):
                    s4 = slice(NE * j, NE * (j + 1))
                    mark(v.tensor_tensor(agg[:, :, s4], agg[:, :, s4],
                                         total[:, :, j:j + 1].broadcast_to([P, n, NE]), ALU.mult))
                dve.wait_ge(S["f_chain"], cf.n)
                link(v.tensor_tensor(agg, agg, per_row(bg), ALU.add))
                mean, sd = st2[:, 0, s], st2[:, 1, s]
                link(v.tensor_reduce(mean, agg, AX.X, ALU.add))
                link(v.tensor_scalar(mean, mean, 1.0 / HC, None, ALU.mult))
                link(v.tensor_tensor(agg, agg, per_token(mean), ALU.subtract))
                link(v.tensor_tensor(tmp, agg, agg, ALU.mult))
                link(v.tensor_reduce(sd, tmp, AX.X, ALU.add))
                v.tensor_scalar(sd, sd, 1.0 / HC, EPS, ALU.mult, ALU.add).then_inc(S["var_go"], 1)
                mark(v.tensor_tensor(agg, agg, per_row(gamma), ALU.mult))
                dve.wait_ge(S["sd_ready"], i + 1)
                link(v.reciprocal(sd, sd))
                link(v.tensor_tensor(agg, agg, per_token(sd), ALU.mult))
                link(v.tensor_tensor(agg, agg, per_row(beta), ALU.add))
                sc_s, cmp_s, gate_s = sc[:, s], cmp[:, s], gate[:, s]
                link(v.tensor_reduce(sc_s, agg.rearrange("p t (h c) -> p t c h", c=NE), AX.X, ALU.add))
                mark(v.tensor_scalar(sc_s, sc_s, 1.0 / HEADS, None, ALU.mult))
                for a in range(NE):
                    mark(v.memset(cmp_s[:, :, a], float(a)))
                dve.wait_ge(S["f_chain"], cf.n)
                for a in range(NE):
                    for b in range(a + 1, NE):
                        over = mtop[:, s, (a + b) % 2]
                        link(v.tensor_tensor(over, sc_s[:, :, b], sc_s[:, :, a], ALU.is_gt))
                        mark(v.tensor_tensor(cmp_s[:, :, a], cmp_s[:, :, a], over, ALU.add))
                        link(v.tensor_tensor(cmp_s[:, :, b], cmp_s[:, :, b], over, ALU.subtract))
                link(v.tensor_reduce(mean, sc_s, AX.X, ALU.max))
                v.tensor_tensor(sc_s, sc_s, per_token(mean, NE), ALU.subtract).then_inc(S["gate_go"], 1)
                link(v.tensor_scalar(cmp_s, cmp_s, 1.5, None, ALU.is_lt))
                dve.wait_ge(S["gate_exp"], i + 1)
                link(v.tensor_tensor(gate_s, sc_s, cmp_s, ALU.mult))
                link(v.tensor_reduce(mean, gate_s, AX.X, ALU.add))
                link(v.reciprocal(mean, mean))
                v.tensor_tensor(gate_s, gate_s, per_token(mean, NE), ALU.mult).then_inc(S["gated"], 1)
                dve.wait_ge(S["gated"], i + 1)
                for e in range(NE - 1):
                    mark(v.tensor_tensor(experts[:, s, e], experts[:, s, e],
                                         gate_s[:, :, e:e + 1].broadcast_to([P, n, F]), ALU.mult))
                dve.wait_ge(S["f_chain"], cf.n)
                mark(v.tensor_tensor(experts[:, s, 0], experts[:, s, 0], experts[:, s, 1], ALU.add))
                link(v.tensor_tensor(h[:, s, :], h[:, s, :], experts[:, s, 2], ALU.add))
                link(v.tensor_tensor(h[:, s, :], h[:, s, :], experts[:, s, 0], ALU.add))
                dve.wait_ge(S["last_gated"], s.start + n)
                v.tensor_tensor(h[:, s, :], h[:, s, :], experts[:, s, NE - 1], ALU.add).then_inc(S["y_done"], 1)

            dve.wait_ge(S["weights_in"], 16 * N_WEIGHTS)
            for i, (first, n) in enumerate(PARTS):
                merge(i, slice(first, first + n), n)


_INS = ["x", "L0_tok_W", "L0_attn_W_alpha", "L0_attn_W_beta", "L0_attn_W_unary", "L0_attn_b_unary",
        "L0_attn_W_r", "L0_ffn_W_gat", "L0_ffn_att_src", "L0_ffn_att_dst", "L0_ffn_b_gat",
        "L0_ffn_ln_gamma", "L0_ffn_ln_beta", "L0_ffn_W1", "L0_ffn_b1", "L0_ffn_W2", "L0_ffn_b2",
        "L0_ffn_edge_index"]


def kernel(**inputs):
    import concourse.bacc as bacc
    from concourse.bass_utils import run_bass_kernel_spmd

    nc = bacc.Bacc("TRN2", target_bir_lowering=False, num_devices=1)
    arrays, args = {}, []
    for name in _INS:
        a = np.ascontiguousarray(inputs[name])
        arrays[f"in_{name}"] = a
        args.append(nc.dram_tensor(f"in_{name}", a.shape, mybir.dt.from_np(a.dtype), kind="ExternalInput").ap())
    b, l, f = inputs["x"].shape
    args.append(nc.dram_tensor("out_0", (b, l // 4, f), F32, kind="ExternalOutput").ap())
    audio_tower(nc, *args)
    r = run_bass_kernel_spmd(nc, [arrays], core_ids=[0])
    return r.results[0]["out_0"]
```
